# Optimizing a Trainium2 kernel written in Bass

```python
import numpy as np
import jax
import jax.numpy as jnp

def _softmax(x, axis=-1):
    return jax.nn.softmax(x, axis=axis)

def _gelu(x):
    return jax.nn.gelu(x, approximate=True)

def _silu(x):
    return jax.nn.silu(x)

def _sigmoid(x):
    return jax.nn.sigmoid(x)

def _layernorm(x, axis=-1, eps=1e-05):
    m = jnp.mean(x, axis=axis, keepdims=True)
    v = jnp.var(x, axis=axis, keepdims=True)
    return (x - m) / jnp.sqrt(v + eps)

def _scatter_add(tgt, idx, src, axis=0):
    return tgt.at[idx].add(src)

def _segment_sum(src, seg, n):
    return jax.ops.segment_sum(src, seg, n)
kernel_name = 'mk_xattn_seq_d2_seqx_r8_a7836f'

def setup_inputs(seed: int=0):
    np.random.seed(seed)
    _w = jnp.asarray

    def _rec_inputs():
        import jax
        import jax.numpy as jnp
        _rk = jax.random.key(seed)
        x = -1.394e-06 + 0.9999 * jax.random.normal(jax.random.fold_in(_rk, 1), (8, 100, 128), jnp.float32)
        _lenS = 100 - jax.random.randint(jax.random.fold_in(_rk, 7), (8,), 0, max(1, 100 // 4) + 1, jnp.int32)
        _lenS2 = 1444 - jax.random.randint(jax.random.fold_in(_rk, 8), (8,), 0, max(1, 1444 // 4) + 1, jnp.int32)
        _ctx_1024P = jax.random.normal(jax.random.fold_in(_rk, 11), (8, 16, 128), jnp.float32)
        _ctx_1024c = jax.random.dirichlet(jax.random.fold_in(_rk, 511), 0.3 * jnp.ones((16,), jnp.float32), (8, 1444))
        _ctx_1024t = jnp.einsum('bsk,bkd->bsd', _ctx_1024c, _ctx_1024P)
        _ctx_1024t = _ctx_1024t * jax.lax.rsqrt(jnp.mean(jnp.square(_ctx_1024t)) + 1e-12) * 0.953939
        ctx_1024 = -0.000292821 + 1.00034 * (_ctx_1024t + 0.3 * jax.random.normal(jax.random.fold_in(_rk, 611), (8, 1444, 128), jnp.float32))
        return (x, ctx_1024)
    x, ctx_1024 = _rec_inputs()

    def _L0_xattn_setup():
        import jax, jax.numpy as jnp
        import numpy as np
        D, H, DFF, MD = (128, 16, 512, 128)
        B, TS, TT = (8, 64, 64)
        EPS = 1e-06

        def _ln(x, s, b):
            m = jnp.mean(x, axis=-1, keepdims=True)
            v = jnp.mean((x - m) ** 2, axis=-1, keepdims=True)
            return (x - m) * jax.lax.rsqrt(v + EPS) * s + b

        def _rel_bias(emb, qlen, klen):
            q = jnp.arange(qlen)[:, None]
            k = jnp.arange(klen)[None, :]
            rp = k - q
            bucket = jnp.where(rp < 0, jnp.minimum(-rp, MD - 1), jnp.minimum(rp, MD - 1) + MD)
            return emb[bucket].transpose(2, 0, 1)

        def _mha(xq, xkv, w_in, b_in, w_out, b_out, bias):
            Bq, Tq, _ = xq.shape
            Tk = xkv.shape[1]
            hd = D // H
            wq, wk, wv = jnp.split(w_in, 3, axis=0)
            bq, bk, bv = jnp.split(b_in, 3, axis=0)
            q = (xq @ wq.T + bq).reshape(Bq, Tq, H, hd).transpose(0, 2, 1, 3)
            k = (xkv @ wk.T + bk).reshape(Bq, Tk, H, hd).transpose(0, 2, 1, 3)
            v = (xkv @ wv.T + bv).reshape(Bq, Tk, H, hd).transpose(0, 2, 1, 3)
            scores = jnp.einsum('bhqd,bhkd->bhqk', q, k) / jnp.sqrt(jnp.asarray(hd, xq.dtype))
            scores = scores + bias[None]
            attn = jax.nn.softmax(scores, axis=-1)
            out = jnp.einsum('bhqk,bhkd->bhqd', attn, v)
            out = out.transpose(0, 2, 1, 3).reshape(Bq, Tq, D)
            return out @ w_out.T + b_out
        key = jax.random.key(seed)
        ks = jax.random.split(key, 40)
        std = 0.02

        def n(i, shape):
            return jax.random.normal(ks[i], shape, dtype=jnp.float32) * std
        return {'src': jax.random.normal(ks[0], (B, TS, D), dtype=jnp.float32), 'tgt': jax.random.normal(ks[1], (B, TT, D), dtype=jnp.float32), 'enc_in_w': n(2, (3 * D, D)), 'enc_in_b': jnp.zeros((3 * D,)), 'enc_out_w': n(3, (D, D)), 'enc_out_b': jnp.zeros((D,)), 'enc_ff1_w': n(4, (DFF, D)), 'enc_ff1_b': jnp.zeros((DFF,)), 'enc_ff2_w': n(5, (D, DFF)), 'enc_ff2_b': jnp.zeros((D,)), 'enc_n1_s': jnp.ones((D,)), 'enc_n1_b': jnp.zeros((D,)), 'enc_n2_s': jnp.ones((D,)), 'enc_n2_b': jnp.zeros((D,)), 'enc_rel': n(6, (2 * MD, H)), 'dec_sa_in_w': n(7, (3 * D, D)), 'dec_sa_in_b': jnp.zeros((3 * D,)), 'dec_sa_out_w': n(8, (D, D)), 'dec_sa_out_b': jnp.zeros((D,)), 'dec_ca_in_w': n(9, (3 * D, D)), 'dec_ca_in_b': jnp.zeros((3 * D,)), 'dec_ca_out_w': n(10, (D, D)), 'dec_ca_out_b': jnp.zeros((D,)), 'dec_ff1_w': n(11, (DFF, D)), 'dec_ff1_b': jnp.zeros((DFF,)), 'dec_ff2_w': n(12, (D, DFF)), 'dec_ff2_b': jnp.zeros((D,)), 'dec_n1_s': jnp.ones((D,)), 'dec_n1_b': jnp.zeros((D,)), 'dec_n2_s': jnp.ones((D,)), 'dec_n2_b': jnp.zeros((D,)), 'dec_n3_s': jnp.ones((D,)), 'dec_n3_b': jnp.zeros((D,)), 'dec_rel_self': n(13, (2 * MD, H)), 'dec_rel_cross': n(14, (2 * MD, H))}
    _L0_xattn_all = _L0_xattn_setup()
    _L0_xattn_in = {k: v for k, v in _L0_xattn_all.items() if k in ('enc_in_w', 'enc_in_b', 'enc_out_w', 'enc_out_b', 'enc_ff1_w', 'enc_ff1_b', 'enc_ff2_w', 'enc_ff2_b', 'enc_n1_s', 'enc_n1_b', 'enc_n2_s', 'enc_n2_b', 'enc_rel', 'dec_sa_in_w', 'dec_sa_in_b', 'dec_sa_out_w', 'dec_sa_out_b', 'dec_ca_in_w', 'dec_ca_in_b', 'dec_ca_out_w', 'dec_ca_out_b', 'dec_ff1_w', 'dec_ff1_b', 'dec_ff2_w', 'dec_ff2_b', 'dec_n1_s', 'dec_n1_b', 'dec_n2_s', 'dec_n2_b', 'dec_n3_s', 'dec_n3_b', 'dec_rel_self', 'dec_rel_cross')}
    del _L0_xattn_all

    def _L1_xattn_setup():
        import jax, jax.numpy as jnp
        import numpy as np
        TOPK = 10
        NUM_HEADS = 16
        key = jax.random.key(seed)
        ks = jax.random.split(key, 8)
        B, N, S, D = (32, 256, 256, 128)
        sc = 1.0 / np.sqrt(D)
        return {'base_hidden': jax.random.normal(ks[0], (B, N, D), jnp.float32), 'scaffold_hidden': jax.random.normal(ks[1], (B, S, D), jnp.float32), 'in_proj_w': jax.random.normal(ks[2], (3 * D, D), jnp.float32) * sc, 'in_proj_b': jax.random.normal(ks[3], (3 * D,), jnp.float32) * 0.02, 'out_w': jax.random.normal(ks[4], (D, D), jnp.float32) * sc, 'out_b': jax.random.normal(ks[5], (D,), jnp.float32) * 0.02, 'score_w': jax.random.normal(ks[6], (1, D), jnp.float32) * sc, 'score_b': jax.random.normal(ks[7], (1,), jnp.float32) * 0.02}
    _L1_xattn_all = _L1_xattn_setup()
    _L1_xattn_in = {k: v for k, v in _L1_xattn_all.items() if k in ('in_proj_w', 'in_proj_b', 'out_w', 'out_b', 'score_w', 'score_b')}
    del _L1_xattn_all
    return {'x': x, 'ctx_1024': ctx_1024, 'L0_xattn_enc_in_w': _L0_xattn_in['enc_in_w'], 'L0_xattn_enc_in_b': _L0_xattn_in['enc_in_b'], 'L0_xattn_enc_out_w': _L0_xattn_in['enc_out_w'], 'L0_xattn_enc_out_b': _L0_xattn_in['enc_out_b'], 'L0_xattn_enc_ff1_w': _L0_xattn_in['enc_ff1_w'], 'L0_xattn_enc_ff1_b': _L0_xattn_in['enc_ff1_b'], 'L0_xattn_enc_ff2_w': _L0_xattn_in['enc_ff2_w'], 'L0_xattn_enc_ff2_b': _L0_xattn_in['enc_ff2_b'], 'L0_xattn_enc_n1_s': _L0_xattn_in['enc_n1_s'], 'L0_xattn_enc_n1_b': _L0_xattn_in['enc_n1_b'], 'L0_xattn_enc_n2_s': _L0_xattn_in['enc_n2_s'], 'L0_xattn_enc_n2_b': _L0_xattn_in['enc_n2_b'], 'L0_xattn_enc_rel': _L0_xattn_in['enc_rel'], 'L0_xattn_dec_sa_in_w': _L0_xattn_in['dec_sa_in_w'], 'L0_xattn_dec_sa_in_b': _L0_xattn_in['dec_sa_in_b'], 'L0_xattn_dec_sa_out_w': _L0_xattn_in['dec_sa_out_w'], 'L0_xattn_dec_sa_out_b': _L0_xattn_in['dec_sa_out_b'], 'L0_xattn_dec_ca_in_w': _L0_xattn_in['dec_ca_in_w'], 'L0_xattn_dec_ca_in_b': _L0_xattn_in['dec_ca_in_b'], 'L0_xattn_dec_ca_out_w': _L0_xattn_in['dec_ca_out_w'], 'L0_xattn_dec_ca_out_b': _L0_xattn_in['dec_ca_out_b'], 'L0_xattn_dec_ff1_w': _L0_xattn_in['dec_ff1_w'], 'L0_xattn_dec_ff1_b': _L0_xattn_in['dec_ff1_b'], 'L0_xattn_dec_ff2_w': _L0_xattn_in['dec_ff2_w'], 'L0_xattn_dec_ff2_b': _L0_xattn_in['dec_ff2_b'], 'L0_xattn_dec_n1_s': _L0_xattn_in['dec_n1_s'], 'L0_xattn_dec_n1_b': _L0_xattn_in['dec_n1_b'], 'L0_xattn_dec_n2_s': _L0_xattn_in['dec_n2_s'], 'L0_xattn_dec_n2_b': _L0_xattn_in['dec_n2_b'], 'L0_xattn_dec_n3_s': _L0_xattn_in['dec_n3_s'], 'L0_xattn_dec_n3_b': _L0_xattn_in['dec_n3_b'], 'L0_xattn_dec_rel_self': _L0_xattn_in['dec_rel_self'], 'L0_xattn_dec_rel_cross': _L0_xattn_in['dec_rel_cross'], 'L1_xattn_in_proj_w': _L1_xattn_in['in_proj_w'], 'L1_xattn_in_proj_b': _L1_xattn_in['in_proj_b'], 'L1_xattn_out_w': _L1_xattn_in['out_w'], 'L1_xattn_out_b': _L1_xattn_in['out_b'], 'L1_xattn_score_w': _L1_xattn_in['score_w'], 'L1_xattn_score_b': _L1_xattn_in['score_b']}

def reference(x, ctx_1024, L0_xattn_enc_in_w, L0_xattn_enc_in_b, L0_xattn_enc_out_w, L0_xattn_enc_out_b, L0_xattn_enc_ff1_w, L0_xattn_enc_ff1_b, L0_xattn_enc_ff2_w, L0_xattn_enc_ff2_b, L0_xattn_enc_n1_s, L0_xattn_enc_n1_b, L0_xattn_enc_n2_s, L0_xattn_enc_n2_b, L0_xattn_enc_rel, L0_xattn_dec_sa_in_w, L0_xattn_dec_sa_in_b, L0_xattn_dec_sa_out_w, L0_xattn_dec_sa_out_b, L0_xattn_dec_ca_in_w, L0_xattn_dec_ca_in_b, L0_xattn_dec_ca_out_w, L0_xattn_dec_ca_out_b, L0_xattn_dec_ff1_w, L0_xattn_dec_ff1_b, L0_xattn_dec_ff2_w, L0_xattn_dec_ff2_b, L0_xattn_dec_n1_s, L0_xattn_dec_n1_b, L0_xattn_dec_n2_s, L0_xattn_dec_n2_b, L0_xattn_dec_n3_s, L0_xattn_dec_n3_b, L0_xattn_dec_rel_self, L0_xattn_dec_rel_cross, L1_xattn_in_proj_w, L1_xattn_in_proj_b, L1_xattn_out_w, L1_xattn_out_b, L1_xattn_score_w, L1_xattn_score_b):
    import jax
    import jax.numpy as jnp

    def _L0_xattn_ref(src, tgt, enc_in_w, enc_in_b, enc_out_w, enc_out_b, enc_ff1_w, enc_ff1_b, enc_ff2_w, enc_ff2_b, enc_n1_s, enc_n1_b, enc_n2_s, enc_n2_b, enc_rel, dec_sa_in_w, dec_sa_in_b, dec_sa_out_w, dec_sa_out_b, dec_ca_in_w, dec_ca_in_b, dec_ca_out_w, dec_ca_out_b, dec_ff1_w, dec_ff1_b, dec_ff2_w, dec_ff2_b, dec_n1_s, dec_n1_b, dec_n2_s, dec_n2_b, dec_n3_s, dec_n3_b, dec_rel_self, dec_rel_cross):
        import jax, jax.numpy as jnp
        import numpy as np
        D, H, DFF, MD = (128, 16, 512, 128)
        B, TS, TT = (8, 64, 64)
        EPS = 1e-06

        def _ln(x, s, b):
            m = jnp.mean(x, axis=-1, keepdims=True)
            v = jnp.mean((x - m) ** 2, axis=-1, keepdims=True)
            return (x - m) * jax.lax.rsqrt(v + EPS) * s + b

        def _rel_bias(emb, qlen, klen):
            q = jnp.arange(qlen)[:, None]
            k = jnp.arange(klen)[None, :]
            rp = k - q
            bucket = jnp.where(rp < 0, jnp.minimum(-rp, MD - 1), jnp.minimum(rp, MD - 1) + MD)
            return emb[bucket].transpose(2, 0, 1)

        def _mha(xq, xkv, w_in, b_in, w_out, b_out, bias):
            Bq, Tq, _ = xq.shape
            Tk = xkv.shape[1]
            hd = D // H
            wq, wk, wv = jnp.split(w_in, 3, axis=0)
            bq, bk, bv = jnp.split(b_in, 3, axis=0)
            q = (xq @ wq.T + bq).reshape(Bq, Tq, H, hd).transpose(0, 2, 1, 3)
            k = (xkv @ wk.T + bk).reshape(Bq, Tk, H, hd).transpose(0, 2, 1, 3)
            v = (xkv @ wv.T + bv).reshape(Bq, Tk, H, hd).transpose(0, 2, 1, 3)
            scores = jnp.einsum('bhqd,bhkd->bhqk', q, k) / jnp.sqrt(jnp.asarray(hd, xq.dtype))
            scores = scores + bias[None]
            attn = jax.nn.softmax(scores, axis=-1)
            out = jnp.einsum('bhqk,bhkd->bhqd', attn, v)
            out = out.transpose(0, 2, 1, 3).reshape(Bq, Tq, D)
            return out @ w_out.T + b_out
        Ts, Tt = (src.shape[1], tgt.shape[1])
        eb = _rel_bias(enc_rel, Ts, Ts)
        x = src
        x = x + _mha(_ln(x, enc_n1_s, enc_n1_b), _ln(x, enc_n1_s, enc_n1_b), enc_in_w, enc_in_b, enc_out_w, enc_out_b, eb)
        h = _ln(x, enc_n2_s, enc_n2_b)
        x = x + (jax.nn.relu(h @ enc_ff1_w.T + enc_ff1_b) @ enc_ff2_w.T + enc_ff2_b)
        memory = x
        causal = jnp.where(jnp.arange(Tt)[None, :] > jnp.arange(Tt)[:, None], -jnp.inf, 0.0)
        sb = _rel_bias(dec_rel_self, Tt, Tt) + causal[None]
        cb = _rel_bias(dec_rel_cross, Tt, Ts)
        y = tgt
        yn = _ln(y, dec_n1_s, dec_n1_b)
        y = y + _mha(yn, yn, dec_sa_in_w, dec_sa_in_b, dec_sa_out_w, dec_sa_out_b, sb)
        y = y + _mha(_ln(y, dec_n2_s, dec_n2_b), memory, dec_ca_in_w, dec_ca_in_b, dec_ca_out_w, dec_ca_out_b, cb)
        h = _ln(y, dec_n3_s, dec_n3_b)
        y = y + (jax.nn.relu(h @ dec_ff1_w.T + dec_ff1_b) @ dec_ff2_w.T + dec_ff2_b)
        return y

    def _L1_xattn_ref(base_hidden, scaffold_hidden, in_proj_w, in_proj_b, out_w, out_b, score_w, score_b):
        import jax, jax.numpy as jnp
        import numpy as np
        TOPK = 10
        NUM_HEADS = 16
        B, N, D = base_hidden.shape
        H = NUM_HEADS
        dh = D // H
        scores = jnp.einsum('bnd,d->bn', base_hidden, score_w[0]) + score_b[0]
        _, topk_idx = jax.lax.top_k(scores, TOPK)
        sparse_hidden = jnp.take_along_axis(base_hidden, topk_idx[:, :, None], axis=1)
        Wq, Wk, Wv = jnp.split(in_proj_w, 3, axis=0)
        bq, bk, bv = jnp.split(in_proj_b, 3)
        q = (sparse_hidden @ Wq.T + bq).reshape(B, TOPK, H, dh).transpose(0, 2, 1, 3)
        k = (scaffold_hidden @ Wk.T + bk).reshape(B, -1, H, dh).transpose(0, 2, 1, 3)
        v = (scaffold_hidden @ Wv.T + bv).reshape(B, -1, H, dh).transpose(0, 2, 1, 3)
        scale = 1.0 / np.sqrt(dh).astype(np.float32)
        logits = jnp.einsum('bhqd,bhkd->bhqk', q, k) * scale
        attn = jax.nn.softmax(logits, axis=-1)
        o = jnp.einsum('bhqk,bhkd->bhqd', attn, v).transpose(0, 2, 1, 3).reshape(B, TOPK, D)
        attn_out = o @ out_w.T + out_b
        return base_hidden.at[jnp.arange(B)[:, None], topk_idx].set(attn_out)
    x = _L0_xattn_ref(ctx_1024, x, L0_xattn_enc_in_w, L0_xattn_enc_in_b, L0_xattn_enc_out_w, L0_xattn_enc_out_b, L0_xattn_enc_ff1_w, L0_xattn_enc_ff1_b, L0_xattn_enc_ff2_w, L0_xattn_enc_ff2_b, L0_xattn_enc_n1_s, L0_xattn_enc_n1_b, L0_xattn_enc_n2_s, L0_xattn_enc_n2_b, L0_xattn_enc_rel, L0_xattn_dec_sa_in_w, L0_xattn_dec_sa_in_b, L0_xattn_dec_sa_out_w, L0_xattn_dec_sa_out_b, L0_xattn_dec_ca_in_w, L0_xattn_dec_ca_in_b, L0_xattn_dec_ca_out_w, L0_xattn_dec_ca_out_b, L0_xattn_dec_ff1_w, L0_xattn_dec_ff1_b, L0_xattn_dec_ff2_w, L0_xattn_dec_ff2_b, L0_xattn_dec_n1_s, L0_xattn_dec_n1_b, L0_xattn_dec_n2_s, L0_xattn_dec_n2_b, L0_xattn_dec_n3_s, L0_xattn_dec_n3_b, L0_xattn_dec_rel_self, L0_xattn_dec_rel_cross)
    x = _L1_xattn_ref(x, ctx_1024, L1_xattn_in_proj_w, L1_xattn_in_proj_b, L1_xattn_out_w, L1_xattn_out_b, L1_xattn_score_w, L1_xattn_score_b)
    return x

_drawn_inputs = setup_inputs


def setup_inputs(seed=0):
    import zlib

    import numpy as np

    out = dict(_drawn_inputs(seed))
    spreads = {'L0_xattn_enc_in_b': (0.0, 0.8),
     'L0_xattn_enc_out_b': (0.0, 0.8),
     'L0_xattn_enc_ff1_b': (0.0, 0.8),
     'L0_xattn_enc_ff2_b': (0.0, 0.8),
     'L0_xattn_enc_n1_s': (1.0, 0.6),
     'L0_xattn_enc_n1_b': (0.0, 0.8),
     'L0_xattn_enc_n2_s': (1.0, 0.6),
     'L0_xattn_enc_n2_b': (0.0, 0.8),
     'L0_xattn_dec_sa_in_b': (0.0, 0.442),
     'L0_xattn_dec_sa_out_b': (0.0, 0.1),
     'L0_xattn_dec_ca_in_b': (0.0, 0.362),
     'L0_xattn_dec_ca_out_b': (0.0, 0.1),
     'L0_xattn_dec_ff1_b': (0.0, 0.285),
     'L0_xattn_dec_ff2_b': (0.0, 0.1),
     'L0_xattn_dec_n1_s': (1.0, 0.6),
     'L0_xattn_dec_n1_b': (0.0, 0.8),
     'L0_xattn_dec_n2_s': (1.0, 0.6),
     'L0_xattn_dec_n2_b': (0.0, 2.0),
     'L0_xattn_dec_n3_s': (1.0, 0.6),
     'L0_xattn_dec_n3_b': (0.0, 0.8)}
    factors = {'L0_xattn_enc_in_w': 8.0,
     'L0_xattn_enc_out_w': 8.0,
     'L0_xattn_enc_ff1_w': 8.0,
     'L0_xattn_enc_ff2_w': 8.0,
     'L0_xattn_enc_rel': 200.0,
     'L0_xattn_dec_sa_in_w': 4.242,
     'L0_xattn_dec_rel_self': 8.0,
     'L0_xattn_dec_rel_cross': 200.0,
     'L1_xattn_in_proj_b': 8.0,
     'L1_xattn_out_b': 7.495}
    for name, (base, spread) in spreads.items():
        noise = np.random.default_rng([zlib.crc32(name.encode()), seed]).standard_normal(out[name].shape)
        drawn = base * np.exp(spread * noise) if base else spread * noise
        out[name] = jnp.asarray(drawn.astype(out[name].dtype))
    for name, factor in factors.items():
        out[name] = (out[name] * factor).astype(out[name].dtype)
    return out
```

```python
import concourse.bass as bass
from concourse import mybir
from contextlib import ExitStack

B, T, Q, D, H, HD = 8, 1444, 100, 128, 16, 8
TOPK = 10
KT, NT = 121, 12
LAST = T - KT * (NT - 1)
CH, NC = 4 * KT, 3
CW = [CH, CH, T - 2 * CH]
QC, NQ = T // 4, 4
MD = 128
HALO = MD - 2
NPROD = 9 * HD
NSTEP = 3 * NT
ROWS = NPROD + NSTEP + 3
SUB = 32
BW = SUB + 2 * HALO
SPLIT = 60
STRIP0 = KT * (NT - 1)
SW = STRIP0 + T
SCALE = float(HD) ** -0.5

WCOL = {}
for _n, _k in (("e_q", 1), ("e_k", 1), ("e_v", 1), ("e_o", 1), ("e_f1", 4), ("e_f2", 4),
               ("s_q", 1), ("s_k", 1), ("s_v", 1), ("s_o", 1), ("c_q", 1), ("c_k", 1), ("c_v", 1), ("c_o", 1),
               ("d_f1", 4), ("d_f2", 4), ("t_q", 1), ("t_k", 1), ("t_v", 1), ("t_o", 1)):
    WCOL[_n] = (sum(k for _, k in WCOL.values()), _k)
NW = sum(k for _, k in WCOL.values())
VCOL = {}
for _n, _k in (("e_bq", 1), ("e_bk", 1), ("e_bo", 1), ("e_b1", 4), ("e_b2", 1), ("e_n1s", 1), ("e_n1b", 1),
               ("e_n2s", 1), ("e_n2b", 1), ("s_bq", 1), ("s_bk", 1), ("s_bo", 1), ("c_bq", 1), ("c_bk", 1),
               ("c_bo", 1), ("d_b1", 4), ("d_b2", 1), ("d_n1s", 1), ("d_n1b", 1), ("d_n2s", 1), ("d_n2b", 1),
               ("d_n3s", 1), ("d_n3b", 1), ("t_bq", 1), ("t_bk", 1), ("t_bv", 1), ("score", 1)):
    VCOL[_n] = (sum(k for _, k in VCOL.values()), _k)
NV = sum(k for _, k in VCOL.values())
ROWV = ["e_bv", "s_bv", "c_bv", "t_bv", "t_bo"]
EPS = 1e-6
NPOS = 3
GLEN = SW + KT - 1
RLEN = BW + SUB
G0 = STRIP0 + KT - 1

DTS = dict(fp32=mybir.dt.float32, bf16=mybir.dt.bfloat16)


class Mem:
    pass


def setup_phase(nc, m):
    fp32, bf16 = DTS["fp32"], DTS["bf16"]
    ALU, ACT = mybir.AluOpType, mybir.ActivationFunctionType
    ctx = ExitStack()
    with ctx:
        sb = lambda name, shape, dt: ctx.enter_context(nc.sbuf_tensor(name, shape, dt))
        sem = lambda name: nc.alloc_semaphore(name)
        band = sb("band", [128, H, BW], fp32)
        rest = sb("rest", [128, H, BW], fp32)
        piece = [sb(f"band_piece{s}", [128, H, BW], bf16) for s in range(3)]
        left = sb("left", [128, H], fp32)
        right = sb("right", [128, H], fp32)
        delta = sb("delta", [128, H], fp32)
        drest = sb("drest", [128, H], fp32)
        dpiece = [sb(f"delta_piece{s}", [128, H], bf16) for s in range(3)]
        dsel = sb("dsel", [128, H], fp32)
        tile_ind = sb("tile_ind", [96, T], bf16)
        steps = sb("steps", [96, 4, T], bf16)
        s_load, s_edge, s_band_in, s_ind = (sem(n) for n in ("s_load", "s_edge", "s_band_in", "s_ind"))
        s_v = sem("s_setup_vector")
        s_band, s_step, s_out = (sem(n) for n in ("s_band", "s_step", "s_setup_out"))
        s_step_out = [sem(f"s_step_out{i}") for i in range(4)]
        block = ctx.enter_context(nc.Block())

        @block.sync
        def _(sp):
            for k, src in enumerate((m.inputs["edge"][0:1, :], m.inputs["edge"][1:2, :])):
                sp.dma_start((left, right)[k][:, :], src.to_broadcast([128, H])).then_inc(s_edge, 16)
            for i in range(4):
                src = bass.AP(m.inputs["rev"].tensor, SUB - 1, [[RLEN - 1, SUB], [SUB * RLEN, H], [1, BW]])
                sp.dma_start(band[SUB * i:SUB * i + SUB, :, :], src).then_inc(s_band_in, 16)
            sp.dma_start(tile_ind[:, :], m.inputs["tile_ind"]).then_inc(s_ind, 16)
            loads = [(m.w[:, :], m.inputs["w"]), (m.vec[:, :], m.inputs["vec"]), (m.ident[:, :], m.inputs["ident"]),
                     (m.mean_w[:, :], m.inputs["mean"]), (m.den_sel[:, :], m.inputs["den_sel"]), (m.eps[:, :], m.inputs["eps"]),
                     (m.head_mask[:, :], m.inputs["head_mask"]), (m.score_b[:, :], m.inputs["score_b"])]
            loads += [(m.rowv[:, j, :], m.inputs["rowv"][j:j + 1, :].to_broadcast([128, D])) for j in range(len(ROWV))]
            for dst, src in loads:
                sp.dma_start(dst, src).then_inc(s_load, 16)
            for s in range(3):
                sp.wait_ge(s_band, s + 1)
                for i in range(4):
                    dst = m.d_band[:, SUB * s:SUB * s + SUB, i, :].rearrange("h r w -> r h w")
                    sp.dma_start(dst, piece[s][SUB * i:SUB * i + SUB, :, :]).then_inc(s_out, 16)
            for h in range(H):
                sp.wait_ge(s_step, h + 1)
                for s in range(3):
                    sp.dma_start(m.d_step[h, NT * s:NT * s + NT, :], steps[32 * s:32 * s + NT, h % 4, :]).then_inc(s_step_out[h % 4], 16)
            sp.wait_ge(s_load, 16 * len(loads))
            sp.wait_ge(s_out, 16 * 12)
            for i in range(4):
                sp.wait_ge(s_step_out[i], 48 * H // 4)

        @block.vector
        def _(dve):
            n = [0]

            def then(ins):
                n[0] += 1
                ins.then_inc(s_v, 1)
                dve.wait_ge(s_v, n[0])

            dve.wait_ge(s_edge, 32)
            then(nc.vector.tensor_copy(m.left[:, :], left[:, :]))
            then(nc.vector.tensor_tensor(delta[:, :], right[:, :], left[:, :], ALU.subtract))
            then(nc.vector.tensor_copy(dpiece[0][:, :], delta[:, :]))
            then(nc.vector.tensor_tensor(drest[:, :], delta[:, :], dpiece[0][:, :], ALU.subtract))
            then(nc.vector.tensor_copy(dpiece[1][:, :], drest[:, :]))
            then(nc.vector.tensor_tensor(dpiece[2][:, :], drest[:, :], dpiece[1][:, :], ALU.subtract))
            for s in range(3):
                then(nc.vector.tensor_copy(dsel[32 * s:32 * s + 32, :], dpiece[s][32 * s:32 * s + 32, :]))
            dve.wait_ge(s_band_in, 64)
            then(nc.vector.tensor_tensor(band[:, :, :], band[:, :, :], left[:, :].unsqueeze(2).to_broadcast([128, H, BW]), ALU.subtract))
            for i in range(4):
                w = SPLIT - SUB * i + HALO
                part = band[SUB * i:SUB * i + SUB, :, 0:w]
                then(nc.vector.tensor_tensor(part, part, delta[SUB * i:SUB * i + SUB, :].unsqueeze(2).to_broadcast([SUB, H, w]), ALU.subtract))
            then(nc.vector.tensor_copy(piece[0][:, :, :], band[:, :, :]))
            nc.vector.tensor_tensor(rest[:, :, :], band[:, :, :], piece[0][:, :, :], ALU.subtract).then_inc(s_band, 1)
            dve.wait_ge(s_band, 1)
            nc.vector.tensor_copy(piece[1][:, :, :], rest[:, :, :]).then_inc(s_band, 1)
            dve.wait_ge(s_band, 2)
            nc.vector.tensor_tensor(piece[2][:, :, :], rest[:, :, :], piece[1][:, :, :], ALU.subtract).then_inc(s_band, 1)
            dve.wait_ge(s_ind, 16)
            for h in range(H):
                if h >= 4:
                    dve.wait_ge(s_step_out[h % 4], 48 * (h // 4))
                nc.vector.tensor_scalar(steps[:, h % 4, :], tile_ind[:, :], dsel[0:96, h:h + 1], None, ALU.mult).then_inc(s_step, 1)


def done(n):
    return n + 1 + NC


def slot_free(n):
    return n + 1


def bank_free(n):
    return n + NC


def norm_and_project_phase(nc, m):
    fp32, bf16 = DTS["fp32"], DTS["bf16"]
    ALU, ACT = mybir.AluOpType, mybir.ActivationFunctionType
    ctx = ExitStack()
    with ctx:
        sb = lambda name, shape, dt: ctx.enter_context(nc.sbuf_tensor(name, shape, dt))
        x = sb("x", [128, NC, CH], fp32)
        xc = sb("xc", [128, NC, CH], fp32)
        sq = sb("sq", [128, NC, CH], fp32)
        sd = sb("sd", [128, NC, CH], fp32)
        xn = sb("xn", [128, NC, CH], fp32)
        q = sb("q", [128, NC, CH], fp32)
        k = sb("k", [128, NC, CH], fp32)
        qp = [sb(f"qp{s}", [128, NC, CH], bf16) for s in range(3)]
        kp = [sb(f"kp{s}", [128, NC, CH], bf16) for s in range(3)]
        v = sb("v", [KT, H, NT, HD], fp32)
        mean_ps, var_ps, q_ps, k_ps, v_ps = (ctx.enter_context(nc.psum_tensor(f"{n}_ps", [128, 512], fp32)) for n in ("mean", "var", "q", "k", "v"))
        (mean, centred, squared, var, dev, recip, scaled, normed, q_mm, k_mm, v_mm, q_out, k_out, v_out,
         q1, q_rest, q2, q3, k1, k_rest, k2, k3, v_st, v_zero) = (nc.alloc_semaphore(f"p1_{n}") for n in (
             "mean", "centred", "squared", "var", "dev", "recip", "scaled", "normed", "q_mm", "k_mm", "v_mm", "q_out", "k_out", "v_out",
             "q1", "q_rest", "q2", "q3", "k1", "k_rest", "k2", "k3", "v_st", "v_zero"))
        x_in, q_st, k_st = ([nc.alloc_semaphore(f"p1_{n}{c}") for c in range(NC)] for n in ("x_in", "q_st", "k_st"))
        block = ctx.enter_context(nc.Block())

        @block.sync
        def _(sp):
            for c in range(NC):
                sp.sem_inc(q_st[c], 48)
                sp.sem_inc(k_st[c], 48)
            sp.sem_inc(v_st, 16)

            with sp.Fori(0, B) as b:
                for c in range(NC):
                    n = b * NC + c
                    sp.wait_ge(q3, done(n))
                    for s in range(3):
                        sp.dma_start(m.d_qp[b, s, :, CH * c:CH * c + CW[c]], qp[s][:, c, 0:CW[c]]).then_inc(q_st[c], 16)
                    sp.wait_ge(k3, done(n))
                    for s in range(3):
                        sp.dma_start(m.d_kp[b, s, :, CH * c:CH * c + CW[c]], kp[s][:, c, 0:CW[c]]).then_inc(k_st[c], 16)
                sp.wait_ge(v_out, done(b * NC + NC - 1))
                sp.dma_start(m.d_v[b].rearrange("h p x -> p h x"), v[:, :, :, :].rearrange("p h t d -> p h (t d)")).then_inc(v_st, 16)
            for c in range(NC):
                sp.wait_ge(q_st[c], 48 * (B + 1))
                sp.wait_ge(k_st[c], 48 * (B + 1))
            sp.wait_ge(v_st, 16 * (B + 1))

        @block.tensor
        def _(pe):
            for s in (mean, var, q_mm, k_mm, v_mm):
                pe.sem_inc(s, NC)
            with pe.Fori(0, B) as b:
                for c in range(NC):
                    n, w = b * NC + c, CW[c]
                    pe.wait_ge(x_in[c], 16 * b + 16)
                    pe.wait_ge(centred, bank_free(n))
                    nc.tensor.matmul(mean_ps[:, 0:w], m.mean_w[:, :], x[:, c, 0:w], start=True, stop=True).then_inc(mean, 1)
                for c in range(NC):
                    n, w = b * NC + c, CW[c]
                    pe.wait_ge(squared, done(n))
                    pe.wait_ge(dev, bank_free(n))
                    nc.tensor.matmul(var_ps[:, 0:w], m.mean_w[:, :], sq[:, c, 0:w], start=True, stop=True).then_inc(var, 1)
                for c in range(NC):
                    n, w = b * NC + c, CW[c]
                    pe.wait_ge(normed, done(n))
                    pe.wait_ge(q_out, bank_free(n))
                    nc.tensor.matmul(q_ps[:, 0:w], m.weight("e_q"), xn[:, c, 0:w], start=True, stop=True).then_inc(q_mm, 1)
                    pe.wait_ge(k_out, bank_free(n))
                    nc.tensor.matmul(k_ps[:, 0:w], m.weight("e_k"), xn[:, c, 0:w], start=True, stop=True).then_inc(k_mm, 1)
                    pe.wait_ge(v_out, bank_free(n))
                    for t in range(4):
                        rows = min(KT, w - KT * t)
                        last = nc.tensor.matmul(v_ps[0:rows, D * t:D * t + D], xn[:, c, KT * t:KT * t + rows], m.weight("e_v"), start=True, stop=True)
                    last.then_inc(v_mm, 1)

        @block.gpsimd
        def _(pool):
            for s in (squared, q_rest, q3, k_rest, k3):
                pool.sem_inc(s, NC)
            with pool.Fori(0, B) as b:
                for c in range(NC):
                    n, w = b * NC + c, CW[c]
                    pool.wait_ge(centred, slot_free(n))
                    pool.dma_start(x[:, c, 0:w], m.inputs["ctx"][b, :, CH * c:CH * c + w]).then_inc(x_in[c], 16)
                for c in range(NC):
                    n, w = b * NC + c, CW[c]
                    pool.wait_ge(centred, done(n))
                    pool.wait_ge(var, slot_free(n))
                    nc.gpsimd.tensor_tensor(sq[:, c, 0:w], xc[:, c, 0:w], xc[:, c, 0:w], ALU.mult).then_inc(squared, 1)
                for c in range(NC):
                    n, w = b * NC + c, CW[c]
                    pool.wait_ge(q1, done(n))
                    nc.gpsimd.tensor_tensor(q[:, c, 0:w], q[:, c, 0:w], qp[0][:, c, 0:w], ALU.subtract).then_inc(q_rest, 1)
                    pool.wait_ge(k1, done(n))
                    nc.gpsimd.tensor_tensor(k[:, c, 0:w], k[:, c, 0:w], kp[0][:, c, 0:w], ALU.subtract).then_inc(k_rest, 1)
                    pool.wait_ge(q2, done(n))
                    nc.gpsimd.tensor_tensor(qp[2][:, c, 0:w], q[:, c, 0:w], qp[1][:, c, 0:w], ALU.subtract).then_inc(q3, 1)
                    pool.wait_ge(k2, done(n))
                    nc.gpsimd.tensor_tensor(kp[2][:, c, 0:w], k[:, c, 0:w], kp[1][:, c, 0:w], ALU.subtract).then_inc(k3, 1)

        @block.scalar
        def _(act):
            for s in (dev, normed, q1, q2, k1, k2):
                act.sem_inc(s, NC)
            with act.Fori(0, B) as b:
                for c in range(NC):
                    n, w = b * NC + c, CW[c]
                    act.wait_ge(var, done(n))
                    act.wait_ge(scaled, slot_free(n))
                    nc.scalar.activation(sd[:, c, 0:w], var_ps[:, 0:w], ACT.Sqrt, bias=m.eps[:, 0:1]).then_inc(dev, 1)
                for c in range(NC):
                    n, w = b * NC + c, CW[c]
                    act.wait_ge(scaled, done(n))
                    act.wait_ge(v_mm, slot_free(n))
                    nc.scalar.activation(xn[:, c, 0:w], xc[:, c, 0:w], ACT.Identity, scale=m.column("e_n1s"), bias=m.column("e_n1b")).then_inc(normed, 1)
                for c in range(NC):
                    n, w = b * NC + c, CW[c]
                    act.wait_ge(q_out, done(n))
                    act.wait_ge(q_st[c], 48 * b + 48)
                    nc.scalar.activation(qp[0][:, c, 0:w], q[:, c, 0:w], ACT.Copy).then_inc(q1, 1)
                    act.wait_ge(k_out, done(n))
                    act.wait_ge(k_st[c], 48 * b + 48)
                    nc.scalar.activation(kp[0][:, c, 0:w], k[:, c, 0:w], ACT.Copy).then_inc(k1, 1)
                    act.wait_ge(q_rest, done(n))
                    nc.scalar.activation(qp[1][:, c, 0:w], q[:, c, 0:w], ACT.Copy).then_inc(q2, 1)
                    act.wait_ge(k_rest, done(n))
                    nc.scalar.activation(kp[1][:, c, 0:w], k[:, c, 0:w], ACT.Copy).then_inc(k2, 1)

        @block.vector
        def _(dve):
            for s in (centred, recip, scaled, q_out, k_out, v_out):
                dve.sem_inc(s, NC)
            nc.vector.memset(v[:, :, :, :], 0.0).then_inc(v_zero, 1)
            dve.wait_ge(v_zero, 1)
            with dve.Fori(0, B) as b:
                for c in range(NC):
                    n, w = b * NC + c, CW[c]
                    dve.wait_ge(mean, done(n))
                    dve.wait_ge(normed, slot_free(n))
                    nc.vector.tensor_tensor(xc[:, c, 0:w], x[:, c, 0:w], mean_ps[:, 0:w], ALU.subtract).then_inc(centred, 1)
                for c in range(NC):
                    n, w = b * NC + c, CW[c]
                    dve.wait_ge(dev, done(n))
                    nc.vector.reciprocal(sd[:, c, 0:w], sd[:, c, 0:w]).then_inc(recip, 1)
                    dve.wait_ge(recip, done(n))
                    nc.vector.tensor_tensor(xc[:, c, 0:w], xc[:, c, 0:w], sd[:, c, 0:w], ALU.mult).then_inc(scaled, 1)
                for c in range(NC):
                    n, w = b * NC + c, CW[c]
                    dve.wait_ge(q_mm, done(n))
                    dve.wait_ge(q3, slot_free(n))
                    nc.vector.tensor_scalar(q[:, c, 0:w], q_ps[:, 0:w], m.column("e_bq"), SCALE, ALU.add, ALU.mult).then_inc(q_out, 1)
                    dve.wait_ge(k_mm, done(n))
                    dve.wait_ge(k3, slot_free(n))
                    nc.vector.tensor_scalar(k[:, c, 0:w], k_ps[:, 0:w], m.column("e_bk"), None, ALU.add).then_inc(k_out, 1)
                    dve.wait_ge(v_mm, done(n))
                    if c == 0:
                        dve.wait_ge(v_st, 16 * b + 16)
                    full = w // KT
                    bv = m.row("e_bv")
                    parts = [(KT, 0, full)] + ([(w - full * KT, full, 1)] if w % KT else [])
                    for rows, t, many in parts:
                        last = nc.vector.tensor_tensor(
                            v[0:rows, :, 4 * c + t:4 * c + t + many, :].rearrange("p h t d -> p t h d"),
                            v_ps[0:rows, D * t:D * (t + many)].rearrange("p (t h d) -> p t h d", t=many, h=H),
                            bv[0:rows, :].rearrange("p (o h d) -> p o h d", o=1, h=H).to_broadcast([rows, many, H, HD]), ALU.add)
                    last.then_inc(v_out, 1)


NU = H * B
SLOTS = 4
NA = NT * NC
A_BANKS = 3
A_EACH = NA // NT
A_AHEAD = 4
LOADS = 9
O_DMAS = NQ + 1


def wait_alone(eng, signal, value, passed):
    eng.wait_ge(signal, value)
    eng.sem_inc(passed, 1)


def rows_of(t):
    return KT if t < NT - 1 else LAST


def attention_phase(nc, m):
    fp32, bf16 = DTS["fp32"], DTS["bf16"]
    ALU, ACT, AX = mybir.AluOpType, mybir.ActivationFunctionType, mybir.AxisListType
    ctx = ExitStack()
    with ctx:
        sb = lambda name, shape, dt: ctx.enter_context(nc.sbuf_tensor(name, shape, dt))
        sem = lambda name: nc.alloc_semaphore(name)
        queries = [sb(f"queries{j}", [ROWS, KT * NT], bf16) for j in range(SLOTS)]
        keys = [sb(f"keys{j}", [ROWS, T], bf16) for j in range(SLOTS)]
        band = [sb(f"band{j}", [3 * SUB, 4, BW], bf16) for j in range(SLOTS)]
        v_in = [sb(f"v_in{j}", [KT, NT * HD], fp32) for j in range(SLOTS)]
        values = [sb(f"values{j}", [KT, NT, 32], fp32) for j in range(SLOTS)]
        ident3 = sb("ident3", [3 * SUB, SUB], bf16)
        probs = sb("probs", [KT, 2, T], fp32)
        strip = [sb(f"strip{i}", [KT, SW], fp32) for i in range(2)]
        tops = [sb(f"tops{i}", [KT, NT, NC], fp32) for i in range(2)]
        shift = sb("shift", [KT, NT], fp32)
        shift_rest = sb("shift_rest", [KT, NT], fp32)
        pieces = sb("pieces", [128, 3, 32], bf16)
        turned = [sb(f"turned{i}", [128, 3, 32], bf16) for i in range(2)]
        result = [sb(f"result{i}", [128, QC], fp32) for i in range(2)]
        a_ps = ctx.enter_context(nc.psum_tensor("a_ps", [128, A_BANKS, 512], fp32))
        b_ps = ctx.enter_context(nc.psum_tensor("b_ps", [128, NQ, 512], fp32))
        o_ps = ctx.enter_context(nc.psum_tensor("o_ps", [128, 512], fp32))
        constants_in, zeroed, dve_zeroed = sem("a_constants_in"), sem("a_zeroed"), sem("a_dve_zeroed")
        loaded = [sem(f"a_loaded{j}") for j in range(SLOTS)]
        strip_in = [sem(f"a_strip_in{i}") for i in range(2)]
        strip_used = sem("a_strip_used")
        padded = sem("a_padded")
        scored = sem("a_scored")
        maxed = sem("a_maxed")
        dve_step = sem("a_dve_step")
        turned_ready = sem("a_turned")
        shift_out = [sem(f"a_shift_out{j}") for j in range(SLOTS)]
        shift_in = [sem(f"a_shift_in{j}") for j in range(SLOTS)]
        exps_in = sem("a_exps_in")
        exp_out = sem("a_exp_out")
        multiplied = sem("a_multiplied")
        unit_done = sem("a_unit_done")
        copied = sem("a_copied")
        passed = {e: sem(f"a_passed_{e}") for e in ("pool", "sp", "dve")}
        stored = [sem(f"a_stored{i}") for i in range(2)]
        block = ctx.enter_context(nc.Block())

        @block.gpsimd
        def _(pool):
            for j in range(SLOTS):
                nc.gpsimd.memset(values[j][:, :, :], 0.0).then_inc(zeroed, 1)
            pool.wait_ge(zeroed, SLOTS)
            for j in range(SLOTS):
                nc.gpsimd.memset(values[j][:, :, HD:HD + 1], 1.0).then_inc(zeroed, 1)
            pool.wait_ge(zeroed, 2 * SLOTS)

            def load_strip(i, h):
                pool.dma_start(strip[i][:, :], bass.AP(m.inputs["line"].tensor, h * (KT * GLEN) + KT - 1, [[GLEN - 1, KT], [1, SW]])).then_inc(strip_in[i], 16)

            def load_head(h, i, another=True):
                with pool.Fori(0, B // SLOTS) as part:
                    for j in range(SLOTS):
                        u = h * B + part * SLOTS + j
                        b = part * SLOTS + j
                        pool.wait_ge(unit_done, u + 1)
                        first = h * HD
                        for s in range(3):
                            src = m.d_qp[b, s:s + 1, bass.ds(first, HD), :].to_broadcast([3, HD, T])
                            pool.dma_start(queries[j][24 * s:24 * s + 24, 0:T], src).then_inc(loaded[j], 16)
                            pool.dma_start(keys[j][24 * s:24 * s + 24, :], m.d_kp[b, :, bass.ds(first, HD), :]).then_inc(loaded[j], 16)
                        pool.dma_start(keys[j][NPROD:NPROD + NSTEP, :], m.d_step[bass.ds(h, 1), :, :].rearrange("o r t -> (o r) t")).then_inc(loaded[j], 16)
                        pool.dma_start(band[j][:, :, :], m.d_band[bass.ds(h, 1), :, :, :].rearrange("o r i w -> (o r) i w")).then_inc(loaded[j], 16)
                        pool.dma_start(v_in[j][:, :], m.d_v[b, bass.ds(h, 1), :, :].rearrange("o p x -> (o p) x")).then_inc(loaded[j], 16)
                        wait_alone(pool, loaded[j], (u - j) * (LOADS * 16 // SLOTS) + LOADS * 16, passed["pool"])
                        nc.gpsimd.tensor_copy(values[j][:, :, 0:HD], v_in[j][:, :].rearrange("p (t d) -> p t d", t=NT)).then_inc(padded, 1)
                if another:
                    wait_alone(pool, strip_used, h + 1, passed["pool"])
                    load_strip(1 - i, h + 1)

            load_strip(0, 0)
            with pool.Fori(0, H // 2 - 1) as pair:
                load_head(pair * 2, 0)
                load_head(pair * 2 + 1, 1)
            load_head(H - 2, 0)
            load_head(H - 1, 1, another=False)

        @block.sync
        def _(sp):
            for j in range(SLOTS):
                sp.dma_start(queries[j][NPROD:NPROD + NSTEP, 0:T], m.inputs["q_steps"]).then_inc(constants_in, 16)
                sp.dma_start(keys[j][NPROD + NSTEP:ROWS, :], m.inputs["ones3"]).then_inc(constants_in, 16)
            sp.dma_start(ident3[:, :], m.inputs["ident3"]).then_inc(constants_in, 16)
            for j in range(SLOTS):
                sp.sem_inc(shift_out[j], 64)

            def store(u, j):
                i = j % 2
                wait_alone(sp, copied, u + 2, passed["sp"])
                for q in range(NQ):
                    sp.dma_start(m.d_att[u, :, QC * q:QC * q + QC], result[i][32 * q:32 * q + HD, :]).then_inc(stored[i], 16)
                sp.dma_start(m.d_den[u, :].rearrange("(q x) -> q x", q=NQ), result[i][HD:128:32, :]).then_inc(stored[i], 16)

            def place_shift(u, j):
                sp.wait_ge(turned_ready, u + 1)
                row = m.d_shift[j]
                for a in range(4):
                    w = min(32, KT - 32 * a)
                    sp.dma_start(row.rearrange("s (t x) -> t s x", x=KT)[:, :, 32 * a:32 * a + w],
                                 turned[j % 2][32 * a:32 * a + NT, :, 0:w]).then_inc(shift_out[j], 16)
                sp.wait_ge(shift_out[j], (u - j) * (64 // SLOTS) + 128)
                sp.dma_start(queries[j][NPROD + NSTEP:ROWS, :], row).then_inc(shift_in[j], 16)

            for u in (0, 1):
                place_shift(u, u)
            with sp.Fori(0, (NU - 4) // SLOTS) as it:
                for k in range(SLOTS):
                    store(it * SLOTS + k, k)
                    place_shift(it * SLOTS + 2 + k, (2 + k) % SLOTS)
            for u in (NU - 2, NU - 1):
                store(u - 2, (u - 2) % SLOTS)
                place_shift(u, u % SLOTS)
            for u in (NU - 2, NU - 1):
                store(u, u % SLOTS)
            for i in range(2):
                sp.wait_ge(stored[i], 16 * O_DMAS * (NU // 2 + 1))

        @block.vector
        def _(dve):
            dve.sem_inc(maxed, A_BANKS)
            dve.sem_inc(strip_used, 1)
            nc.vector.memset(pieces[:, :, :], 0.0).then_inc(dve_zeroed, 1)
            for i in range(2):
                nc.vector.memset(tops[i][:, :, :], 0.0).then_inc(dve_zeroed, 1)
            dve.wait_ge(dve_zeroed, 3)
            with dve.Fori(0, H // 2) as pair:
                for i in range(2):
                    wait_alone(dve, strip_in[i], pair * 16 + 16, passed["dve"])
                    h = pair * 2 + i
                    with dve.Fori(0, B // SLOTS) as part:
                        for j in range(SLOTS):
                            u = pair * (2 * B) + i * B + part * SLOTS + j
                            for n in range(NA):
                                t, c = n // NC, n % NC
                                rows, w = rows_of(t), CW[c]
                                x0 = CH * c - KT * t + STRIP0
                                wait_alone(dve, scored, u * NA + n + 1, passed["dve"])
                                block_ps = a_ps[0:rows, n % A_BANKS, 0:w]
                                nc.vector.tensor_tensor_reduce(
                                    out=block_ps, in0=block_ps, in1=strip[i][0:rows, x0:x0 + w], scale=1.0, scalar=-3e38,
                                    op0=ALU.add, op1=ALU.max, accum_out=tops[j % 2][0:rows, t, c:c + 1]).then_inc(maxed, 1)
                            s = u * 6
                            dve.wait_ge(maxed, u * NA + NA + A_BANKS)
                            nc.vector.tensor_reduce(shift[:, :], tops[j % 2][:, :, :], AX.X, ALU.max, negate=True).then_inc(dve_step, 1)
                            dve.wait_ge(dve_step, s + 1)
                            nc.vector.tensor_scalar(shift[:, :], shift[:, :], m.left[0:KT, bass.ds(h, 1)], None, ALU.add).then_inc(dve_step, 1)
                            dve.wait_ge(dve_step, s + 2)
                            nc.vector.tensor_copy(pieces[0:KT, 0, 0:NT], shift[:, :]).then_inc(dve_step, 1)
                            dve.wait_ge(dve_step, s + 3)
                            nc.vector.tensor_tensor(shift_rest[:, :], shift[:, :], pieces[0:KT, 0, 0:NT], ALU.subtract).then_inc(dve_step, 1)
                            dve.wait_ge(dve_step, s + 4)
                            nc.vector.tensor_copy(pieces[0:KT, 1, 0:NT], shift_rest[:, :]).then_inc(dve_step, 1)
                            dve.wait_ge(dve_step, s + 5)
                            nc.vector.tensor_tensor(pieces[0:KT, 2, 0:NT], shift_rest[:, :], pieces[0:KT, 1, 0:NT], ALU.subtract).then_inc(dve_step, 1)
                            dve.wait_ge(dve_step, s + 6)
                            dve.wait_ge(shift_out[(j + 2) % SLOTS], (u - j) * (64 // SLOTS) + 64 * (1 if j < 2 else 2))
                            nc.vector.transpose(turned[j % 2][:, :, :].rearrange("p s x -> p (s x)"), pieces[:, :, :].rearrange("p s x -> p (s x)")).then_inc(turned_ready, 1)
                    dve.sem_inc(strip_used, 1)

        @block.tensor
        def _(pe):
            pe.sem_inc(multiplied, 2)
            pe.sem_inc(unit_done, SLOTS)
            pe.wait_ge(constants_in, 16 * (2 * SLOTS + 1))

            def first_pass(u, j, ns):
                for n in ns:
                    t, c = n // NC, n % NC
                    rows, w = rows_of(t), CW[c]
                    pe.wait_ge(maxed, u * NA + n + 1)
                    nc.tensor.matmul(a_ps[0:rows, n % A_BANKS, 0:w], queries[j][0:NPROD, KT * t:KT * t + rows],
                                     keys[j][0:NPROD, CH * c:CH * c + w], start=True, stop=True).then_inc(scored, 1)

            def exponents(u, j, t, half):
                rows = rows_of(t)
                pe.wait_ge(exp_out, u * (2 * NT) + 2 * t + half + 1)
                todo = []
                for q in (2 * half, 2 * half + 1):
                    todo.append((q, 0, rows, 0, QC, None))
                for i in range(4):
                    lo = KT * t + SUB * i - HALO
                    for q in (2 * half, 2 * half + 1):
                        a, z = max(lo, QC * q, 0), min(lo + BW, QC * q + QC)
                        if a < z:
                            todo.append((q, SUB * i, min(SUB, rows - SUB * i), a - QC * q, z - QC * q, (i, a - lo)))
                for n, (q, p, k, a, z, near) in enumerate(todo):
                    out = b_ps[p:p + k, q, a:z]
                    ends = not any(x[0] == q for x in todo[n + 1:])
                    if near is None:
                        last = nc.tensor.matmul(out, keys[j][0:ROWS, KT * t:KT * t + rows], queries[j][0:ROWS, QC * q:QC * q + QC],
                                                start=True, stop=ends, skip_group_check=True)
                    else:
                        i, w0 = near
                        last = nc.tensor.matmul(out, ident3[:, 0:k], band[j][:, i, w0:w0 + z - a], start=False, stop=ends, skip_group_check=True)
                last.then_inc(exps_in, 1)

            def multiply(u, j, t):
                rows = rows_of(t)
                pe.wait_ge(exp_out, u * (2 * NT) + 2 * t + 4)
                if t == 0:
                    pe.wait_ge(padded, u + 1)
                    pe.wait_ge(copied, u + 1)
                for q in range(NQ):
                    last = nc.tensor.matmul(o_ps[32 * q:32 * q + 32, 0:QC], values[j][0:rows, t, :], probs[0:rows, t % 2, QC * q:QC * q + QC],
                                            start=(t == 0), stop=(t == NT - 1))
                last.then_inc(multiplied, 1)

            def blocks(v, jv, t):
                first = A_EACH * (t + A_AHEAD)
                later = first >= NA
                return (v + later, (jv + later) % SLOTS, range(first % NA, first % NA + A_EACH))

            def unit(v, jv, with_b=True, with_last=True, with_next=True, with_a=True):
                u, j = v - 1, (jv - 1) % SLOTS
                if with_b:
                    pe.wait_ge(shift_in[j], (u - j) * (16 // SLOTS) + 16)
                for t in range(NT):
                    va, ja, ns = blocks(v, jv, t)
                    if not (with_next if ns[0] < A_EACH * A_AHEAD else with_a):
                        ns = ()
                    elif ns[0] == 0:
                        pe.wait_ge(loaded[ja], (va - ja) * (LOADS * 16 // SLOTS) + LOADS * 16)
                    first_pass(va, ja, ns[0:1])
                    if with_b:
                        exponents(u, j, t, 0)
                    first_pass(va, ja, ns[1:2])
                    if with_b:
                        exponents(u, j, t, 1)
                    first_pass(va, ja, ns[2:3])
                    if with_b:
                        if t > 0:
                            multiply(u, j, t - 1)
                        elif with_last:
                            finish(u - 1, (j - 1) % SLOTS)

            def finish(u, j):
                multiply(u, j, NT - 1)
                pe.wait_ge(multiplied, u * NT + NT + 2)
                pe.sem_inc(unit_done, 1)

            pe.wait_ge(loaded[0], LOADS * 16)
            first_pass(0, 0, range(A_EACH * A_AHEAD))
            unit(0, 0, with_b=False)
            unit(1, 1, with_last=False)
            with pe.Fori(0, (NU - 4) // SLOTS) as it:
                for k in range(SLOTS):
                    unit(it * SLOTS + 2 + k, (2 + k) % SLOTS)
            unit(NU - 2, (NU - 2) % SLOTS)
            unit(NU - 1, (NU - 1) % SLOTS, with_next=False)
            unit(NU, NU % SLOTS, with_next=False, with_a=False)
            finish(NU - 1, (NU - 1) % SLOTS)

        @block.scalar
        def _(act):
            act.sem_inc(exp_out, 2)
            act.sem_inc(copied, 1)
            for i in range(2):
                act.sem_inc(stored[i], 16 * O_DMAS)

            def exponentiate(u, ts):
                for t in ts:
                    rows = rows_of(t)
                    for half in range(2):
                        act.wait_ge(exps_in, u * (2 * NT) + 2 * t + half + 1)
                        if half == 0:
                            act.wait_ge(multiplied, u * NT + t + 1)
                        nc.scalar.activation(
                            probs[0:rows, t % 2, 2 * QC * half:2 * QC * (half + 1)].rearrange("p (q x) -> p q x", q=2),
                            b_ps[0:rows, 2 * half:2 * half + 2, 0:QC], ACT.Exp).then_inc(exp_out, 1)

            def copy_result(u, i):
                act.wait_ge(multiplied, u * NT + NT + 2)
                act.wait_ge(stored[i], (u - i) * (16 * O_DMAS // 2) + 16 * O_DMAS)
                nc.scalar.activation(result[i][:, :], o_ps[:, 0:QC], ACT.Copy).then_inc(copied, 1)

            def unit(u, i):
                exponentiate(u, range(1))
                copy_result(u - 1, 1 - i)
                exponentiate(u, range(1, NT))

            exponentiate(0, range(NT))
            with act.Fori(0, (NU - 2) // 2) as pair:
                unit(pair * 2 + 1, 1)
                unit(pair * 2 + 2, 0)
            unit(NU - 1, 1)
            copy_result(NU - 1, 1)


def context_phase(nc, m):
    fp32, bf16 = DTS["fp32"], DTS["bf16"]
    ALU, ACT = mybir.AluOpType, mybir.ActivationFunctionType
    ctx = ExitStack()
    with ctx:
        sb = lambda name, shape, dt: ctx.enter_context(nc.sbuf_tensor(name, shape, dt))
        sem = lambda name: nc.alloc_semaphore(name)
        den = sb("den", [B * H, T], fp32)
        x, att, inv, x1, xc, sq, sd, xn, kc, kl = (sb(f"c_{n}", [128, NC, CH], fp32) for n in ("x", "att", "inv", "x1", "xc", "sq", "sd", "xn", "kc", "kl"))
        hid = sb("hid", [128, NC, 4, CH], fp32)
        vc, vl = (sb(f"c_{n}", [KT, NC, 4, D], fp32) for n in ("vc", "vl"))
        o_ps, mean_ps, var_ps, f2_ps, k_ps, v_ps = (ctx.enter_context(nc.psum_tensor(f"c_{n}_ps", [128, 512], fp32)) for n in ("o", "mean", "var", "f2", "k", "v"))
        f1_ps = ctx.enter_context(nc.psum_tensor("c_f1_ps", [128, 2, 512], fp32))
        (den_in, den_done, den_out, attn, proj, x1_out, mean, centred, squared, var, dev, recip, scaled, normed, f1_mm, relu, f2_mm, mem,
         kl_mm, kl_out, kc_mm, kc_out, vl_mm, vl_out, vc_mm, vc_out, v_zero) = (sem(f"c_{n}") for n in (
             "den_in", "den_done", "den_out", "attn", "proj", "x1_out", "mean", "centred", "squared", "var", "dev", "recip", "scaled", "normed", "f1_mm", "relu", "f2_mm", "mem",
             "kl_mm", "kl_out", "kc_mm", "kc_out", "vl_mm", "vl_out", "vc_mm", "vc_out", "v_zero"))
        passed = sem("c_passed")
        loaded, x_loaded, kl_st, kc_st, vl_st, vc_st = ([sem(f"c_{n}{c}") for c in range(NC)] for n in ("loaded", "x_loaded", "kl_st", "kc_st", "vl_st", "vc_st"))
        block = ctx.enter_context(nc.Block())

        @block.sync
        def _(sp):
            sp.dma_start(den[:, :], m.d_den).then_inc(den_in, 16)
            sp.wait_ge(den_done, 1)
            sp.dma_start(m.d_inv, den[:, :]).then_inc(den_out, 16)
            for s in (kl_st, kc_st, vl_st, vc_st):
                for c in range(NC):
                    sp.sem_inc(s[c], 16)
            with sp.Fori(0, B) as b:
                for store, ready, src, dst in ((kl_st, kl_out, kl, m.d_kl), (kc_st, kc_out, kc, m.d_kc)):
                    for c in range(NC):
                        n, w = b * NC + c, CW[c]
                        sp.wait_ge(ready, done(n))
                        sp.dma_start(dst[b, :, CH * c:CH * c + w], src[:, c, 0:w]).then_inc(store[c], 16)
                for store, ready, src, dst in ((vl_st, vl_out, vl, m.d_vl), (vc_st, vc_out, vc, m.d_vc)):
                    for c in range(NC):
                        n = b * NC + c
                        sp.wait_ge(ready, done(n))
                        sp.dma_start(dst[b, :, 4 * c:4 * c + 4, :], src[:, c, :, :]).then_inc(store[c], 16)
            for s in (kl_st, kc_st, vl_st, vc_st):
                for c in range(NC):
                    sp.wait_ge(s[c], 16 * (B + 1))

        @block.gpsimd
        def _(pool):
            for s in (attn, squared):
                pool.sem_inc(s, NC)
            pool.wait_ge(den_out, 16)
            with pool.Fori(0, B) as b:
                for c in range(NC):
                    n, w = b * NC + c, CW[c]
                    pool.wait_ge(x1_out, slot_free(n))
                    wait_alone(pool, vl_mm, slot_free(n), passed)
                    pool.dma_start(x[:, c, 0:w], m.inputs["ctx"][b, :, CH * c:CH * c + w]).then_inc(x_loaded[c], 16)
                    wait_alone(pool, proj, slot_free(n), passed)
                    pool.dma_start(att[:, c, 0:w], m.d_att.rearrange("(h b) d t -> b h d t", b=B)[b, :, :, CH * c:CH * c + w]).then_inc(loaded[c], 16)
                    pool.dma_start(inv[:, c, 0:w], m.d_inv.rearrange("(h b) t -> b h t", b=B)[b, :, CH * c:CH * c + w].unsqueeze(1).to_broadcast([H, HD, w])).then_inc(loaded[c], 16)
                for c in range(NC):
                    n, w = b * NC + c, CW[c]
                    pool.wait_ge(loaded[c], b * 32 + 32)
                    nc.gpsimd.tensor_tensor(att[:, c, 0:w], att[:, c, 0:w], inv[:, c, 0:w], ALU.mult).then_inc(attn, 1)
                for c in range(NC):
                    n, w = b * NC + c, CW[c]
                    pool.wait_ge(centred, done(n))
                    pool.wait_ge(var, slot_free(n))
                    nc.gpsimd.tensor_tensor(sq[:, c, 0:w], xc[:, c, 0:w], xc[:, c, 0:w], ALU.mult).then_inc(squared, 1)

        @block.tensor
        def _(pe):
            for s in (proj, mean, var, f2_mm, kl_mm, kc_mm, vl_mm, vc_mm):
                pe.sem_inc(s, NC)

            def keys_values(b, src, k_name, v_name, ready, k_mm, v_mm, k_free, v_free):
                for c in range(NC):
                    n, w = b * NC + c, CW[c]
                    ready(c, n)
                    if c:
                        pe.wait_ge(k_free, bank_free(n))
                    nc.tensor.matmul(k_ps[:, 0:w], m.weight(k_name), src[:, c, 0:w], start=True, stop=True).then_inc(k_mm, 1)
                    if c:
                        pe.wait_ge(v_free, bank_free(n))
                    for t in range(4):
                        rows = min(KT, w - KT * t)
                        last = nc.tensor.matmul(v_ps[0:rows, D * t:D * t + D], src[:, c, KT * t:KT * t + rows], m.weight(v_name), start=True, stop=True)
                    last.then_inc(v_mm, 1)

            with pe.Fori(0, B) as b:
                pe.wait_ge(kc_out, slot_free(b * NC + NC - 1))
                pe.wait_ge(vc_out, slot_free(b * NC + NC - 1))
                keys_values(b, x, "t_k", "t_v", lambda c, n: pe.wait_ge(x_loaded[c], b * 16 + 16), kl_mm, vl_mm, kl_out, vl_out)
                for c in range(NC):
                    n, w = b * NC + c, CW[c]
                    pe.wait_ge(attn, done(n))
                    pe.wait_ge(x1_out, bank_free(n))
                    nc.tensor.matmul(o_ps[:, 0:w], m.weight("e_o"), att[:, c, 0:w], start=True, stop=True).then_inc(proj, 1)
                for c in range(NC):
                    n, w = b * NC + c, CW[c]
                    pe.wait_ge(x1_out, done(n))
                    pe.wait_ge(centred, bank_free(n))
                    nc.tensor.matmul(mean_ps[:, 0:w], m.mean_w[:, :], x1[:, c, 0:w], start=True, stop=True).then_inc(mean, 1)
                for c in range(NC):
                    n, w = b * NC + c, CW[c]
                    pe.wait_ge(squared, done(n))
                    pe.wait_ge(dev, bank_free(n))
                    nc.tensor.matmul(var_ps[:, 0:w], m.mean_w[:, :], sq[:, c, 0:w], start=True, stop=True).then_inc(var, 1)
                for c in range(NC):
                    n, w = b * NC + c, CW[c]
                    pe.wait_ge(normed, done(n))
                    for j in range(4):
                        pe.wait_ge(relu, n * 4 + j + 1)
                        nc.tensor.matmul(f1_ps[:, j % 2, 0:w], m.weight("e_f1", j), xn[:, c, 0:w], start=True, stop=True).then_inc(f1_mm, 1)
                    pe.wait_ge(mem, bank_free(n))
                    for j in range(4):
                        pe.wait_ge(relu, n * 4 + j + 3)
                        last = nc.tensor.matmul(f2_ps[:, 0:w], m.weight("e_f2", j), hid[:, c, j, 0:w], start=(j == 0), stop=(j == 3))
                    last.then_inc(f2_mm, 1)
                pe.wait_ge(kl_out, done(b * NC + NC - 1))
                pe.wait_ge(vl_out, done(b * NC + NC - 1))
                keys_values(b, x1, "c_k", "c_v", lambda c, n: pe.wait_ge(mem, done(n)), kc_mm, vc_mm, kc_out, vc_out)

        @block.scalar
        def _(act):
            for s in (dev, normed, kl_out, kc_out, vl_out, vc_out):
                act.sem_inc(s, NC)
            act.sem_inc(relu, 2)

            def keys_values(b, k, v, k_name, k_mm, v_mm, k_out, v_out, k_st, v_st):
                for c in range(NC):
                    n, w = b * NC + c, CW[c]
                    act.wait_ge(k_mm, done(n))
                    act.wait_ge(k_st[c], b * 16 + 16)
                    nc.scalar.activation(k[:, c, 0:w], k_ps[:, 0:w], ACT.Identity, bias=m.column(k_name)).then_inc(k_out, 1)
                    act.wait_ge(v_mm, done(n))
                    act.wait_ge(v_st[c], b * 16 + 16)
                    full = w // KT
                    last = nc.scalar.activation(v[:, c, 0:full, :], v_ps[0:KT, 0:D * full].rearrange("p (t d) -> p t d", t=full), ACT.Copy)
                    if w % KT:
                        rows = w - KT * full
                        last = nc.scalar.activation(v[0:rows, c, full, :], v_ps[0:rows, D * full:D * full + D], ACT.Copy)
                    last.then_inc(v_out, 1)

            act.wait_ge(v_zero, 2)
            with act.Fori(0, B) as b:
                keys_values(b, kl, vl, "t_bk", kl_mm, vl_mm, kl_out, vl_out, kl_st, vl_st)
                for c in range(NC):
                    n, w = b * NC + c, CW[c]
                    act.wait_ge(var, done(n))
                    act.wait_ge(scaled, slot_free(n))
                    nc.scalar.activation(sd[:, c, 0:w], var_ps[:, 0:w], ACT.Sqrt, bias=m.eps[:, 0:1]).then_inc(dev, 1)
                for c in range(NC):
                    n, w = b * NC + c, CW[c]
                    act.wait_ge(scaled, done(n))
                    act.wait_ge(f2_mm, slot_free(n))
                    nc.scalar.activation(xn[:, c, 0:w], xc[:, c, 0:w], ACT.Identity, scale=m.column("e_n2s"), bias=m.column("e_n2b")).then_inc(normed, 1)
                for c in range(NC):
                    n, w = b * NC + c, CW[c]
                    act.wait_ge(f2_mm, slot_free(n))
                    for j in range(4):
                        act.wait_ge(f1_mm, n * 4 + j + 1)
                        nc.scalar.activation(hid[:, c, j, 0:w], f1_ps[:, j % 2, 0:w], ACT.Relu, bias=m.column("e_b1", j)).then_inc(relu, 1)
                keys_values(b, kc, vc, "c_bk", kc_mm, vc_mm, kc_out, vc_out, kc_st, vc_st)

        @block.vector
        def _(dve):
            for s in (x1_out, centred, recip, scaled, mem):
                dve.sem_inc(s, NC)
            nc.vector.memset(vc[:, NC - 1, 3, :], 0.0).then_inc(v_zero, 1)
            nc.vector.memset(vl[:, NC - 1, 3, :], 0.0).then_inc(v_zero, 1)
            dve.wait_ge(den_in, 16)
            nc.vector.reciprocal(den[:, :], den[:, :]).then_inc(den_done, 1)
            with dve.Fori(0, B) as b:
                for c in range(NC):
                    n, w = b * NC + c, CW[c]
                    dve.wait_ge(proj, done(n))
                    dve.wait_ge(x_loaded[c], b * 16 + 16)
                    dve.wait_ge(vc_mm, slot_free(n))
                    nc.vector.scalar_tensor_tensor(out=x1[:, c, 0:w], in0=o_ps[:, 0:w], scalar=m.column("e_bo"), in1=x[:, c, 0:w], op0=ALU.add, op1=ALU.add).then_inc(x1_out, 1)
                for c in range(NC):
                    n, w = b * NC + c, CW[c]
                    dve.wait_ge(mean, done(n))
                    dve.wait_ge(normed, slot_free(n))
                    nc.vector.tensor_tensor(xc[:, c, 0:w], x1[:, c, 0:w], mean_ps[:, 0:w], ALU.subtract).then_inc(centred, 1)
                for c in range(NC):
                    n, w = b * NC + c, CW[c]
                    dve.wait_ge(dev, done(n))
                    nc.vector.reciprocal(sd[:, c, 0:w], sd[:, c, 0:w]).then_inc(recip, 1)
                    dve.wait_ge(recip, done(n))
                    nc.vector.tensor_tensor(xc[:, c, 0:w], xc[:, c, 0:w], sd[:, c, 0:w], ALU.mult).then_inc(scaled, 1)
                for c in range(NC):
                    n, w = b * NC + c, CW[c]
                    dve.wait_ge(f2_mm, done(n))
                    nc.vector.scalar_tensor_tensor(out=x1[:, c, 0:w], in0=f2_ps[:, 0:w], scalar=m.column("e_b2"), in1=x1[:, c, 0:w], op0=ALU.add, op1=ALU.add).then_inc(mem, 1)


NB = 2
HW = B * Q // NB
LEAD = 2


class Norm:

    def __init__(self, nc, ctx, m, tag, scale, shift):
        sem = lambda n: nc.alloc_semaphore(f"{tag}_{n}")
        self.nc, self.m, self.scale, self.shift = nc, m, scale, shift
        self.mean, self.centred, self.squared, self.var, self.dev, self.recip, self.scaled, self.normed = (
            sem(n) for n in ("mean", "centred", "squared", "var", "dev", "recip", "scaled", "normed"))
        sb = lambda n: ctx.enter_context(nc.sbuf_tensor(f"{tag}_{n}", [128, NB, HW], mybir.dt.float32))
        self.xc, self.sq, self.sd, self.out = sb("xc"), sb("sq"), sb("sd"), sb("out")

    def tensor(self, pe, src, src_ready, mean_ps, var_ps):
        for i in range(NB):
            if src_ready is not None:
                pe.wait_ge(src_ready, i + 1)
            self.nc.tensor.matmul(mean_ps[i][:, 0:HW], self.m.mean_w[:, :], src[:, i, :], start=True, stop=True).then_inc(self.mean, 1)
        for i in range(NB):
            pe.wait_ge(self.squared, i + 1)
            self.nc.tensor.matmul(var_ps[i][:, 0:HW], self.m.mean_w[:, :], self.sq[:, i, :], start=True, stop=True).then_inc(self.var, 1)

    def vector(self, dve, src, mean_ps):
        ALU = mybir.AluOpType
        for i in range(NB):
            dve.wait_ge(self.mean, i + 1)
            self.nc.vector.tensor_tensor(self.xc[:, i, :], src[:, i, :], mean_ps[i][:, 0:HW], ALU.subtract).then_inc(self.centred, 1)
        for i in range(NB):
            dve.wait_ge(self.dev, i + 1)
            self.nc.vector.reciprocal(self.sd[:, i, :], self.sd[:, i, :]).then_inc(self.recip, 1)
            dve.wait_ge(self.recip, i + 1)
            self.nc.vector.tensor_tensor(self.xc[:, i, :], self.xc[:, i, :], self.sd[:, i, :], ALU.mult).then_inc(self.scaled, 1)

    def gpsimd(self, pool):
        for i in range(NB):
            pool.wait_ge(self.centred, i + 1)
            self.nc.gpsimd.tensor_tensor(self.sq[:, i, :], self.xc[:, i, :], self.xc[:, i, :], mybir.AluOpType.mult).then_inc(self.squared, 1)

    def scalar(self, act, var_ps):
        ACT = mybir.ActivationFunctionType
        for i in range(NB):
            act.wait_ge(self.var, i + 1)
            self.nc.scalar.activation(self.sd[:, i, :], var_ps[i][:, 0:HW], ACT.Sqrt, bias=self.m.eps[:, 0:1]).then_inc(self.dev, 1)
        for i in range(NB):
            act.wait_ge(self.scaled, i + 1)
            self.nc.scalar.activation(self.out[:, i, :], self.xc[:, i, :], ACT.Identity, scale=self.m.column(self.scale), bias=self.m.column(self.shift)).then_inc(self.normed, 1)


def target_self_phase(nc, m):
    fp32 = DTS["fp32"]
    ALU, ACT, AX = mybir.AluOpType, mybir.ActivationFunctionType, mybir.AxisListType
    ctx = ExitStack()
    with ctx:
        sb = lambda name, shape: ctx.enter_context(nc.sbuf_tensor(f"s_{name}", shape, fp32))
        sem = lambda name: nc.alloc_semaphore(f"s_{name}")
        q, k = sb("q", [128, B, Q]), sb("k", [128, B, Q])
        v = sb("v", [Q, B, D])
        bias, mask = sb("bias", [Q, H, Q]), sb("mask", [Q, Q])
        att = sb("att", [128, NB, HW])
        qh, kb, vb = sb("qh", [128, H, Q]), sb("kb", [128, Q]), sb("vb", [Q, D])
        probs, turned = sb("probs", [Q, H, Q]), sb("turned", [Q, H, Q])
        top, total = sb("top", [Q, H]), sb("total", [Q, H])
        out, biased = sb("o", [Q, D]), sb("biased", [Q, D])
        bank = ctx.enter_context(nc.psum_tensor("s_bank", [128, 8, 512], fp32))
        n1 = Norm(nc, ctx, m, "n1", "d_n1s", "d_n1b")
        n2 = Norm(nc, ctx, m, "n2", "d_n2s", "d_n2b")
        (y_in, const_in, masked, q_mm, k_mm, v_mm, q_out, k_out, v_out, gathered, scored, biased_s, topped, shifted, expd, summed,
         inverted, turned_mm, turned_out, averaged, scaled, biased_o, back, att_out, proj, y_out, cq_mm, cq_out) = (sem(n) for n in (
             "y_in", "const_in", "masked", "q_mm", "k_mm", "v_mm", "q_out", "k_out", "v_out", "gathered", "scored", "biased_s", "topped", "shifted", "expd", "summed",
             "inverted", "turned_mm", "turned_out", "averaged", "scaled", "biased_o", "back", "att_out", "proj", "y_out", "cq_mm", "cq_out"))
        passed = {e: sem(f"passed_{e}") for e in ("pool", "dve", "act")}
        block = ctx.enter_context(nc.Block())
        mean_ps, var_ps = [bank[:, i, :] for i in (0, 1)], [bank[:, i, :] for i in (2, 3)]

        @block.sync
        def _(sp):
            for i in range(NB):
                sp.dma_start(m.y[:, i, :], m.inputs["tgt"][:, HW * i:HW * i + HW]).then_inc(y_in, 16)
            sp.dma_start(bias[:, :, :], bass.AP(m.inputs["self_line"].tensor, Q - 1, [[2 * Q - 1, Q], [Q * 2 * Q, H], [1, Q]])).then_inc(const_in, 16)
            sp.dma_start(mask[:, :], m.inputs["causal"]).then_inc(const_in, 16)

        @block.tensor
        def _(pe):
            for s in (scored, turned_mm, averaged, back):
                pe.sem_inc(s, LEAD)
            pe.wait_ge(y_in, 32)
            n1.tensor(pe, m.y, None, mean_ps, var_ps)
            for i in range(NB):
                pe.wait_ge(n1.normed, i + 1)
                nc.tensor.matmul(bank[:, 4 + i, 0:HW], m.weight("s_q"), n1.out[:, i, :], start=True, stop=True).then_inc(q_mm, 1)
                nc.tensor.matmul(bank[:, 6 + i, 0:HW], m.weight("s_k"), n1.out[:, i, :], start=True, stop=True).then_inc(k_mm, 1)
            pe.wait_ge(n1.dev, 2)
            for i in range(NB):
                for b in range(4):
                    last = nc.tensor.matmul(bank[0:Q, i, D * b:D * b + D], n1.out[:, i, Q * b:Q * b + Q], m.weight("s_v"), start=True, stop=True)
                last.then_inc(v_mm, 1)
            pe.wait_ge(v_out, 2)
            pe.wait_ge(q_out, 2)
            pe.wait_ge(k_out, 2)
            with pe.Fori(0, B) as b:
                pe.wait_ge(gathered, b * 3 + 3 + LEAD)
                pe.wait_ge(biased_s, b * 4 + LEAD)
                for h in range(H):
                    last = nc.tensor.matmul(bank[0:Q, h // 4, Q * (h % 4):Q * (h % 4) + Q], qh[:, h, :], kb[:, :], start=True, stop=True)
                    if h % 4 == 3:
                        last.then_inc(scored, 1)
                pe.wait_ge(expd, b + 1 + LEAD)
                for r in range(2):
                    pe.wait_ge(turned_out, b * 2 + r + LEAD)
                    for h in range(8):
                        last = nc.tensor.transpose(bank[0:Q, 4 + h // 4, Q * (h % 4):Q * (h % 4) + Q], probs[:, 8 * r + h, :], m.ident[0:Q, 0:Q])
                    last.then_inc(turned_mm, 1)
                pe.wait_ge(turned_out, b * 2 + 2 + LEAD)
                pe.wait_ge(scaled, b + LEAD)
                for h in range(H):
                    last = nc.tensor.matmul(bank[0:Q, 6, HD * h:HD * h + HD], turned[:, h, :], vb[:, HD * h:HD * h + HD], start=True, stop=True)
                last.then_inc(averaged, 1)
                pe.wait_ge(biased_o, b + 1 + LEAD)
                pe.wait_ge(att_out, b + LEAD)
                nc.tensor.transpose(bank[:, 7, 0:Q], biased[:, :], m.ident[0:Q, 0:Q]).then_inc(back, 1)
            pe.wait_ge(att_out, B + LEAD)
            for i in range(NB):
                nc.tensor.matmul(bank[:, 4 + i, 0:HW], m.weight("s_o"), att[:, i, :], start=True, stop=True).then_inc(proj, 1)
            n2.tensor(pe, m.y, y_out, mean_ps, var_ps)
            for i in range(NB):
                pe.wait_ge(n2.normed, i + 1)
                nc.tensor.matmul(bank[:, 6 + i, 0:HW], m.weight("c_q"), n2.out[:, i, :], start=True, stop=True).then_inc(cq_mm, 1)

        @block.gpsimd
        def _(pool):
            for s in (gathered,):
                pool.sem_inc(s, LEAD)
            n1.gpsimd(pool)
            pool.wait_ge(q_out, 2)
            pool.wait_ge(k_out, 2)
            pool.wait_ge(v_out, 2)
            with pool.Fori(0, B) as b:
                wait_alone(pool, scored, b * 4 + LEAD, passed["pool"])
                wait_alone(pool, averaged, b + LEAD, passed["pool"])
                nc.gpsimd.tensor_tensor(qh[:, :, :], q[:, bass.ds(b, 1), :].to_broadcast([128, H, Q]), m.head_mask[:, :].unsqueeze(2).to_broadcast([128, H, Q]), ALU.mult).then_inc(gathered, 1)
                nc.gpsimd.tensor_copy(kb[:, :], k[:, bass.ds(b, 1), :].rearrange("p o x -> p (o x)")).then_inc(gathered, 1)
                nc.gpsimd.tensor_copy(vb[:, :], v[:, bass.ds(b, 1), :].rearrange("p o x -> p (o x)")).then_inc(gathered, 1)
            n2.gpsimd(pool)

        @block.scalar
        def _(act):
            for s in (expd, turned_out):
                act.sem_inc(s, LEAD)
            n1.scalar(act, var_ps)
            for i in range(NB):
                act.wait_ge(k_mm, i + 1)
                nc.scalar.activation(k[:, 4 * i:4 * i + 4, :].rearrange("p b x -> p (b x)"), bank[:, 6 + i, 0:HW], ACT.Identity, bias=m.column("s_bk")).then_inc(k_out, 1)
            with act.Fori(0, B) as b:
                wait_alone(act, shifted, b + 1 + LEAD, passed["act"])
                nc.scalar.activation(probs[:, :, :], probs[:, :, :], ACT.Exp).then_inc(expd, 1)
                for r in range(2):
                    wait_alone(act, turned_mm, b * 2 + r + 1 + LEAD, passed["act"])
                    wait_alone(act, averaged, b + LEAD, passed["act"])
                    nc.scalar.activation(turned[:, 8 * r:8 * r + 8, :].rearrange("p (g h) x -> p g (h x)", g=2), bank[0:Q, 4:6, 0:4 * Q], ACT.Copy).then_inc(turned_out, 1)
            n2.scalar(act, var_ps)

        @block.vector
        def _(dve):
            for s in (biased_s, topped, shifted, summed, inverted, scaled, biased_o, att_out):
                dve.sem_inc(s, LEAD)
            n1.vector(dve, m.y, mean_ps)
            for i in range(NB):
                dve.wait_ge(q_mm, i + 1)
                nc.vector.tensor_scalar(q[:, 4 * i:4 * i + 4, :].rearrange("p b x -> p (b x)"), bank[:, 4 + i, 0:HW], m.column("s_bq"), SCALE, ALU.add, ALU.mult).then_inc(q_out, 1)
            dve.wait_ge(const_in, 32)
            nc.vector.tensor_tensor(bias[:, :, :], bias[:, :, :], mask[:, :].unsqueeze(1).to_broadcast([Q, H, Q]), ALU.add).then_inc(masked, 1)
            for i in range(NB):
                dve.wait_ge(v_mm, i + 1)
                nc.vector.tensor_copy(v[:, 4 * i:4 * i + 4, :].rearrange("p b x -> p (b x)"), bank[0:Q, i, :]).then_inc(v_out, 1)
            dve.wait_ge(masked, 1)
            with dve.Fori(0, B) as b:
                for g in range(4):
                    dve.wait_ge(scored, b * 4 + g + 1 + LEAD)
                    if g == 0:
                        dve.wait_ge(turned_mm, b * 2 + LEAD)
                    nc.vector.tensor_tensor(probs[:, 4 * g:4 * g + 4, :], bank[0:Q, g, 0:4 * Q].rearrange("p (h x) -> p h x", h=4), bias[:, 4 * g:4 * g + 4, :], ALU.add).then_inc(biased_s, 1)
                dve.wait_ge(biased_s, b * 4 + 4 + LEAD)
                nc.vector.tensor_reduce(top[:, :], probs[:, :, :], AX.X, ALU.max).then_inc(topped, 1)
                dve.wait_ge(topped, b + 1 + LEAD)
                nc.vector.tensor_tensor(probs[:, :, :], probs[:, :, :], top[:, :].unsqueeze(2).to_broadcast([Q, H, Q]), ALU.subtract).then_inc(shifted, 1)
                dve.wait_ge(expd, b + 1 + LEAD)
                nc.vector.tensor_reduce(total[:, :], probs[:, :, :], AX.X, ALU.add).then_inc(summed, 1)
                dve.wait_ge(summed, b + 1 + LEAD)
                nc.vector.reciprocal(total[:, :], total[:, :]).then_inc(inverted, 1)
                dve.wait_ge(inverted, b + 1 + LEAD)
                dve.wait_ge(averaged, b + 1 + LEAD)
                nc.vector.tensor_tensor(out[:, :].rearrange("p (h d) -> p h d", h=H), bank[0:Q, 6, 0:D].rearrange("p (h d) -> p h d", h=H), total[:, :].unsqueeze(2).to_broadcast([Q, H, HD]), ALU.mult).then_inc(scaled, 1)
                dve.wait_ge(scaled, b + 1 + LEAD)
                dve.wait_ge(back, b + LEAD)
                nc.vector.tensor_tensor(biased[:, :], out[:, :], m.row("s_bv")[0:Q, :], ALU.add).then_inc(biased_o, 1)
                dve.wait_ge(back, b + 1 + LEAD)
                nc.vector.tensor_copy(att[:, :, :].rearrange("p i (b x) -> p (i b) x", x=Q)[:, bass.ds(b, 1), :].rearrange("p o x -> p (o x)"), bank[:, 7, 0:Q]).then_inc(att_out, 1)
            for i in range(NB):
                dve.wait_ge(proj, i + 1)
                nc.vector.scalar_tensor_tensor(out=m.y[:, i, :], in0=bank[:, 4 + i, 0:HW], scalar=m.column("s_bo"), in1=m.y[:, i, :], op0=ALU.add, op1=ALU.add).then_inc(y_out, 1)
            n2.vector(dve, m.y, mean_ps)
            for i in range(NB):
                dve.wait_ge(cq_mm, i + 1)
                nc.vector.tensor_scalar(m.cq[:, 4 * i:4 * i + 4, :].rearrange("p b x -> p (b x)"), bank[:, 6 + i, 0:HW], m.column("c_bq"), SCALE, ALU.add, ALU.mult).then_inc(cq_out, 1)


def target_cross_phase(nc, m):
    fp32 = DTS["fp32"]
    ALU, ACT, AX = mybir.AluOpType, mybir.ActivationFunctionType, mybir.AxisListType
    ctx = ExitStack()
    with ctx:
        sb = lambda name, shape: ctx.enter_context(nc.sbuf_tensor(f"x_{name}", shape, fp32))
        sem = lambda name: nc.alloc_semaphore(f"x_{name}")
        bias = sb("bias", [Q, H, T])
        keys = [sb(f"keys{i}", [128, T]) for i in range(2)]
        vals = [sb(f"vals{i}", [KT, NT, D]) for i in range(2)]
        qh = [sb(f"qh{i}", [128, H, Q]) for i in range(2)]
        probs = sb("probs", [Q, NQ, QC])
        turned = sb("turned", [KT, NT, Q])
        tops, top = sb("tops", [Q, 2, NQ]), sb("top", [Q, 2])
        total = sb("total", [Q, H])
        out, biased = sb("o", [Q, D]), sb("biased", [Q, D])
        s_ps = ctx.enter_context(nc.psum_tensor("x_s_ps", [128, NQ, 512], fp32))
        t_ps = ctx.enter_context(nc.psum_tensor("x_t_ps", [128, 3, 512], fp32))
        o_ps = ctx.enter_context(nc.psum_tensor("x_o_ps", [128, 512], fp32))
        (bias_in, gathered, scored, biased_s, topped, expd, turned_mm, turned_out, averaged, inverted, scaled, biased_o, back, att_out) = (sem(n) for n in (
            "bias_in", "gathered", "scored", "biased_s", "topped", "expd", "turned_mm", "turned_out", "averaged", "inverted", "scaled", "biased_o", "back", "att_out"))
        loaded = [sem(f"loaded{i}") for i in range(2)]
        passed = {e: sem(f"passed_{e}") for e in ("pool", "dve", "act", "sp")}
        block = ctx.enter_context(nc.Block())

        @block.sync
        def _(sp):
            for g in range(4):
                sp.dma_start(bias[:, 4 * g:4 * g + 4, :], bass.AP(m.inputs["cross_line"].tensor, 4 * g * Q * (T + Q) + Q - 1, [[T + Q - 1, Q], [Q * (T + Q), 4], [1, T]])).then_inc(bias_in, 16)
            with sp.Fori(0, B // 2) as pair:
                for i in range(2):
                    b = pair * 2 + i
                    wait_alone(sp, att_out, pair * 2 + i - 1 + LEAD, passed["sp"])
                    sp.dma_start(keys[i][:, :], m.d_kc[b, :, :]).then_inc(loaded[i], 16)
                    sp.dma_start(vals[i][:, :, :], m.d_vc[b, :, :, :]).then_inc(loaded[i], 16)

        @block.gpsimd
        def _(pool):
            for s in (gathered,):
                pool.sem_inc(s, LEAD)
            with pool.Fori(0, B // 2) as pair:
                for i in range(2):
                    b = pair * 2 + i
                    wait_alone(pool, att_out, pair * 2 + i - 1 + LEAD, passed["pool"])
                    nc.gpsimd.tensor_tensor(qh[i][:, :, :], m.cq[:, bass.ds(b, 1), :].to_broadcast([128, H, Q]), m.head_mask[:, :].unsqueeze(2).to_broadcast([128, H, Q]), ALU.mult).then_inc(gathered, 1)

        @block.tensor
        def _(pe):
            for s in (scored, turned_mm, averaged, back):
                pe.sem_inc(s, LEAD)
            def scores(i, n, h):
                for c in range(NQ):
                    pe.wait_ge(expd, n + LEAD)
                    nc.tensor.matmul(s_ps[0:Q, c, 0:QC], qh[i][:, h, :], keys[i][:, QC * c:QC * c + QC], start=True, stop=True).then_inc(scored, 1)

            def average(i, n, h):
                pe.wait_ge(expd, n + 1 + LEAD)
                pe.wait_ge(turned_out, n + LEAD)
                for t in range(NT):
                    rows = rows_of(t)
                    last = nc.tensor.transpose(t_ps[0:rows, t // 4, Q * (t % 4):Q * (t % 4) + Q],
                                               probs[:, :, :].rearrange("p c x -> p (c x)")[:, KT * t:KT * t + rows], m.ident[0:Q, 0:Q])
                last.then_inc(turned_mm, 1)
                pe.wait_ge(turned_out, n + 1 + LEAD)
                for t in range(NT):
                    rows = rows_of(t)
                    last = nc.tensor.matmul(o_ps[0:Q, HD * h:HD * h + HD], turned[0:rows, t, :], vals[i][0:rows, t, HD * h:HD * h + HD], start=(t == 0), stop=(t == NT - 1))
                last.then_inc(averaged, 1)

            with pe.Fori(0, B // 2) as pair:
                for i in range(2):
                    pe.wait_ge(loaded[i], pair * 32 + 32)
                    pe.wait_ge(gathered, pair * 2 + i + 1 + LEAD)
                    for h in range(H):
                        n = (pair * 2 + i) * H + h
                        scores(i, n, h)
                        average(i, n, h)
                    pe.wait_ge(biased_o, pair * 2 + i + 1 + LEAD)
                    nc.tensor.transpose(o_ps[:, 256:256 + Q], biased[:, :], m.ident[0:Q, 0:Q]).then_inc(back, 1)
                    pe.wait_ge(att_out, pair * 2 + i + 1 + LEAD)

        @block.scalar
        def _(act):
            for s in (expd,):
                act.sem_inc(s, LEAD)
            with act.Fori(0, B) as b:
                for h in range(H):
                    n = b * H + h
                    wait_alone(act, topped, n + 1 + LEAD, passed["act"])
                    wait_alone(act, turned_mm, n + LEAD, passed["act"])
                    nc.scalar.activation(probs[:, :, :], s_ps[0:Q, :, 0:QC], ACT.Exp, bias=top[:, h % 2:h % 2 + 1], accum_out=total[:, h:h + 1]).then_inc(expd, 1)

        @block.vector
        def _(dve):
            for s in (biased_s, topped, turned_out, inverted, scaled, biased_o, att_out):
                dve.sem_inc(s, LEAD)
            dve.wait_ge(bias_in, 64)
            with dve.Fori(0, B) as b:
                for h in range(H):
                    n = b * H + h
                    for c in range(NQ):
                        wait_alone(dve, scored, n * NQ + c + 1 + LEAD, passed["dve"])
                        part = s_ps[0:Q, c, 0:QC]
                        nc.vector.tensor_tensor_reduce(out=part, in0=part, in1=bias[:, h, QC * c:QC * c + QC], scale=1.0, scalar=-3e38,
                                                       op0=ALU.add, op1=ALU.max, accum_out=tops[:, h % 2, c:c + 1]).then_inc(biased_s, 1)
                    dve.wait_ge(biased_s, n * NQ + NQ + LEAD)
                    dve.wait_ge(expd, n + LEAD)
                    nc.vector.tensor_reduce(top[:, h % 2:h % 2 + 1], tops[:, h % 2, :], AX.X, ALU.max, negate=True).then_inc(topped, 1)
                    dve.wait_ge(turned_mm, n + 1 + LEAD)
                    nc.vector.tensor_copy(turned[0:KT, :, :].rearrange("p (g t) x -> p g (t x)", g=3)[:, 0:2, :], t_ps[0:KT, 0:2, 0:4 * Q])
                    nc.vector.tensor_copy(turned[0:KT, 8:11, :].rearrange("p t x -> p (t x)"), t_ps[0:KT, 2, 0:3 * Q])
                    nc.vector.tensor_copy(turned[0:LAST, 11, :], t_ps[0:LAST, 2, 3 * Q:4 * Q]).then_inc(turned_out, 1)
                dve.wait_ge(expd, b * H + H + LEAD)
                nc.vector.reciprocal(total[:, :], total[:, :]).then_inc(inverted, 1)
                dve.wait_ge(inverted, b + 1 + LEAD)
                dve.wait_ge(averaged, b * H + H + LEAD)
                nc.vector.tensor_tensor(out[:, :].rearrange("p (h d) -> p h d", h=H), o_ps[0:Q, 0:D].rearrange("p (h d) -> p h d", h=H), total[:, :].unsqueeze(2).to_broadcast([Q, H, HD]), ALU.mult).then_inc(scaled, 1)
                dve.wait_ge(scaled, b + 1 + LEAD)
                nc.vector.tensor_tensor(biased[:, :], out[:, :], m.row("c_bv")[0:Q, :], ALU.add).then_inc(biased_o, 1)
                dve.wait_ge(back, b + 1 + LEAD)
                nc.vector.tensor_copy(m.att[:, :, :].rearrange("p i (b x) -> p (i b) x", x=Q)[:, bass.ds(b, 1), :].rearrange("p o x -> p (o x)"), o_ps[:, 256:256 + Q]).then_inc(att_out, 1)



def target_forward_phase(nc, m):
    fp32 = DTS["fp32"]
    ALU, ACT, AX = mybir.AluOpType, mybir.ActivationFunctionType, mybir.AxisListType
    ctx = ExitStack()
    with ctx:
        sb = lambda name, shape: ctx.enter_context(nc.sbuf_tensor(f"f_{name}", shape, fp32))
        sem = lambda name: nc.alloc_semaphore(f"f_{name}")
        hid = sb("hid", [128, NB, 4, HW])
        score = sb("score", [1, B * Q])
        row, col = sb("row", [Q, B, Q]), sb("col", [Q, B])
        above, level = sb("above", [Q, B, Q]), sb("level", [Q, B, Q])
        rank = sb("rank", [Q, B])
        onehot = sb("onehot", [Q, B, TOPK])
        before, slots = sb("before", [Q, Q]), sb("slots", [Q, TOPK])
        picked, tq = sb("picked", [128, B * TOPK]), sb("tq", [128, B, TOPK])
        bank = ctx.enter_context(nc.psum_tensor("f_bank", [128, 8, 512], fp32))
        n3 = Norm(nc, ctx, m, "n3", "d_n3s", "d_n3b")
        (const_in, proj, y2, f1_mm, relu, f2_mm, y3, score_mm, score_out, score_st, rank_in, tok_mm, tok_out, ranked, pick_mm, picked_s,
         q_mm, q_out, hot_mm, step) = (sem(n) for n in (
             "const_in", "proj", "y2", "f1_mm", "relu", "f2_mm", "y3", "score_mm", "score_out", "score_st", "rank_in", "tok_mm", "tok_out", "ranked", "pick_mm", "picked_s",
             "q_mm", "q_out", "hot_mm", "step"))
        block = ctx.enter_context(nc.Block())
        mean_ps, var_ps = [bank[:, i, :] for i in (0, 1)], [bank[:, i, :] for i in (2, 3)]

        @block.sync
        def _(sp):
            sp.dma_start(before[:, :], m.inputs["before"]).then_inc(const_in, 16)
            sp.dma_start(slots[:, :], m.inputs["slots"]).then_inc(const_in, 16)
            sp.wait_ge(score_out, 3)
            sp.dma_start(m.d_score[0:1, :], score[:, :]).then_inc(score_st, 16)
            sp.wait_ge(score_st, 16)
            sp.dma_start(row[:, :, :], m.d_score[0:1, :].to_broadcast([Q, B * Q]).rearrange("p (b x) -> p b x", b=B)).then_inc(rank_in, 16)
            sp.dma_start(col[:, :], m.d_score[0, :].rearrange("(b x) -> x b", b=B), allow_slow_non_contiguous=True).then_inc(rank_in, 16)
            sp.wait_ge(const_in, 32)

        @block.tensor
        def _(pe):
            for i in range(NB):
                nc.tensor.matmul(bank[:, 4 + i, 0:HW], m.weight("c_o"), m.att[:, i, :], start=True, stop=True).then_inc(proj, 1)
            n3.tensor(pe, m.y, y2, mean_ps, var_ps)
            for i in range(NB):
                pe.wait_ge(n3.normed, i + 1)
                for j in range(4):
                    k = 4 * i + j
                    if k >= 2:
                        pe.wait_ge(relu, k - 1)
                    nc.tensor.matmul(bank[:, 4 + k % 2, 0:HW], m.weight("d_f1", j), n3.out[:, i, :], start=True, stop=True).then_inc(f1_mm, 1)
                for j in range(4):
                    pe.wait_ge(relu, 4 * i + j + 1)
                    last = nc.tensor.matmul(bank[:, 6 + i, 0:HW], m.weight("d_f2", j), hid[:, i, j, :], start=(j == 0), stop=(j == 3))
                last.then_inc(f2_mm, 1)
            for i in range(NB):
                pe.wait_ge(y3, i + 1)
                nc.tensor.matmul(bank[0:1, i, 0:HW], m.column("score"), m.y[:, i, :], start=True, stop=True).then_inc(score_mm, 1)
            for i in range(NB):
                for b in range(4):
                    last = nc.tensor.transpose(bank[0:Q, 2 + i, D * b:D * b + D], m.y[:, i, Q * b:Q * b + Q], m.ident[:, :])
                last.then_inc(tok_mm, 1)
            pe.wait_ge(tok_out, 2)
            pe.wait_ge(ranked, 1)
            for b in range(B):
                last = nc.tensor.matmul(bank[:, 4, TOPK * b:TOPK * b + TOPK], m.tok[:, b, :], onehot[:, b, :], start=True, stop=True)
            last.then_inc(pick_mm, 1)
            for b in range(B):
                last = nc.tensor.transpose(bank[0:TOPK, 6 + b // 4, Q * (b % 4):Q * (b % 4) + Q], onehot[:, b, :], m.ident[0:Q, 0:Q])
            last.then_inc(hot_mm, 1)
            pe.wait_ge(picked_s, 1)
            nc.tensor.matmul(bank[:, 5, 0:B * TOPK], m.weight("t_q"), picked[:, :], start=True, stop=True).then_inc(q_mm, 1)

        @block.gpsimd
        def _(pool):
            n3.gpsimd(pool)
            pool.wait_ge(q_out, 1)
            nc.gpsimd.tensor_tensor(m.tqh[:, :, :, :], tq[:, :, :].unsqueeze(2).to_broadcast([128, B, H, TOPK]),
                                    m.head_mask[:, :].unsqueeze(1).unsqueeze(3).to_broadcast([128, B, H, TOPK]), ALU.mult).then_inc(q_out, 1)

        @block.scalar
        def _(act):
            n3.scalar(act, var_ps)
            for k in range(4 * NB):
                act.wait_ge(f1_mm, k + 1)
                nc.scalar.activation(hid[:, k // 4, k % 4, :], bank[:, 4 + k % 2, 0:HW], ACT.Relu, bias=m.column("d_b1", k % 4)).then_inc(relu, 1)
            act.wait_ge(hot_mm, 1)
            nc.scalar.activation(m.hot[:, :, :].rearrange("p (g b) x -> p g (b x)", g=2), bank[0:TOPK, 6:8, 0:4 * Q], ACT.Copy).then_inc(hot_mm, 1)

        @block.vector
        def _(dve):
            for i in range(NB):
                dve.wait_ge(proj, i + 1)
                nc.vector.scalar_tensor_tensor(out=m.y[:, i, :], in0=bank[:, 4 + i, 0:HW], scalar=m.column("c_bo"), in1=m.y[:, i, :], op0=ALU.add, op1=ALU.add).then_inc(y2, 1)
            n3.vector(dve, m.y, mean_ps)
            for i in range(NB):
                dve.wait_ge(f2_mm, i + 1)
                nc.vector.scalar_tensor_tensor(out=m.y[:, i, :], in0=bank[:, 6 + i, 0:HW], scalar=m.column("d_b2"), in1=m.y[:, i, :], op0=ALU.add, op1=ALU.add).then_inc(y3, 1)
            for i in range(NB):
                dve.wait_ge(score_mm, i + 1)
                nc.vector.tensor_copy(score[:, HW * i:HW * i + HW], bank[0:1, i, 0:HW]).then_inc(score_out, 1)
            dve.wait_ge(score_out, 2)
            nc.vector.tensor_scalar(score[:, :], score[:, :], m.score_b[0:1, 0:1], None, ALU.add).then_inc(score_out, 1)
            for i in range(NB):
                dve.wait_ge(tok_mm, i + 1)
                nc.vector.tensor_copy(m.tok[:, 4 * i:4 * i + 4, :].rearrange("p b x -> p (b x)"), bank[0:Q, 2 + i, :]).then_inc(tok_out, 1)
            dve.wait_ge(const_in, 32)
            dve.wait_ge(rank_in, 32)
            mine = col[:, :].unsqueeze(2).to_broadcast([Q, B, Q])
            nc.vector.tensor_tensor(above[:, :, :], row[:, :, :], mine, ALU.is_gt).then_inc(step, 1)
            nc.vector.tensor_tensor(level[:, :, :], row[:, :, :], mine, ALU.is_equal).then_inc(step, 1)
            dve.wait_ge(step, 2)
            nc.vector.tensor_tensor(level[:, :, :], level[:, :, :], before[:, :].unsqueeze(1).to_broadcast([Q, B, Q]), ALU.mult).then_inc(step, 1)
            dve.wait_ge(step, 3)
            nc.vector.tensor_tensor(above[:, :, :], above[:, :, :], level[:, :, :], ALU.add).then_inc(step, 1)
            dve.wait_ge(step, 4)
            nc.vector.tensor_reduce(rank[:, :], above[:, :, :], AX.X, ALU.add).then_inc(step, 1)
            dve.wait_ge(step, 5)
            nc.vector.tensor_scalar(m.kept[:, :], rank[:, :], float(TOPK), None, ALU.is_ge).then_inc(step, 1)
            nc.vector.tensor_tensor(onehot[:, :, :], rank[:, :].unsqueeze(2).to_broadcast([Q, B, TOPK]), slots[:, :].unsqueeze(1).to_broadcast([Q, B, TOPK]), ALU.is_equal).then_inc(ranked, 1)
            dve.wait_ge(pick_mm, 1)
            nc.vector.tensor_copy(picked[:, :], bank[:, 4, 0:B * TOPK]).then_inc(picked_s, 1)
            dve.wait_ge(q_mm, 1)
            nc.vector.tensor_scalar(tq[:, :, :].rearrange("p b r -> p (b r)"), bank[:, 5, 0:B * TOPK], m.column("t_bq"), SCALE, ALU.add, ALU.mult).then_inc(q_out, 1)


GH = H // 2
GR = GH * TOPK


def last_attention_phase(nc, m):
    fp32 = DTS["fp32"]
    ALU, ACT, AX = mybir.AluOpType, mybir.ActivationFunctionType, mybir.AxisListType
    ctx = ExitStack()
    with ctx:
        sb = lambda name, shape: ctx.enter_context(nc.sbuf_tensor(f"l_{name}", shape, fp32))
        sem = lambda name: nc.alloc_semaphore(f"l_{name}")
        keys = [sb(f"keys{i}", [128, T]) for i in range(2)]
        vals = [sb(f"vals{i}", [KT, NT, D]) for i in range(2)]
        qh = [sb(f"qh{i}", [128, H, TOPK]) for i in range(2)]
        probs, turned = sb("probs", [GR, NQ, QC]), sb("turned", [KT, NT, GR])
        top, total = sb("top", [GR, 2]), sb("total", [GR, 2])
        own = sb("own", [GR, 2, D])
        fold = sb("fold", [GR, TOPK])
        mine = sb("mine", [GR, 2, D])
        joined, rows_out = sb("joined", [128, TOPK]), sb("rows_out", [TOPK, B, D])
        final = sb("final", [Q, B, D])
        s_ps = ctx.enter_context(nc.psum_tensor("l_s_ps", [128, NQ, 512], fp32))
        t_ps = ctx.enter_context(nc.psum_tensor("l_t_ps", [128, 2, 512], fp32))
        o_ps = ctx.enter_context(nc.psum_tensor("l_o_ps", [128, 512], fp32))
        j_ps = ctx.enter_context(nc.psum_tensor("l_j_ps", [128, 512], fp32))
        (const_in, gathered, scored, topped, expd, turned_mm, turned_out, averaged, inverted, masked, folded, joined_s, proj, rows_s, placed, out_s, out_st) = (sem(n) for n in (
            "const_in", "gathered", "scored", "topped", "expd", "turned_mm", "turned_out", "averaged", "inverted", "masked", "folded", "joined_s", "proj", "rows_s", "placed", "out_s", "out_st"))
        loaded = [sem(f"loaded{i}") for i in range(2)]
        passed = {e: sem(f"passed_{e}") for e in ("pool", "sp", "act", "dve")}
        block = ctx.enter_context(nc.Block())

        @block.sync
        def _(sp):
            sp.dma_start(own[:, :, :], m.inputs["own"]).then_inc(const_in, 16)
            sp.dma_start(fold[:, :], m.inputs["fold"]).then_inc(const_in, 16)
            with sp.Fori(0, B // 2) as pair:
                for i in range(2):
                    b = pair * 2 + i
                    wait_alone(sp, rows_s, b - 1 + LEAD, passed["sp"])
                    sp.dma_start(keys[i][:, :], m.d_kl[b, :, :]).then_inc(loaded[i], 16)
                    sp.dma_start(vals[i][:, :, :], m.d_vl[b, :, :, :]).then_inc(loaded[i], 16)
            for b in range(B):
                sp.wait_ge(out_s, b + 1)
                sp.dma_start(m.out[b, :, :], final[:, b, :]).then_inc(out_st, 16)
            sp.wait_ge(out_st, 16 * B)

        @block.gpsimd
        def _(pool):
            pool.sem_inc(gathered, LEAD)
            with pool.Fori(0, B // 2) as pair:
                for i in range(2):
                    b = pair * 2 + i
                    wait_alone(pool, rows_s, b - 1 + LEAD, passed["pool"])
                    nc.gpsimd.tensor_copy(qh[i][:, :, :], m.tqh[:, bass.ds(b, 1), :, :].rearrange("p o h r -> p (o h) r")).then_inc(gathered, 1)

        @block.tensor
        def _(pe):
            for s in (scored, turned_mm, averaged, folded, proj):
                pe.sem_inc(s, LEAD)
            pe.wait_ge(const_in, 32)
            with pe.Fori(0, B // 2) as pair:
                for i in range(2):
                    b = pair * 2 + i
                    pe.wait_ge(loaded[i], pair * 32 + 32)
                    pe.wait_ge(gathered, b + 1 + LEAD)
                    for g in range(2):
                        n = b * 2 + g
                        pe.wait_ge(expd, n + LEAD)
                        for c in range(NQ):
                            last = nc.tensor.matmul(s_ps[0:GR, c, 0:QC], qh[i][:, GH * g:GH * g + GH, :].rearrange("p h r -> p (h r)"), keys[i][:, QC * c:QC * c + QC], start=True, stop=True)
                        last.then_inc(scored, 1)
                        pe.wait_ge(expd, n + 1 + LEAD)
                        pe.wait_ge(turned_out, n + LEAD)
                        for t in range(NT):
                            rows = rows_of(t)
                            last = nc.tensor.transpose(t_ps[0:rows, t // 6, GR * (t % 6):GR * (t % 6) + GR], probs[:, :, :].rearrange("p c x -> p (c x)")[:, KT * t:KT * t + rows], m.ident[0:GR, 0:GR])
                        last.then_inc(turned_mm, 1)
                        pe.wait_ge(turned_out, n + 1 + LEAD)
                        pe.wait_ge(masked, n + LEAD)
                        for t in range(NT):
                            rows = rows_of(t)
                            last = nc.tensor.matmul(o_ps[0:GR, 0:D], turned[0:rows, t, :], vals[i][0:rows, t, :], start=(t == 0), stop=(t == NT - 1))
                        last.then_inc(averaged, 1)
                    pe.wait_ge(masked, b * 2 + 2 + LEAD)
                    pe.wait_ge(rows_s, b + LEAD)
                    for g in range(2):
                        last = nc.tensor.matmul(j_ps[:, 0:TOPK], mine[:, g, :], fold[:, :], start=(g == 0), stop=(g == 1))
                    last.then_inc(folded, 1)
                    pe.wait_ge(joined_s, b + 1 + LEAD)
                    nc.tensor.matmul(j_ps[0:TOPK, 128:128 + D], joined[:, :], m.weight("t_o"), start=True, stop=True).then_inc(proj, 1)
            pe.wait_ge(rows_s, B + LEAD)
            for b in range(B):
                last = nc.tensor.matmul(s_ps[0:Q, b // 4, D * (b % 4):D * (b % 4) + D], m.hot[:, b, :], rows_out[:, b, :], start=True, stop=True)
                last.then_inc(placed, 1)

        @block.scalar
        def _(act):
            act.sem_inc(expd, LEAD)
            act.sem_inc(turned_out, LEAD)
            with act.Fori(0, B) as b:
                for g in range(2):
                    n = b * 2 + g
                    wait_alone(act, topped, n + 1 + LEAD, passed["act"])
                    wait_alone(act, turned_mm, n + LEAD, passed["act"])
                    nc.scalar.activation(probs[:, :, :], s_ps[0:GR, :, 0:QC], ACT.Exp, bias=top[:, g:g + 1], accum_out=total[:, g:g + 1]).then_inc(expd, 1)
                    wait_alone(act, turned_mm, n + 1 + LEAD, passed["act"])
                    nc.scalar.activation(turned[0:KT, 0:6, :].rearrange("p t x -> p (t x)"), t_ps[0:KT, 0, 0:6 * GR], ACT.Copy)
                    nc.scalar.activation(turned[0:KT, 6:11, :].rearrange("p t x -> p (t x)"), t_ps[0:KT, 1, 0:5 * GR], ACT.Copy)
                    nc.scalar.activation(turned[0:LAST, 11, :], t_ps[0:LAST, 1, 5 * GR:6 * GR], ACT.Copy).then_inc(turned_out, 1)

        @block.vector
        def _(dve):
            for s in (topped, inverted, masked, joined_s, rows_s):
                dve.sem_inc(s, LEAD)
            dve.wait_ge(const_in, 32)
            with dve.Fori(0, B) as b:
                for g in range(2):
                    n = b * 2 + g
                    dve.wait_ge(scored, n + 1 + LEAD)
                    nc.vector.tensor_reduce(top[:, g:g + 1], s_ps[0:GR, :, 0:QC], AX.XY, ALU.max, negate=True).then_inc(topped, 1)
                    dve.wait_ge(expd, n + 1 + LEAD)
                    nc.vector.reciprocal(total[:, g:g + 1], total[:, g:g + 1]).then_inc(inverted, 1)
                    dve.wait_ge(inverted, n + 1 + LEAD)
                    dve.wait_ge(averaged, n + 1 + LEAD)
                    dve.wait_ge(folded, b + LEAD)
                    nc.vector.scalar_tensor_tensor(out=mine[:, g, :], in0=o_ps[0:GR, 0:D], scalar=total[:, g:g + 1], in1=own[:, g, :], op0=ALU.mult, op1=ALU.mult).then_inc(masked, 1)
                dve.wait_ge(folded, b + 1 + LEAD)
                nc.vector.tensor_scalar(joined[:, :], j_ps[:, 0:TOPK], m.column("t_bv"), None, ALU.add).then_inc(joined_s, 1)
                dve.wait_ge(proj, b + 1 + LEAD)
                nc.vector.tensor_tensor(rows_out[:, bass.ds(b, 1), :].rearrange("p o x -> p (o x)"), j_ps[0:TOPK, 128:128 + D], m.row("t_bo")[0:TOPK, :], ALU.add).then_inc(rows_s, 1)
            for b in range(B):
                dve.wait_ge(placed, b // 4 * 4 + 4)
                nc.vector.scalar_tensor_tensor(out=final[:, b, :], in0=m.tok[:, b, :], scalar=m.kept[:, b:b + 1], in1=s_ps[0:Q, b // 4, D * (b % 4):D * (b % 4) + D], op0=ALU.mult, op1=ALU.add).then_inc(out_s, 1)



PHASES = [setup_phase, norm_and_project_phase, attention_phase, context_phase,
          target_self_phase, target_cross_phase, target_forward_phase, last_attention_phase]


def build(nc, inputs, out):
    fp32, bf16 = DTS["fp32"], DTS["bf16"]
    m = Mem()
    m.inputs = inputs
    m.out = out

    def dram(name, shape, dt):
        return nc.dram_tensor(name, shape, dt, kind="Internal").ap()

    m.d_qp = dram("d_qp", (B, 3, D, T), bf16)
    m.d_kp = dram("d_kp", (B, 3, D, T), bf16)
    m.d_v = dram("d_v", (B, H, KT, NT * HD), fp32)
    m.d_band = dram("d_band", (H, 3 * SUB, 4, BW), bf16)
    m.d_step = dram("d_step", (H, NSTEP, T), bf16)
    m.d_att = dram("d_att", (NU, HD, T), fp32)
    m.d_den = dram("d_den", (NU, T), fp32)
    m.d_shift = dram("d_shift", (SLOTS, 3, KT * NT), bf16)
    m.d_inv = dram("d_inv", (NU, T), fp32)
    m.d_kl, m.d_kc = (dram(n, (B, D, T), fp32) for n in ("d_kl", "d_kc"))
    m.d_vl, m.d_vc = (dram(n, (B, KT, NT, D), fp32) for n in ("d_vl", "d_vc"))
    m.d_score = dram("d_score", (1, B * Q), fp32)
    ctx = ExitStack()
    with ctx:
        sb = lambda name, shape, dt: ctx.enter_context(nc.sbuf_tensor(name, shape, dt))
        m.w = sb("w", [128, NW * 128], fp32)
        m.vec = sb("vec", [128, NV], fp32)
        m.rowv = sb("rowv", [128, len(ROWV), D], fp32)
        m.ident = sb("ident", [128, 128], fp32)
        m.mean_w = sb("mean_w", [128, 128], fp32)
        m.den_sel = sb("den_sel", [128, 128], fp32)
        m.eps = sb("eps", [128, 1], fp32)
        m.left = sb("left_bias", [128, H], fp32)
        m.head_mask = sb("head_mask", [128, H], fp32)
        m.score_b = sb("score_b", [1, 1], fp32)
        m.y = sb("y", [128, NB, HW], fp32)
        m.att = sb("att", [128, NB, HW], fp32)
        m.cq = sb("cq", [128, B, Q], fp32)
        m.tok = sb("tok", [Q, B, D], fp32)
        m.kept = sb("kept", [Q, B], fp32)
        m.hot = sb("hot", [TOPK, B, Q], fp32)
        m.tqh = sb("tqh", [128, B, H, TOPK], fp32)
        m.weight = lambda n, j=0: m.w[:, 128 * (WCOL[n][0] + j):128 * (WCOL[n][0] + j + 1)]
        m.column = lambda n, j=0: m.vec[:, VCOL[n][0] + j:VCOL[n][0] + j + 1]
        m.row = lambda n: m.rowv[:, ROWV.index(n), :]
        for phase in PHASES:
            with nc.cleanup_on_exit():
                phase(nc, m)


def lay_out(x):
    import numpy as np

    g = lambda n: np.asarray(x[n])
    e, t = "L0_xattn_", "L1_xattn_"

    def qkv(w):
        return [w[0:D].T, w[D:2 * D].T, w[2 * D:3 * D].T]

    def down(w):
        return [w.T[D * j:D * j + D] for j in range(4)]

    w = qkv(g(e + "enc_in_w")) + [g(e + "enc_out_w").T, g(e + "enc_ff1_w").T] + down(g(e + "enc_ff2_w"))
    w += qkv(g(e + "dec_sa_in_w")) + [g(e + "dec_sa_out_w").T] + qkv(g(e + "dec_ca_in_w")) + [g(e + "dec_ca_out_w").T]
    w += [g(e + "dec_ff1_w").T] + down(g(e + "dec_ff2_w")) + qkv(g(t + "in_proj_w")) + [g(t + "out_w").T]
    two = lambda n: [g(n)[0:D], g(n)[D:2 * D]]
    four = lambda n: [g(n)[D * j:D * j + D] for j in range(4)]
    vec = two(e + "enc_in_b") + [g(e + "enc_out_b")] + four(e + "enc_ff1_b") + [g(e + "enc_ff2_b")]
    vec += [g(e + n) for n in ("enc_n1_s", "enc_n1_b", "enc_n2_s", "enc_n2_b")]
    vec += two(e + "dec_sa_in_b") + [g(e + "dec_sa_out_b")] + two(e + "dec_ca_in_b") + [g(e + "dec_ca_out_b")]
    vec += four(e + "dec_ff1_b") + [g(e + "dec_ff2_b")]
    vec += [g(e + n) for n in ("dec_n1_s", "dec_n1_b", "dec_n2_s", "dec_n2_b", "dec_n3_s", "dec_n3_b")]
    vec += two(t + "in_proj_b") + [g(t + "in_proj_b")[2 * D:], g(t + "score_w")[0]]
    rowv = [g(n)[2 * D:] for n in (e + "enc_in_b", e + "dec_sa_in_b", e + "dec_ca_in_b", t + "in_proj_b")] + [g(t + "out_b")]
    pos = np.arange(GLEN) - G0
    at = lambda p: np.where(p < 0, np.minimum(-p, MD - 1), np.minimum(p, MD - 1) + MD)
    rev = HALO + SUB - 1 - np.arange(RLEN)
    keys, part = np.arange(T), np.arange(128)
    tile_of = keys // KT
    ind = np.zeros((96, T), np.float32)
    q_steps = np.zeros((NSTEP, T), np.float32)
    for s in range(3):
        for k in range(NT):
            ind[32 * s + k] = tile_of == k
            q_steps[NT * s + k] = keys < KT * k + SPLIT
    line = lambda n, many: np.tile(g(e + n)[at(np.arange(many) - (Q - 1))].T, (1, Q))
    token, group_row = np.arange(Q), np.arange(8 * TOPK)
    own = part[None, None, :] // HD == (8 * np.arange(2)[None, :, None] + group_row[:, None, None] // TOPK)
    bf16 = mybir.dt.np(mybir.dt.bfloat16)
    return {
        "ctx": g("ctx_1024").transpose(0, 2, 1), "tgt": g("x").transpose(2, 0, 1).reshape(D, B * Q),
        "w": np.concatenate(w, 1), "vec": np.stack(vec, 1), "rowv": np.stack(rowv),
        "line": np.tile(g(e + "enc_rel")[at(pos)].T, (1, KT)), "rev": np.tile(g(e + "enc_rel")[at(rev)].T, (1, SUB)),
        "edge": np.stack([g(e + "enc_rel")[MD - 1], g(e + "enc_rel")[2 * MD - 1]]),
        "tile_ind": ind.astype(bf16), "q_steps": q_steps.astype(bf16),
        "ones3": np.ones((3, T), bf16), "ident3": np.tile(np.eye(SUB), (3, 1)).astype(bf16),
        "ident": np.eye(128, dtype=np.float32), "mean": np.full((128, 128), 1 / D, np.float32),
        "den_sel": (part[:, None] == part[None, :] // 32 * 32 + HD).astype(np.float32),
        "self_line": line("dec_rel_self", 2 * Q), "cross_line": line("dec_rel_cross", T + Q),
        "causal": np.where(token[None, :] > token[:, None], -1e30, 0).astype(np.float32),
        "head_mask": (part[:, None] // HD == np.arange(H)[None, :]).astype(np.float32),
        "score_b": g(t + "score_b").reshape(1, 1),
        "before": (token[None, :] < token[:, None]).astype(np.float32),
        "slots": np.tile(np.arange(TOPK, dtype=np.float32), (Q, 1)),
        "own": own.astype(np.float32), "fold": (group_row[:, None] % TOPK == np.arange(TOPK)[None, :]).astype(np.float32),
        "eps": np.full((128, 1), EPS, np.float32),
    }


def kernel(**inputs):
    import numpy as np
    import concourse.bacc as bacc
    from concourse.bass_utils import run_bass_kernel_spmd

    arrays = {f"in_{n}": np.ascontiguousarray(a) for n, a in lay_out(inputs).items()}
    nc = bacc.Bacc("TRN2", target_bir_lowering=False, num_devices=1)
    aps = {n[3:]: nc.dram_tensor(n, a.shape, mybir.dt.from_np(a.dtype), kind="ExternalInput").ap() for n, a in arrays.items()}
    out = nc.dram_tensor("out", (B, Q, D), mybir.dt.float32, kind="ExternalOutput").ap()
    build(nc, aps, out)
    return run_bass_kernel_spmd(nc, [arrays], core_ids=[0]).results[0]["out"]
```

```python
import concourse.bass as bass
from concourse import mybir
from contextlib import ExitStack

B, T, Q, D, H, HD = 8, 1444, 100, 128, 16, 8
TOPK = 10
KT, NT = 121, 12
LAST = T - KT * (NT - 1)
CH, NC = 4 * KT, 3
CW = [CH, CH, T - 2 * CH]
QC, NQ = T // 4, 4
MD = 128
HALO = MD - 2
NPROD = 9 * HD
NSTEP = 3 * NT
ROWS = NPROD + NSTEP + 3
SUB = 32
BW = SUB + 2 * HALO
SPLIT = 60
STRIP0 = KT * (NT - 1)
SW = STRIP0 + T
SCALE = float(HD) ** -0.5

WCOL = {}
for _n, _k in (("e_q", 1), ("e_k", 1), ("e_v", 1), ("e_o", 1), ("e_f1", 4), ("e_f2", 4),
               ("s_q", 1), ("s_k", 1), ("s_v", 1), ("s_o", 1), ("c_q", 1), ("c_k", 1), ("c_v", 1), ("c_o", 1),
               ("d_f1", 4), ("d_f2", 4), ("t_q", 1), ("t_k", 1), ("t_v", 1), ("t_o", 1)):
    WCOL[_n] = (sum(k for _, k in WCOL.values()), _k)
NW = sum(k for _, k in WCOL.values())
VCOL = {}
for _n, _k in (("e_bq", 1), ("e_bk", 1), ("e_bo", 1), ("e_b1", 4), ("e_b2", 1), ("e_n1s", 1), ("e_n1b", 1),
               ("e_n2s", 1), ("e_n2b", 1), ("s_bq", 1), ("s_bk", 1), ("s_bo", 1), ("c_bq", 1), ("c_bk", 1), ("c_bv", 1),
               ("c_bo", 1), ("d_b1", 4), ("d_b2", 1), ("d_n1s", 1), ("d_n1b", 1), ("d_n2s", 1), ("d_n2b", 1),
               ("d_n3s", 1), ("d_n3b", 1), ("t_bq", 1), ("t_bk", 1), ("t_bv", 1), ("score", 1)):
    VCOL[_n] = (sum(k for _, k in VCOL.values()), _k)
NV = sum(k for _, k in VCOL.values())
ROWV = ["e_bv", "s_bv", "t_bo"]
EPS = 1e-6
NPOS = 3
GLEN = SW + KT - 1
RLEN = BW + SUB
G0 = STRIP0 + KT - 1

DTS = dict(fp32=mybir.dt.float32, bf16=mybir.dt.bfloat16)


class Mem:
    pass


def setup_phase(nc, m):
    fp32, bf16 = DTS["fp32"], DTS["bf16"]
    ALU, ACT = mybir.AluOpType, mybir.ActivationFunctionType
    ctx = ExitStack()
    with ctx:
        sb = lambda name, shape, dt: ctx.enter_context(nc.sbuf_tensor(name, shape, dt))
        sem = lambda name: nc.alloc_semaphore(name)
        band = sb("band", [128, H, BW], fp32)
        rest = sb("rest", [128, H, BW], fp32)
        piece = [sb(f"band_piece{s}", [128, H, BW], bf16) for s in range(3)]
        left = sb("left", [128, H], fp32)
        right = sb("right", [128, H], fp32)
        delta = sb("delta", [128, H], fp32)
        drest = sb("drest", [128, H], fp32)
        dpiece = [sb(f"delta_piece{s}", [128, H], bf16) for s in range(3)]
        dsel = sb("dsel", [128, H], fp32)
        tile_ind = sb("tile_ind", [96, T], bf16)
        steps = sb("steps", [96, 4, T], bf16)
        s_load, s_edge, s_band_in, s_ind = (sem(n) for n in ("s_load", "s_edge", "s_band_in", "s_ind"))
        s_v = sem("s_setup_vector")
        s_band, s_step, s_out = (sem(n) for n in ("s_band", "s_step", "s_setup_out"))
        s_step_out = [sem(f"s_step_out{i}") for i in range(4)]
        block = ctx.enter_context(nc.Block())

        @block.sync
        def _(sp):
            for k, src in enumerate((m.inputs["edge"][0:1, :], m.inputs["edge"][1:2, :])):
                sp.dma_start((left, right)[k][:, :], src.to_broadcast([128, H])).then_inc(s_edge, 16)
            for i in range(4):
                src = bass.AP(m.inputs["rev"].tensor, SUB - 1, [[RLEN - 1, SUB], [SUB * RLEN, H], [1, BW]])
                sp.dma_start(band[SUB * i:SUB * i + SUB, :, :], src).then_inc(s_band_in, 16)
            sp.dma_start(tile_ind[:, :], m.inputs["tile_ind"]).then_inc(s_ind, 16)
            loads = [(m.w[:, :], m.inputs["w"]), (m.vec[:, :], m.inputs["vec"]), (m.ident[:, :], m.inputs["ident"]),
                     (m.mean_w[:, :], m.inputs["mean"]), (m.den_sel[:, :], m.inputs["den_sel"]), (m.eps[:, :], m.inputs["eps"]),
                     (m.head_mask[:, :], m.inputs["head_mask"]), (m.score_b[:, :], m.inputs["score_b"])]
            loads += [(m.rowv[:, j, :], m.inputs["rowv"][j:j + 1, :].to_broadcast([128, D])) for j in range(len(ROWV))]
            for dst, src in loads:
                sp.dma_start(dst, src).then_inc(s_load, 16)
            for s in range(3):
                sp.wait_ge(s_band, s + 1)
                for i in range(4):
                    dst = m.d_band[:, SUB * s:SUB * s + SUB, i, :].rearrange("h r w -> r h w")
                    sp.dma_start(dst, piece[s][SUB * i:SUB * i + SUB, :, :]).then_inc(s_out, 16)
            for h in range(H):
                sp.wait_ge(s_step, h + 1)
                for s in range(3):
                    sp.dma_start(m.d_step[h, NT * s:NT * s + NT, :], steps[32 * s:32 * s + NT, h % 4, :]).then_inc(s_step_out[h % 4], 16)
            sp.wait_ge(s_load, 16 * len(loads))
            sp.wait_ge(s_out, 16 * 12)
            for i in range(4):
                sp.wait_ge(s_step_out[i], 48 * H // 4)

        @block.vector
        def _(dve):
            n = [0]

            def then(ins):
                n[0] += 1
                ins.then_inc(s_v, 1)
                dve.wait_ge(s_v, n[0])

            dve.wait_ge(s_edge, 32)
            then(nc.vector.tensor_copy(m.left[:, :], left[:, :]))
            then(nc.vector.tensor_tensor(delta[:, :], right[:, :], left[:, :], ALU.subtract))
            then(nc.vector.tensor_copy(dpiece[0][:, :], delta[:, :]))
            then(nc.vector.tensor_tensor(drest[:, :], delta[:, :], dpiece[0][:, :], ALU.subtract))
            then(nc.vector.tensor_copy(dpiece[1][:, :], drest[:, :]))
            then(nc.vector.tensor_tensor(dpiece[2][:, :], drest[:, :], dpiece[1][:, :], ALU.subtract))
            for s in range(3):
                then(nc.vector.tensor_copy(dsel[32 * s:32 * s + 32, :], dpiece[s][32 * s:32 * s + 32, :]))
            dve.wait_ge(s_band_in, 64)
            then(nc.vector.tensor_tensor(band[:, :, :], band[:, :, :], left[:, :].unsqueeze(2).to_broadcast([128, H, BW]), ALU.subtract))
            for i in range(4):
                w = SPLIT - SUB * i + HALO
                part = band[SUB * i:SUB * i + SUB, :, 0:w]
                then(nc.vector.tensor_tensor(part, part, delta[SUB * i:SUB * i + SUB, :].unsqueeze(2).to_broadcast([SUB, H, w]), ALU.subtract))
            then(nc.vector.tensor_copy(piece[0][:, :, :], band[:, :, :]))
            nc.vector.tensor_tensor(rest[:, :, :], band[:, :, :], piece[0][:, :, :], ALU.subtract).then_inc(s_band, 1)
            dve.wait_ge(s_band, 1)
            nc.vector.tensor_copy(piece[1][:, :, :], rest[:, :, :]).then_inc(s_band, 1)
            dve.wait_ge(s_band, 2)
            nc.vector.tensor_tensor(piece[2][:, :, :], rest[:, :, :], piece[1][:, :, :], ALU.subtract).then_inc(s_band, 1)
            dve.wait_ge(s_ind, 16)
            for h in range(H):
                if h >= 4:
                    dve.wait_ge(s_step_out[h % 4], 48 * (h // 4))
                nc.vector.tensor_scalar(steps[:, h % 4, :], tile_ind[:, :], dsel[0:96, h:h + 1], None, ALU.mult).then_inc(s_step, 1)


def done(n):
    return n + 1 + NC


def slot_free(n):
    return n + 1


def bank_free(n):
    return n + NC


def norm_and_project_phase(nc, m):
    fp32, bf16 = DTS["fp32"], DTS["bf16"]
    ALU, ACT = mybir.AluOpType, mybir.ActivationFunctionType
    ctx = ExitStack()
    with ctx:
        sb = lambda name, shape, dt: ctx.enter_context(nc.sbuf_tensor(name, shape, dt))
        x = sb("x", [128, NC, CH], fp32)
        xc = sb("xc", [128, NC, CH], fp32)
        sq = sb("sq", [128, NC, CH], fp32)
        sd = sb("sd", [128, NC, CH], fp32)
        xn = sb("xn", [128, NC, CH], fp32)
        q = sb("q", [128, NC, CH], fp32)
        k = sb("k", [128, NC, CH], fp32)
        qp = [sb(f"qp{s}", [128, NC, CH], bf16) for s in range(3)]
        kp = [sb(f"kp{s}", [128, NC, CH], bf16) for s in range(3)]
        v = sb("v", [KT, H, NT, HD], fp32)
        mean_ps, var_ps, q_ps, k_ps, v_ps = (ctx.enter_context(nc.psum_tensor(f"{n}_ps", [128, 512], fp32)) for n in ("mean", "var", "q", "k", "v"))
        (mean, centred, squared, var, dev, recip, scaled, normed, q_mm, k_mm, v_mm, q_out, k_out, v_out,
         q1, q_rest, q2, q3, k1, k_rest, k2, k3, v_st, v_zero) = (nc.alloc_semaphore(f"p1_{n}") for n in (
             "mean", "centred", "squared", "var", "dev", "recip", "scaled", "normed", "q_mm", "k_mm", "v_mm", "q_out", "k_out", "v_out",
             "q1", "q_rest", "q2", "q3", "k1", "k_rest", "k2", "k3", "v_st", "v_zero"))
        x_in, q_st, k_st = ([nc.alloc_semaphore(f"p1_{n}{c}") for c in range(NC)] for n in ("x_in", "q_st", "k_st"))
        block = ctx.enter_context(nc.Block())

        @block.sync
        def _(sp):
            for c in range(NC):
                sp.sem_inc(q_st[c], 48)
                sp.sem_inc(k_st[c], 48)
            sp.sem_inc(v_st, 16)

            with sp.Fori(0, B) as b:
                for c in range(NC):
                    n = b * NC + c
                    sp.wait_ge(q3, done(n))
                    for s in range(3):
                        sp.dma_start(m.d_qp[b, s, :, CH * c:CH * c + CW[c]], qp[s][:, c, 0:CW[c]]).then_inc(q_st[c], 16)
                    sp.wait_ge(k3, done(n))
                    for s in range(3):
                        sp.dma_start(m.d_kp[b, s, :, CH * c:CH * c + CW[c]], kp[s][:, c, 0:CW[c]]).then_inc(k_st[c], 16)
                sp.wait_ge(v_out, done(b * NC + NC - 1))
                sp.dma_start(m.d_v[b].rearrange("h p x -> p h x"), v[:, :, :, :].rearrange("p h t d -> p h (t d)")).then_inc(v_st, 16)
            for c in range(NC):
                sp.wait_ge(q_st[c], 48 * (B + 1))
                sp.wait_ge(k_st[c], 48 * (B + 1))
            sp.wait_ge(v_st, 16 * (B + 1))

        @block.tensor
        def _(pe):
            for s in (mean, var, q_mm, k_mm, v_mm):
                pe.sem_inc(s, NC)

            def norm(b):
                for c in range(NC):
                    n, w = b * NC + c, CW[c]
                    pe.wait_ge(x_in[c], 16 * b + 16)
                    pe.wait_ge(centred, bank_free(n))
                    nc.tensor.matmul(mean_ps[:, 0:w], m.mean_w[:, :], x[:, c, 0:w], start=True, stop=True).then_inc(mean, 1)
                for c in range(NC):
                    n, w = b * NC + c, CW[c]
                    pe.wait_ge(squared, done(n))
                    pe.wait_ge(dev, bank_free(n))
                    nc.tensor.matmul(var_ps[:, 0:w], m.mean_w[:, :], sq[:, c, 0:w], start=True, stop=True).then_inc(var, 1)

            def project(b):
                for c in range(NC):
                    n, w = b * NC + c, CW[c]
                    pe.wait_ge(normed, done(n))
                    pe.wait_ge(q_out, bank_free(n))
                    nc.tensor.matmul(q_ps[:, 0:w], m.weight("e_q"), xn[:, c, 0:w], start=True, stop=True).then_inc(q_mm, 1)
                    pe.wait_ge(k_out, bank_free(n))
                    nc.tensor.matmul(k_ps[:, 0:w], m.weight("e_k"), xn[:, c, 0:w], start=True, stop=True).then_inc(k_mm, 1)
                    pe.wait_ge(v_out, bank_free(n))
                    for t in range(4):
                        rows = min(KT, w - KT * t)
                        last = nc.tensor.matmul(v_ps[0:rows, D * t:D * t + D], xn[:, c, KT * t:KT * t + rows], m.weight("e_v"), start=True, stop=True)
                    last.then_inc(v_mm, 1)

            norm(0)
            with pe.Fori(0, B - 1) as b:
                norm(b + 1)
                project(b)
            project(B - 1)

        @block.gpsimd
        def _(pool):
            for s in (squared, q_rest, q3, k_rest, k3):
                pool.sem_inc(s, NC)

            def load(b):
                for c in range(NC):
                    n, w = b * NC + c, CW[c]
                    pool.wait_ge(centred, slot_free(n))
                    pool.dma_start(x[:, c, 0:w], m.inputs["ctx"][b, :, CH * c:CH * c + w]).then_inc(x_in[c], 16)

            def square(b):
                for c in range(NC):
                    n, w = b * NC + c, CW[c]
                    pool.wait_ge(centred, done(n))
                    pool.wait_ge(var, slot_free(n))
                    nc.gpsimd.tensor_tensor(sq[:, c, 0:w], xc[:, c, 0:w], xc[:, c, 0:w], ALU.mult).then_inc(squared, 1)

            def split(b):
                for c in range(NC):
                    n, w = b * NC + c, CW[c]
                    pool.wait_ge(q1, done(n))
                    nc.gpsimd.tensor_tensor(q[:, c, 0:w], q[:, c, 0:w], qp[0][:, c, 0:w], ALU.subtract).then_inc(q_rest, 1)
                    pool.wait_ge(k1, done(n))
                    nc.gpsimd.tensor_tensor(k[:, c, 0:w], k[:, c, 0:w], kp[0][:, c, 0:w], ALU.subtract).then_inc(k_rest, 1)
                    pool.wait_ge(q2, done(n))
                    nc.gpsimd.tensor_tensor(qp[2][:, c, 0:w], q[:, c, 0:w], qp[1][:, c, 0:w], ALU.subtract).then_inc(q3, 1)
                    pool.wait_ge(k2, done(n))
                    nc.gpsimd.tensor_tensor(kp[2][:, c, 0:w], k[:, c, 0:w], kp[1][:, c, 0:w], ALU.subtract).then_inc(k3, 1)

            load(0)
            square(0)
            load(1)
            with pool.Fori(0, B - 2) as b:
                square(b + 1)
                load(b + 2)
                split(b)
            square(B - 1)
            split(B - 2)
            split(B - 1)

        @block.scalar
        def _(act):
            for s in (dev, normed, q1, q2, k1, k2):
                act.sem_inc(s, NC)

            def deviate(b):
                for c in range(NC):
                    n, w = b * NC + c, CW[c]
                    act.wait_ge(var, done(n))
                    act.wait_ge(scaled, slot_free(n))
                    nc.scalar.activation(sd[:, c, 0:w], var_ps[:, 0:w], ACT.Sqrt, bias=m.eps[:, 0:1]).then_inc(dev, 1)

            def norm(b):
                for c in range(NC):
                    n, w = b * NC + c, CW[c]
                    act.wait_ge(scaled, done(n))
                    act.wait_ge(v_mm, slot_free(n))
                    nc.scalar.activation(xn[:, c, 0:w], xc[:, c, 0:w], ACT.Identity, scale=m.column("e_n1s"), bias=m.column("e_n1b")).then_inc(normed, 1)

            def split(b):
                for c in range(NC):
                    n, w = b * NC + c, CW[c]
                    act.wait_ge(q_out, done(n))
                    act.wait_ge(q_st[c], 48 * b + 48)
                    nc.scalar.activation(qp[0][:, c, 0:w], q[:, c, 0:w], ACT.Copy).then_inc(q1, 1)
                    act.wait_ge(k_out, done(n))
                    act.wait_ge(k_st[c], 48 * b + 48)
                    nc.scalar.activation(kp[0][:, c, 0:w], k[:, c, 0:w], ACT.Copy).then_inc(k1, 1)
                    act.wait_ge(q_rest, done(n))
                    nc.scalar.activation(qp[1][:, c, 0:w], q[:, c, 0:w], ACT.Copy).then_inc(q2, 1)
                    act.wait_ge(k_rest, done(n))
                    nc.scalar.activation(kp[1][:, c, 0:w], k[:, c, 0:w], ACT.Copy).then_inc(k2, 1)

            deviate(0)
            norm(0)
            with act.Fori(0, B - 1) as b:
                deviate(b + 1)
                split(b)
                norm(b + 1)
            split(B - 1)

        @block.vector
        def _(dve):
            for s in (centred, recip, scaled, q_out, k_out, v_out):
                dve.sem_inc(s, NC)
            nc.vector.memset(v[:, :, :, :], 0.0).then_inc(v_zero, 1)
            dve.wait_ge(v_zero, 1)

            def norm(b):
                for c in range(NC):
                    n, w = b * NC + c, CW[c]
                    dve.wait_ge(mean, done(n))
                    dve.wait_ge(normed, slot_free(n))
                    nc.vector.tensor_tensor(xc[:, c, 0:w], x[:, c, 0:w], mean_ps[:, 0:w], ALU.subtract).then_inc(centred, 1)
                for c in range(NC):
                    n, w = b * NC + c, CW[c]
                    dve.wait_ge(dev, done(n))
                    nc.vector.reciprocal(sd[:, c, 0:w], sd[:, c, 0:w]).then_inc(recip, 1)
                    dve.wait_ge(recip, done(n))
                    nc.vector.tensor_tensor(xc[:, c, 0:w], xc[:, c, 0:w], sd[:, c, 0:w], ALU.mult).then_inc(scaled, 1)

            def project(b):
                for c in range(NC):
                    n, w = b * NC + c, CW[c]
                    dve.wait_ge(q_mm, done(n))
                    dve.wait_ge(q3, slot_free(n))
                    nc.vector.tensor_scalar(q[:, c, 0:w], q_ps[:, 0:w], m.column("e_bq"), SCALE, ALU.add, ALU.mult).then_inc(q_out, 1)
                    dve.wait_ge(k_mm, done(n))
                    dve.wait_ge(k3, slot_free(n))
                    nc.vector.tensor_scalar(k[:, c, 0:w], k_ps[:, 0:w], m.column("e_bk"), None, ALU.add).then_inc(k_out, 1)
                    dve.wait_ge(v_mm, done(n))
                    if c == 0:
                        dve.wait_ge(v_st, 16 * b + 16)
                    full = w // KT
                    bv = m.row("e_bv")
                    parts = [(KT, 0, full)] + ([(w - full * KT, full, 1)] if w % KT else [])
                    for rows, t, many in parts:
                        last = nc.vector.tensor_tensor(
                            v[0:rows, :, 4 * c + t:4 * c + t + many, :].rearrange("p h t d -> p t h d"),
                            v_ps[0:rows, D * t:D * (t + many)].rearrange("p (t h d) -> p t h d", t=many, h=H),
                            bv[0:rows, :].rearrange("p (o h d) -> p o h d", o=1, h=H).to_broadcast([rows, many, H, HD]), ALU.add)
                    last.then_inc(v_out, 1)

            norm(0)
            with dve.Fori(0, B - 1) as b:
                norm(b + 1)
                project(b)
            project(B - 1)


NU = H * B
SLOTS = 4
NA = NT * NC
A_BANKS = 3
A_EACH = NA // NT
A_AHEAD = 6
LOADS = 9
O_DMAS = NQ + 1


def wait_alone(eng, signal, value, passed):
    eng.wait_ge(signal, value)
    eng.sem_inc(passed, 1)


def rows_of(t):
    return KT if t < NT - 1 else LAST


def attention_phase(nc, m):
    fp32, bf16 = DTS["fp32"], DTS["bf16"]
    ALU, ACT, AX = mybir.AluOpType, mybir.ActivationFunctionType, mybir.AxisListType
    ctx = ExitStack()
    with ctx:
        sb = lambda name, shape, dt: ctx.enter_context(nc.sbuf_tensor(name, shape, dt))
        sem = lambda name: nc.alloc_semaphore(name)
        queries = [sb(f"queries{j}", [ROWS, KT * NT], bf16) for j in range(SLOTS)]
        keys = [sb(f"keys{j}", [ROWS, T], bf16) for j in range(SLOTS)]
        band = [sb(f"band{j}", [3 * SUB, 4, BW], bf16) for j in range(SLOTS)]
        v_in = [sb(f"v_in{j}", [KT, NT * HD], fp32) for j in range(SLOTS)]
        values = [sb(f"values{j}", [KT, NT, 32], fp32) for j in range(SLOTS)]
        ident3 = sb("ident3", [3 * SUB, SUB], bf16)
        probs = sb("probs", [KT, 2, T], fp32)
        strip = [sb(f"strip{i}", [KT, SW], fp32) for i in range(2)]
        tops = [sb(f"tops{i}", [KT, NT, NC], fp32) for i in range(2)]
        shift = sb("shift", [KT, NT], fp32)
        shift_rest = sb("shift_rest", [KT, NT], fp32)
        pieces = sb("pieces", [128, 3, 32], bf16)
        turned = [sb(f"turned{i}", [128, 3, 32], bf16) for i in range(2)]
        result = [sb(f"result{i}", [128, QC], fp32) for i in range(2)]
        a_ps = ctx.enter_context(nc.psum_tensor("a_ps", [128, A_BANKS, 512], fp32))
        b_ps = ctx.enter_context(nc.psum_tensor("b_ps", [128, NQ, 512], fp32))
        o_ps = ctx.enter_context(nc.psum_tensor("o_ps", [128, 512], fp32))
        constants_in, zeroed, dve_zeroed = sem("a_constants_in"), sem("a_zeroed"), sem("a_dve_zeroed")
        loaded = [sem(f"a_loaded{j}") for j in range(SLOTS)]
        strip_in = [sem(f"a_strip_in{i}") for i in range(2)]
        strip_used = sem("a_strip_used")
        padded = sem("a_padded")
        scored = sem("a_scored")
        maxed = sem("a_maxed")
        dve_step = sem("a_dve_step")
        turned_ready = sem("a_turned")
        shift_out = [sem(f"a_shift_out{j}") for j in range(SLOTS)]
        shift_in = [sem(f"a_shift_in{j}") for j in range(SLOTS)]
        exps_in = sem("a_exps_in")
        exp_out = sem("a_exp_out")
        multiplied = sem("a_multiplied")
        unit_done = sem("a_unit_done")
        copied = sem("a_copied")
        passed = {e: sem(f"a_passed_{e}") for e in ("pool", "sp", "dve")}
        stored = [sem(f"a_stored{i}") for i in range(2)]
        block = ctx.enter_context(nc.Block())

        @block.gpsimd
        def _(pool):
            for j in range(SLOTS):
                nc.gpsimd.memset(values[j][:, :, :], 0.0).then_inc(zeroed, 1)
            pool.wait_ge(zeroed, SLOTS)
            for j in range(SLOTS):
                nc.gpsimd.memset(values[j][:, :, HD:HD + 1], 1.0).then_inc(zeroed, 1)
            pool.wait_ge(zeroed, 2 * SLOTS)

            def load_strip(i, h):
                pool.dma_start(strip[i][:, :], bass.AP(m.inputs["line"].tensor, h * (KT * GLEN) + KT - 1, [[GLEN - 1, KT], [1, SW]])).then_inc(strip_in[i], 16)

            def load_head(h, i, another=True):
                with pool.Fori(0, B // SLOTS) as part:
                    for j in range(SLOTS):
                        u = h * B + part * SLOTS + j
                        b = part * SLOTS + j
                        pool.wait_ge(unit_done, u + 1)
                        first = h * HD
                        for s in range(3):
                            src = m.d_qp[b, s:s + 1, bass.ds(first, HD), :].to_broadcast([3, HD, T])
                            pool.dma_start(queries[j][24 * s:24 * s + 24, 0:T], src).then_inc(loaded[j], 16)
                            pool.dma_start(keys[j][24 * s:24 * s + 24, :], m.d_kp[b, :, bass.ds(first, HD), :]).then_inc(loaded[j], 16)
                        pool.dma_start(keys[j][NPROD:NPROD + NSTEP, :], m.d_step[bass.ds(h, 1), :, :].rearrange("o r t -> (o r) t")).then_inc(loaded[j], 16)
                        pool.dma_start(band[j][:, :, :], m.d_band[bass.ds(h, 1), :, :, :].rearrange("o r i w -> (o r) i w")).then_inc(loaded[j], 16)
                        pool.dma_start(v_in[j][:, :], m.d_v[b, bass.ds(h, 1), :, :].rearrange("o p x -> (o p) x")).then_inc(loaded[j], 16)
                        wait_alone(pool, loaded[j], (u - j) * (LOADS * 16 // SLOTS) + LOADS * 16, passed["pool"])
                        nc.gpsimd.tensor_copy(values[j][:, :, 0:HD], v_in[j][:, :].rearrange("p (t d) -> p t d", t=NT)).then_inc(padded, 1)
                if another:
                    wait_alone(pool, strip_used, h + 1, passed["pool"])
                    load_strip(1 - i, h + 1)

            load_strip(0, 0)
            with pool.Fori(0, H // 2 - 1) as pair:
                load_head(pair * 2, 0)
                load_head(pair * 2 + 1, 1)
            load_head(H - 2, 0)
            load_head(H - 1, 1, another=False)

        @block.sync
        def _(sp):
            for j in range(SLOTS):
                sp.dma_start(queries[j][NPROD:NPROD + NSTEP, 0:T], m.inputs["q_steps"]).then_inc(constants_in, 16)
                sp.dma_start(keys[j][NPROD + NSTEP:ROWS, :], m.inputs["ones3"]).then_inc(constants_in, 16)
            sp.dma_start(ident3[:, :], m.inputs["ident3"]).then_inc(constants_in, 16)
            for j in range(SLOTS):
                sp.sem_inc(shift_out[j], 64)

            def store(u, j):
                i = j % 2
                wait_alone(sp, copied, u + 2, passed["sp"])
                for q in range(NQ):
                    sp.dma_start(m.d_att[u, :, QC * q:QC * q + QC], result[i][32 * q:32 * q + HD, :]).then_inc(stored[i], 16)
                sp.dma_start(m.d_den[u, :].rearrange("(q x) -> q x", q=NQ), result[i][HD:128:32, :]).then_inc(stored[i], 16)

            def place_shift(u, j):
                sp.wait_ge(turned_ready, u + 1)
                row = m.d_shift[j]
                for a in range(4):
                    w = min(32, KT - 32 * a)
                    sp.dma_start(row.rearrange("s (t x) -> t s x", x=KT)[:, :, 32 * a:32 * a + w],
                                 turned[j % 2][32 * a:32 * a + NT, :, 0:w]).then_inc(shift_out[j], 16)
                sp.wait_ge(shift_out[j], (u - j) * (64 // SLOTS) + 128)
                sp.dma_start(queries[j][NPROD + NSTEP:ROWS, :], row).then_inc(shift_in[j], 16)

            for u in (0, 1):
                place_shift(u, u)
            with sp.Fori(0, (NU - 4) // SLOTS) as it:
                for k in range(SLOTS):
                    store(it * SLOTS + k, k)
                    place_shift(it * SLOTS + 2 + k, (2 + k) % SLOTS)
            for u in (NU - 2, NU - 1):
                store(u - 2, (u - 2) % SLOTS)
                place_shift(u, u % SLOTS)
            for u in (NU - 2, NU - 1):
                store(u, u % SLOTS)
            for i in range(2):
                sp.wait_ge(stored[i], 16 * O_DMAS * (NU // 2 + 1))

        @block.vector
        def _(dve):
            dve.sem_inc(maxed, A_BANKS)
            dve.sem_inc(strip_used, 1)
            nc.vector.memset(pieces[:, :, :], 0.0).then_inc(dve_zeroed, 1)
            for i in range(2):
                nc.vector.memset(tops[i][:, :, :], 0.0).then_inc(dve_zeroed, 1)
            dve.wait_ge(dve_zeroed, 3)
            with dve.Fori(0, H // 2) as pair:
                for i in range(2):
                    wait_alone(dve, strip_in[i], pair * 16 + 16, passed["dve"])
                    h = pair * 2 + i
                    with dve.Fori(0, B // SLOTS) as part:
                        for j in range(SLOTS):
                            u = pair * (2 * B) + i * B + part * SLOTS + j
                            for n in range(NA):
                                t, c = n // NC, n % NC
                                rows, w = rows_of(t), CW[c]
                                x0 = CH * c - KT * t + STRIP0
                                wait_alone(dve, scored, u * NA + n + 1, passed["dve"])
                                block_ps = a_ps[0:rows, n % A_BANKS, 0:w]
                                nc.vector.tensor_tensor_reduce(
                                    out=block_ps, in0=block_ps, in1=strip[i][0:rows, x0:x0 + w], scale=1.0, scalar=-3e38,
                                    op0=ALU.add, op1=ALU.max, accum_out=tops[j % 2][0:rows, t, c:c + 1]).then_inc(maxed, 1)
                            s = u * 6
                            dve.wait_ge(maxed, u * NA + NA + A_BANKS)
                            nc.vector.tensor_reduce(shift[:, :], tops[j % 2][:, :, :], AX.X, ALU.max, negate=True).then_inc(dve_step, 1)
                            dve.wait_ge(dve_step, s + 1)
                            nc.vector.tensor_scalar(shift[:, :], shift[:, :], m.left[0:KT, bass.ds(h, 1)], None, ALU.add).then_inc(dve_step, 1)
                            dve.wait_ge(dve_step, s + 2)
                            nc.vector.tensor_copy(pieces[0:KT, 0, 0:NT], shift[:, :]).then_inc(dve_step, 1)
                            dve.wait_ge(dve_step, s + 3)
                            nc.vector.tensor_tensor(shift_rest[:, :], shift[:, :], pieces[0:KT, 0, 0:NT], ALU.subtract).then_inc(dve_step, 1)
                            dve.wait_ge(dve_step, s + 4)
                            nc.vector.tensor_copy(pieces[0:KT, 1, 0:NT], shift_rest[:, :]).then_inc(dve_step, 1)
                            dve.wait_ge(dve_step, s + 5)
                            nc.vector.tensor_tensor(pieces[0:KT, 2, 0:NT], shift_rest[:, :], pieces[0:KT, 1, 0:NT], ALU.subtract).then_inc(dve_step, 1)
                            dve.wait_ge(dve_step, s + 6)
                            dve.wait_ge(shift_out[(j + 2) % SLOTS], (u - j) * (64 // SLOTS) + 64 * (1 if j < 2 else 2))
                            nc.vector.transpose(turned[j % 2][:, :, :].rearrange("p s x -> p (s x)"), pieces[:, :, :].rearrange("p s x -> p (s x)")).then_inc(turned_ready, 1)
                    dve.sem_inc(strip_used, 1)

        @block.tensor
        def _(pe):
            pe.sem_inc(multiplied, 2)
            pe.sem_inc(unit_done, SLOTS)
            pe.wait_ge(constants_in, 16 * (2 * SLOTS + 1))

            def first_pass(u, j, ns):
                for n in ns:
                    t, c = n // NC, n % NC
                    rows, w = rows_of(t), CW[c]
                    pe.wait_ge(maxed, u * NA + n + 1)
                    nc.tensor.matmul(a_ps[0:rows, n % A_BANKS, 0:w], queries[j][0:NPROD, KT * t:KT * t + rows],
                                     keys[j][0:NPROD, CH * c:CH * c + w], start=True, stop=True).then_inc(scored, 1)

            def exponents(u, j, t, half):
                rows = rows_of(t)
                pe.wait_ge(exp_out, u * (2 * NT) + 2 * t + half + 1)
                todo = []
                for q in (2 * half, 2 * half + 1):
                    todo.append((q, 0, rows, 0, QC, None))
                for i in range(4):
                    lo = KT * t + SUB * i - HALO
                    for q in (2 * half, 2 * half + 1):
                        a, z = max(lo, QC * q, 0), min(lo + BW, QC * q + QC)
                        if a < z:
                            todo.append((q, SUB * i, min(SUB, rows - SUB * i), a - QC * q, z - QC * q, (i, a - lo)))
                for n, (q, p, k, a, z, near) in enumerate(todo):
                    out = b_ps[p:p + k, q, a:z]
                    ends = not any(x[0] == q for x in todo[n + 1:])
                    if near is None:
                        last = nc.tensor.matmul(out, keys[j][0:ROWS, KT * t:KT * t + rows], queries[j][0:ROWS, QC * q:QC * q + QC],
                                                start=True, stop=ends, skip_group_check=True)
                    else:
                        i, w0 = near
                        last = nc.tensor.matmul(out, ident3[:, 0:k], band[j][:, i, w0:w0 + z - a], start=False, stop=ends, skip_group_check=True)
                last.then_inc(exps_in, 1)

            def multiply(u, j, t):
                rows = rows_of(t)
                pe.wait_ge(exp_out, u * (2 * NT) + 2 * t + 4)
                if t == 0:
                    pe.wait_ge(padded, u + 1)
                    pe.wait_ge(copied, u + 1)
                for q in range(NQ):
                    last = nc.tensor.matmul(o_ps[32 * q:32 * q + 32, 0:QC], values[j][0:rows, t, :], probs[0:rows, t % 2, QC * q:QC * q + QC],
                                            start=(t == 0), stop=(t == NT - 1))
                last.then_inc(multiplied, 1)

            def blocks(v, jv, t):
                first = A_EACH * (t + A_AHEAD)
                later = first >= NA
                return (v + later, (jv + later) % SLOTS, range(first % NA, first % NA + A_EACH))

            def unit(v, jv, with_b=True, with_last=True, with_next=True, with_a=True):
                u, j = v - 1, (jv - 1) % SLOTS
                if with_b:
                    pe.wait_ge(shift_in[j], (u - j) * (16 // SLOTS) + 16)
                for t in range(NT):
                    va, ja, ns = blocks(v, jv, t)
                    if not (with_next if ns[0] < A_EACH * A_AHEAD else with_a):
                        ns = ()
                    elif ns[0] == 0:
                        pe.wait_ge(loaded[ja], (va - ja) * (LOADS * 16 // SLOTS) + LOADS * 16)
                    first_pass(va, ja, ns[0:1])
                    if with_b:
                        exponents(u, j, t, 0)
                    first_pass(va, ja, ns[1:2])
                    if with_b:
                        exponents(u, j, t, 1)
                    first_pass(va, ja, ns[2:3])
                    if with_b:
                        if t > 0:
                            multiply(u, j, t - 1)
                        elif with_last:
                            finish(u - 1, (j - 1) % SLOTS)

            def finish(u, j):
                multiply(u, j, NT - 1)
                pe.wait_ge(multiplied, u * NT + NT + 2)
                pe.sem_inc(unit_done, 1)

            pe.wait_ge(loaded[0], LOADS * 16)
            first_pass(0, 0, range(A_EACH * A_AHEAD))
            unit(0, 0, with_b=False)
            unit(1, 1, with_last=False)
            with pe.Fori(0, (NU - 4) // SLOTS) as it:
                for k in range(SLOTS):
                    unit(it * SLOTS + 2 + k, (2 + k) % SLOTS)
            unit(NU - 2, (NU - 2) % SLOTS)
            unit(NU - 1, (NU - 1) % SLOTS, with_next=False)
            unit(NU, NU % SLOTS, with_next=False, with_a=False)
            finish(NU - 1, (NU - 1) % SLOTS)

        @block.scalar
        def _(act):
            act.sem_inc(exp_out, 2)
            act.sem_inc(copied, 1)
            for i in range(2):
                act.sem_inc(stored[i], 16 * O_DMAS)

            def exponentiate(u, ts):
                for t in ts:
                    rows = rows_of(t)
                    for half in range(2):
                        act.wait_ge(exps_in, u * (2 * NT) + 2 * t + half + 1)
                        if half == 0:
                            act.wait_ge(multiplied, u * NT + t + 1)
                        nc.scalar.activation(
                            probs[0:rows, t % 2, 2 * QC * half:2 * QC * (half + 1)].rearrange("p (q x) -> p q x", q=2),
                            b_ps[0:rows, 2 * half:2 * half + 2, 0:QC], ACT.Exp).then_inc(exp_out, 1)

            def copy_result(u, i):
                act.wait_ge(multiplied, u * NT + NT + 2)
                act.wait_ge(stored[i], (u - i) * (16 * O_DMAS // 2) + 16 * O_DMAS)
                nc.scalar.activation(result[i][:, :], o_ps[:, 0:QC], ACT.Copy).then_inc(copied, 1)

            def unit(u, i):
                exponentiate(u, range(1))
                copy_result(u - 1, 1 - i)
                exponentiate(u, range(1, NT))

            exponentiate(0, range(NT))
            with act.Fori(0, (NU - 2) // 2) as pair:
                unit(pair * 2 + 1, 1)
                unit(pair * 2 + 2, 0)
            unit(NU - 1, 1)
            copy_result(NU - 1, 1)


def context_phase(nc, m):
    fp32, bf16 = DTS["fp32"], DTS["bf16"]
    ALU, ACT = mybir.AluOpType, mybir.ActivationFunctionType
    ctx = ExitStack()
    with ctx:
        sb = lambda name, shape, dt: ctx.enter_context(nc.sbuf_tensor(name, shape, dt))
        sem = lambda name: nc.alloc_semaphore(name)
        den = sb("den", [B * H, T], fp32)
        x, att, inv, x1, xc, sq, sd, xn, kc, kl = (sb(f"c_{n}", [128, NC, CH], fp32) for n in ("x", "att", "inv", "x1", "xc", "sq", "sd", "xn", "kc", "kl"))
        hid = sb("hid", [128, NC, 4, CH], fp32)
        vc, vl = (sb(f"c_{n}", [KT, NC, 4, D], fp32) for n in ("vc", "vl"))
        o_ps, mean_ps, var_ps, f2_ps, k_ps, v_ps = (ctx.enter_context(nc.psum_tensor(f"c_{n}_ps", [128, 512], fp32)) for n in ("o", "mean", "var", "f2", "k", "v"))
        f1_ps = ctx.enter_context(nc.psum_tensor("c_f1_ps", [128, 2, 512], fp32))
        (den_in, den_done, den_out, attn, proj, x1_out, mean, centred, squared, var, dev, recip, scaled, normed, f1_mm, relu, f2_mm, mem,
         kl_mm, kl_out, kc_mm, kc_out, vl_mm, vl_out, vc_mm, vc_out, v_zero) = (sem(f"c_{n}") for n in (
             "den_in", "den_done", "den_out", "attn", "proj", "x1_out", "mean", "centred", "squared", "var", "dev", "recip", "scaled", "normed", "f1_mm", "relu", "f2_mm", "mem",
             "kl_mm", "kl_out", "kc_mm", "kc_out", "vl_mm", "vl_out", "vc_mm", "vc_out", "v_zero"))
        passed = sem("c_passed")
        loaded, x_loaded, kl_st, kc_st, vl_st, vc_st = ([sem(f"c_{n}{c}") for c in range(NC)] for n in ("loaded", "x_loaded", "kl_st", "kc_st", "vl_st", "vc_st"))
        block = ctx.enter_context(nc.Block())

        @block.sync
        def _(sp):
            sp.dma_start(den[:, :], m.d_den).then_inc(den_in, 16)
            sp.wait_ge(den_done, 1)
            sp.dma_start(m.d_inv, den[:, :]).then_inc(den_out, 16)
            for s in (kl_st, kc_st, vl_st, vc_st):
                for c in range(NC):
                    sp.sem_inc(s[c], 16)
            with sp.Fori(0, B) as b:
                for store, ready, src, dst in ((kl_st, kl_out, kl, m.d_kl), (kc_st, kc_out, kc, m.d_kc)):
                    for c in range(NC):
                        n, w = b * NC + c, CW[c]
                        sp.wait_ge(ready, done(n))
                        sp.dma_start(dst[b, :, CH * c:CH * c + w], src[:, c, 0:w]).then_inc(store[c], 16)
                for store, ready, src, dst in ((vl_st, vl_out, vl, m.d_vl), (vc_st, vc_out, vc, m.d_vc)):
                    for c in range(NC):
                        n = b * NC + c
                        sp.wait_ge(ready, done(n))
                        sp.dma_start(dst[b, :, 4 * c:4 * c + 4, :], src[:, c, :, :]).then_inc(store[c], 16)
            for s in (kl_st, kc_st, vl_st, vc_st):
                for c in range(NC):
                    sp.wait_ge(s[c], 16 * (B + 1))

        @block.gpsimd
        def _(pool):
            for s in (attn, squared):
                pool.sem_inc(s, NC)
            pool.wait_ge(den_out, 16)
            with pool.Fori(0, B) as b:
                for c in range(NC):
                    n, w = b * NC + c, CW[c]
                    pool.wait_ge(x1_out, slot_free(n))
                    wait_alone(pool, vl_mm, slot_free(n), passed)
                    pool.dma_start(x[:, c, 0:w], m.inputs["ctx"][b, :, CH * c:CH * c + w]).then_inc(x_loaded[c], 16)
                    wait_alone(pool, proj, slot_free(n), passed)
                    pool.dma_start(att[:, c, 0:w], m.d_att.rearrange("(h b) d t -> b h d t", b=B)[b, :, :, CH * c:CH * c + w]).then_inc(loaded[c], 16)
                    pool.dma_start(inv[:, c, 0:w], m.d_inv.rearrange("(h b) t -> b h t", b=B)[b, :, CH * c:CH * c + w].unsqueeze(1).to_broadcast([H, HD, w])).then_inc(loaded[c], 16)
                for c in range(NC):
                    n, w = b * NC + c, CW[c]
                    pool.wait_ge(loaded[c], b * 32 + 32)
                    nc.gpsimd.tensor_tensor(att[:, c, 0:w], att[:, c, 0:w], inv[:, c, 0:w], ALU.mult).then_inc(attn, 1)
                for c in range(NC):
                    n, w = b * NC + c, CW[c]
                    pool.wait_ge(centred, done(n))
                    pool.wait_ge(var, slot_free(n))
                    nc.gpsimd.tensor_tensor(sq[:, c, 0:w], xc[:, c, 0:w], xc[:, c, 0:w], ALU.mult).then_inc(squared, 1)

        @block.tensor
        def _(pe):
            for s in (proj, mean, var, f2_mm, kl_mm, kc_mm, vl_mm, vc_mm):
                pe.sem_inc(s, NC)

            def keys_values(b, chunks, src, k_name, v_name, ready, k_mm, v_mm, k_free, v_free):
                for c in chunks:
                    n, w = b * NC + c, CW[c]
                    ready(c, n)
                    if c:
                        pe.wait_ge(k_free, bank_free(n))
                    nc.tensor.matmul(k_ps[:, 0:w], m.weight(k_name), src[:, c, 0:w], start=True, stop=True).then_inc(k_mm, 1)
                    if c:
                        pe.wait_ge(v_free, bank_free(n))
                    for t in range(4):
                        rows = min(KT, w - KT * t)
                        last = nc.tensor.matmul(v_ps[0:rows, D * t:D * t + D], src[:, c, KT * t:KT * t + rows], m.weight(v_name), start=True, stop=True)
                    last.then_inc(v_mm, 1)

            with pe.Fori(0, B) as b:
                def last_keys_values(chunks):
                    keys_values(b, chunks, x, "t_k", "t_v", lambda c, n: pe.wait_ge(x_loaded[c], b * 16 + 16), kl_mm, vl_mm, kl_out, vl_out)

                for c in range(NC):
                    n, w = b * NC + c, CW[c]
                    pe.wait_ge(attn, done(n))
                    pe.wait_ge(x1_out, bank_free(n))
                    nc.tensor.matmul(o_ps[:, 0:w], m.weight("e_o"), att[:, c, 0:w], start=True, stop=True).then_inc(proj, 1)
                for c in range(NC):
                    n, w = b * NC + c, CW[c]
                    pe.wait_ge(x1_out, done(n))
                    pe.wait_ge(centred, bank_free(n))
                    nc.tensor.matmul(mean_ps[:, 0:w], m.mean_w[:, :], x1[:, c, 0:w], start=True, stop=True).then_inc(mean, 1)
                pe.wait_ge(kc_out, slot_free(b * NC + NC - 1))
                pe.wait_ge(vc_out, slot_free(b * NC + NC - 1))
                last_keys_values([0])
                for c in range(NC):
                    n, w = b * NC + c, CW[c]
                    pe.wait_ge(squared, done(n))
                    pe.wait_ge(dev, bank_free(n))
                    nc.tensor.matmul(var_ps[:, 0:w], m.mean_w[:, :], sq[:, c, 0:w], start=True, stop=True).then_inc(var, 1)
                last_keys_values([1, 2])
                for c in range(NC):
                    n, w = b * NC + c, CW[c]
                    pe.wait_ge(normed, done(n))
                    for j in range(4):
                        pe.wait_ge(relu, n * 4 + j + 1)
                        nc.tensor.matmul(f1_ps[:, j % 2, 0:w], m.weight("e_f1", j), xn[:, c, 0:w], start=True, stop=True).then_inc(f1_mm, 1)
                    pe.wait_ge(mem, bank_free(n))
                    for j in range(4):
                        pe.wait_ge(relu, n * 4 + j + 3)
                        last = nc.tensor.matmul(f2_ps[:, 0:w], m.weight("e_f2", j), hid[:, c, j, 0:w], start=(j == 0), stop=(j == 3))
                    last.then_inc(f2_mm, 1)
                pe.wait_ge(kl_out, done(b * NC + NC - 1))
                pe.wait_ge(vl_out, done(b * NC + NC - 1))
                keys_values(b, range(NC), x1, "c_k", "c_v", lambda c, n: pe.wait_ge(mem, done(n)), kc_mm, vc_mm, kc_out, vc_out)

        @block.scalar
        def _(act):
            for s in (dev, normed, kl_out, kc_out, vl_out, vc_out):
                act.sem_inc(s, NC)
            act.sem_inc(relu, 2)

            def keys_values(b, chunks, k, v, k_name, k_mm, v_mm, k_out, v_out, k_st, v_st):
                for c in chunks:
                    n, w = b * NC + c, CW[c]
                    act.wait_ge(k_mm, done(n))
                    act.wait_ge(k_st[c], b * 16 + 16)
                    nc.scalar.activation(k[:, c, 0:w], k_ps[:, 0:w], ACT.Identity, bias=m.column(k_name)).then_inc(k_out, 1)
                    act.wait_ge(v_mm, done(n))
                    act.wait_ge(v_st[c], b * 16 + 16)
                    full = w // KT
                    last = nc.scalar.activation(v[:, c, 0:full, :], v_ps[0:KT, 0:D * full].rearrange("p (t d) -> p t d", t=full), ACT.Copy)
                    if w % KT:
                        rows = w - KT * full
                        last = nc.scalar.activation(v[0:rows, c, full, :], v_ps[0:rows, D * full:D * full + D], ACT.Copy)
                    last.then_inc(v_out, 1)

            act.wait_ge(v_zero, 2)
            with act.Fori(0, B) as b:
                keys_values(b, [0], kl, vl, "t_bk", kl_mm, vl_mm, kl_out, vl_out, kl_st, vl_st)
                for c in range(NC):
                    n, w = b * NC + c, CW[c]
                    act.wait_ge(var, done(n))
                    act.wait_ge(scaled, slot_free(n))
                    nc.scalar.activation(sd[:, c, 0:w], var_ps[:, 0:w], ACT.Sqrt, bias=m.eps[:, 0:1]).then_inc(dev, 1)
                keys_values(b, [1, 2], kl, vl, "t_bk", kl_mm, vl_mm, kl_out, vl_out, kl_st, vl_st)
                for c in range(NC):
                    n, w = b * NC + c, CW[c]
                    act.wait_ge(scaled, done(n))
                    act.wait_ge(f2_mm, slot_free(n))
                    nc.scalar.activation(xn[:, c, 0:w], xc[:, c, 0:w], ACT.Identity, scale=m.column("e_n2s"), bias=m.column("e_n2b")).then_inc(normed, 1)
                for c in range(NC):
                    n, w = b * NC + c, CW[c]
                    act.wait_ge(f2_mm, slot_free(n))
                    for j in range(4):
                        act.wait_ge(f1_mm, n * 4 + j + 1)
                        nc.scalar.activation(hid[:, c, j, 0:w], f1_ps[:, j % 2, 0:w], ACT.Relu, bias=m.column("e_b1", j)).then_inc(relu, 1)
                keys_values(b, range(NC), kc, vc, "c_bk", kc_mm, vc_mm, kc_out, vc_out, kc_st, vc_st)

        @block.vector
        def _(dve):
            for s in (x1_out, centred, recip, scaled, mem):
                dve.sem_inc(s, NC)
            nc.vector.memset(vc[:, NC - 1, 3, :], 0.0).then_inc(v_zero, 1)
            nc.vector.memset(vl[:, NC - 1, 3, :], 0.0).then_inc(v_zero, 1)
            dve.wait_ge(den_in, 16)
            nc.vector.reciprocal(den[:, :], den[:, :]).then_inc(den_done, 1)
            with dve.Fori(0, B) as b:
                for c in range(NC):
                    n, w = b * NC + c, CW[c]
                    dve.wait_ge(proj, done(n))
                    dve.wait_ge(x_loaded[c], b * 16 + 16)
                    dve.wait_ge(vc_mm, slot_free(n))
                    nc.vector.scalar_tensor_tensor(out=x1[:, c, 0:w], in0=o_ps[:, 0:w], scalar=m.column("e_bo"), in1=x[:, c, 0:w], op0=ALU.add, op1=ALU.add).then_inc(x1_out, 1)
                for c in range(NC):
                    n, w = b * NC + c, CW[c]
                    dve.wait_ge(mean, done(n))
                    dve.wait_ge(normed, slot_free(n))
                    nc.vector.tensor_tensor(xc[:, c, 0:w], x1[:, c, 0:w], mean_ps[:, 0:w], ALU.subtract).then_inc(centred, 1)
                for c in range(NC):
                    n, w = b * NC + c, CW[c]
                    dve.wait_ge(dev, done(n))
                    nc.vector.reciprocal(sd[:, c, 0:w], sd[:, c, 0:w]).then_inc(recip, 1)
                    dve.wait_ge(recip, done(n))
                    nc.vector.tensor_tensor(xc[:, c, 0:w], xc[:, c, 0:w], sd[:, c, 0:w], ALU.mult).then_inc(scaled, 1)
                for c in range(NC):
                    n, w = b * NC + c, CW[c]
                    dve.wait_ge(f2_mm, done(n))
                    nc.vector.scalar_tensor_tensor(out=x1[:, c, 0:w], in0=f2_ps[:, 0:w], scalar=m.column("e_b2"), in1=x1[:, c, 0:w], op0=ALU.add, op1=ALU.add).then_inc(mem, 1)


NB = 2
HW = B * Q // NB
LEAD = 2


class Norm:

    def __init__(self, nc, ctx, m, tag, scale, shift):
        sem = lambda n: nc.alloc_semaphore(f"{tag}_{n}")
        self.nc, self.m, self.scale, self.shift = nc, m, scale, shift
        self.mean, self.centred, self.squared, self.var, self.dev, self.recip, self.scaled, self.normed = (
            sem(n) for n in ("mean", "centred", "squared", "var", "dev", "recip", "scaled", "normed"))
        sb = lambda n: ctx.enter_context(nc.sbuf_tensor(f"{tag}_{n}", [128, NB, HW], mybir.dt.float32))
        self.xc, self.sq, self.sd, self.out = sb("xc"), sb("sq"), sb("sd"), sb("out")

    def tensor(self, pe, src, src_ready, mean_ps, var_ps):
        for i in range(NB):
            if src_ready is not None:
                pe.wait_ge(src_ready, i + 1)
            self.nc.tensor.matmul(mean_ps[i][:, 0:HW], self.m.mean_w[:, :], src[:, i, :], start=True, stop=True).then_inc(self.mean, 1)
        for i in range(NB):
            pe.wait_ge(self.squared, i + 1)
            self.nc.tensor.matmul(var_ps[i][:, 0:HW], self.m.mean_w[:, :], self.sq[:, i, :], start=True, stop=True).then_inc(self.var, 1)

    def vector(self, dve, src, mean_ps):
        ALU = mybir.AluOpType
        for i in range(NB):
            dve.wait_ge(self.mean, i + 1)
            self.nc.vector.tensor_tensor(self.xc[:, i, :], src[:, i, :], mean_ps[i][:, 0:HW], ALU.subtract).then_inc(self.centred, 1)
        for i in range(NB):
            dve.wait_ge(self.dev, i + 1)
            self.nc.vector.reciprocal(self.sd[:, i, :], self.sd[:, i, :]).then_inc(self.recip, 1)
            dve.wait_ge(self.recip, i + 1)
            self.nc.vector.tensor_tensor(self.xc[:, i, :], self.xc[:, i, :], self.sd[:, i, :], ALU.mult).then_inc(self.scaled, 1)

    def gpsimd(self, pool):
        for i in range(NB):
            pool.wait_ge(self.centred, i + 1)
            self.nc.gpsimd.tensor_tensor(self.sq[:, i, :], self.xc[:, i, :], self.xc[:, i, :], mybir.AluOpType.mult).then_inc(self.squared, 1)

    def scalar(self, act, var_ps):
        ACT = mybir.ActivationFunctionType
        for i in range(NB):
            act.wait_ge(self.var, i + 1)
            self.nc.scalar.activation(self.sd[:, i, :], var_ps[i][:, 0:HW], ACT.Sqrt, bias=self.m.eps[:, 0:1]).then_inc(self.dev, 1)
        for i in range(NB):
            act.wait_ge(self.scaled, i + 1)
            self.nc.scalar.activation(self.out[:, i, :], self.xc[:, i, :], ACT.Identity, scale=self.m.column(self.scale), bias=self.m.column(self.shift)).then_inc(self.normed, 1)


def target_self_phase(nc, m):
    fp32 = DTS["fp32"]
    ALU, ACT, AX = mybir.AluOpType, mybir.ActivationFunctionType, mybir.AxisListType
    ctx = ExitStack()
    with ctx:
        sb = lambda name, shape: ctx.enter_context(nc.sbuf_tensor(f"s_{name}", shape, fp32))
        sem = lambda name: nc.alloc_semaphore(f"s_{name}")
        q, k = sb("q", [128, B, Q]), sb("k", [128, B, Q])
        v = sb("v", [Q, B, D])
        bias, mask = sb("bias", [Q, H, Q]), sb("mask", [Q, Q])
        att = sb("att", [128, NB, HW])
        qhs, kbs, vbs, probss = ([sb(f"{n}{i}", shape) for i in range(2)] for n, shape in (
            ("qh", [128, H, Q]), ("kb", [128, Q]), ("vb", [Q, D]), ("probs", [Q, H, Q])))
        turned = sb("turned", [Q, H, Q])
        top, total = sb("top", [Q, H]), sb("total", [Q, H])
        out, biased = sb("o", [Q, D]), sb("biased", [Q, D])
        bank = ctx.enter_context(nc.psum_tensor("s_bank", [128, 8, 512], fp32))
        n1 = Norm(nc, ctx, m, "n1", "d_n1s", "d_n1b")
        n2 = Norm(nc, ctx, m, "n2", "d_n2s", "d_n2b")
        (y_in, const_in, masked, q_mm, k_mm, v_mm, q_out, k_out, v_out, gathered, scored, biased_s, topped, shifted, expd, summed,
         inverted, turned_mm, turned_out, averaged, scaled, biased_o, back, att_out, proj, y_out, cq_mm, cq_out) = (sem(n) for n in (
             "y_in", "const_in", "masked", "q_mm", "k_mm", "v_mm", "q_out", "k_out", "v_out", "gathered", "scored", "biased_s", "topped", "shifted", "expd", "summed",
             "inverted", "turned_mm", "turned_out", "averaged", "scaled", "biased_o", "back", "att_out", "proj", "y_out", "cq_mm", "cq_out"))
        passed = {e: sem(f"passed_{e}") for e in ("pool", "dve", "act")}
        block = ctx.enter_context(nc.Block())
        mean_ps, var_ps = [bank[:, i, :] for i in (0, 1)], [bank[:, i, :] for i in (2, 3)]

        def in_pairs(eng, step):
            with eng.Fori(0, B // 2 - 1) as pair:
                for i in range(2):
                    step(pair * 2 + i, i, True)
            step(B - 2, 0, True)
            step(B - 1, 1, False)

        @block.sync
        def _(sp):
            for i in range(NB):
                sp.dma_start(m.y[:, i, :], m.inputs["tgt"][:, HW * i:HW * i + HW]).then_inc(y_in, 16)
            sp.dma_start(bias[:, :, :], bass.AP(m.inputs["self_line"].tensor, Q - 1, [[2 * Q - 1, Q], [Q * 2 * Q, H], [1, Q]])).then_inc(const_in, 16)
            sp.dma_start(mask[:, :], m.inputs["causal"]).then_inc(const_in, 16)

        @block.tensor
        def _(pe):
            for s in (scored, averaged, back):
                pe.sem_inc(s, LEAD)
            pe.sem_inc(turned_mm, 2 * LEAD)
            pe.wait_ge(y_in, 32)
            n1.tensor(pe, m.y, None, mean_ps, var_ps)
            for i in range(NB):
                pe.wait_ge(n1.normed, i + 1)
                nc.tensor.matmul(bank[:, 4 + i, 0:HW], m.weight("s_q"), n1.out[:, i, :], start=True, stop=True).then_inc(q_mm, 1)
                nc.tensor.matmul(bank[:, 6 + i, 0:HW], m.weight("s_k"), n1.out[:, i, :], start=True, stop=True).then_inc(k_mm, 1)
            pe.wait_ge(n1.dev, 2)
            for i in range(NB):
                for b in range(4):
                    last = nc.tensor.matmul(bank[0:Q, i, D * b:D * b + D], n1.out[:, i, Q * b:Q * b + Q], m.weight("s_v"), start=True, stop=True)
                last.then_inc(v_mm, 1)
            pe.wait_ge(v_out, 2)
            pe.wait_ge(q_out, 2)
            pe.wait_ge(k_out, 2)

            def scores(b, i):
                pe.wait_ge(gathered, b * 3 + 3 + LEAD)
                pe.wait_ge(biased_s, b * 4 + LEAD)
                for h in range(H):
                    last = nc.tensor.matmul(bank[0:Q, h // 4, Q * (h % 4):Q * (h % 4) + Q], qhs[i][:, h, :], kbs[i][:, :], start=True, stop=True)
                    if h % 4 == 3:
                        last.then_inc(scored, 1)

            def step(b, i, ahead):
                if ahead:
                    scores(b + 1, 1 - i)
                pe.wait_ge(expd, b + 1 + LEAD)
                for r in range(2):
                    pe.wait_ge(turned_out, b * 2 + r + LEAD)
                    for h in range(8):
                        last = nc.tensor.transpose(bank[0:Q, 4 + h // 4, Q * (h % 4):Q * (h % 4) + Q], probss[i][:, 8 * r + h, :], m.ident[0:Q, 0:Q])
                    last.then_inc(turned_mm, 1)
                pe.wait_ge(turned_out, b * 2 + 2 + LEAD)
                pe.wait_ge(scaled, b + LEAD)
                for h in range(H):
                    last = nc.tensor.matmul(bank[0:Q, 6, HD * h:HD * h + HD], turned[:, h, :], vbs[i][:, HD * h:HD * h + HD], start=True, stop=True)
                last.then_inc(averaged, 1)
                pe.wait_ge(biased_o, b + 1 + LEAD)
                pe.wait_ge(att_out, b + LEAD)
                nc.tensor.transpose(bank[:, 7, 0:Q], biased[:, :], m.ident[0:Q, 0:Q]).then_inc(back, 1)

            scores(0, 0)
            in_pairs(pe, step)
            pe.wait_ge(att_out, B + LEAD)
            for i in range(NB):
                nc.tensor.matmul(bank[:, 4 + i, 0:HW], m.weight("s_o"), att[:, i, :], start=True, stop=True).then_inc(proj, 1)
            n2.tensor(pe, m.y, y_out, mean_ps, var_ps)
            for i in range(NB):
                pe.wait_ge(n2.normed, i + 1)
                nc.tensor.matmul(bank[:, 6 + i, 0:HW], m.weight("c_q"), n2.out[:, i, :], start=True, stop=True).then_inc(cq_mm, 1)

        @block.gpsimd
        def _(pool):
            for s in (gathered,):
                pool.sem_inc(s, LEAD)
            n1.gpsimd(pool)
            pool.wait_ge(q_out, 2)
            pool.wait_ge(k_out, 2)
            pool.wait_ge(v_out, 2)
            with pool.Fori(0, B // 2) as pair:
                for i in range(2):
                    b = pair * 2 + i
                    wait_alone(pool, averaged, b - 1 + LEAD, passed["pool"])
                    nc.gpsimd.tensor_tensor(qhs[i][:, :, :], q[:, bass.ds(b, 1), :].to_broadcast([128, H, Q]), m.head_mask[:, :].unsqueeze(2).to_broadcast([128, H, Q]), ALU.mult).then_inc(gathered, 1)
                    nc.gpsimd.tensor_copy(kbs[i][:, :], k[:, bass.ds(b, 1), :].rearrange("p o x -> p (o x)")).then_inc(gathered, 1)
                    nc.gpsimd.tensor_copy(vbs[i][:, :], v[:, bass.ds(b, 1), :].rearrange("p o x -> p (o x)")).then_inc(gathered, 1)
            n2.gpsimd(pool)

        @block.scalar
        def _(act):
            for s in (expd, turned_out):
                act.sem_inc(s, LEAD)
            n1.scalar(act, var_ps)
            for i in range(NB):
                act.wait_ge(k_mm, i + 1)
                nc.scalar.activation(k[:, 4 * i:4 * i + 4, :].rearrange("p b x -> p (b x)"), bank[:, 6 + i, 0:HW], ACT.Identity, bias=m.column("s_bk")).then_inc(k_out, 1)

            def exponentiate(b, i):
                wait_alone(act, shifted, b + 1 + LEAD, passed["act"])
                nc.scalar.activation(probss[i][:, :, :], probss[i][:, :, :], ACT.Exp).then_inc(expd, 1)

            def step(b, i, ahead):
                for r in range(2):
                    wait_alone(act, turned_mm, b * 2 + r + 1 + 2 * LEAD, passed["act"])
                    wait_alone(act, averaged, b + LEAD, passed["act"])
                    nc.scalar.activation(turned[:, 8 * r:8 * r + 8, :].rearrange("p (g h) x -> p g (h x)", g=2), bank[0:Q, 4:6, 0:4 * Q], ACT.Copy).then_inc(turned_out, 1)
                if ahead:
                    exponentiate(b + 1, 1 - i)

            exponentiate(0, 0)
            in_pairs(act, step)
            n2.scalar(act, var_ps)

        @block.vector
        def _(dve):
            for s in (biased_s, topped, shifted, summed, inverted, scaled, biased_o, att_out):
                dve.sem_inc(s, LEAD)
            n1.vector(dve, m.y, mean_ps)
            for i in range(NB):
                dve.wait_ge(q_mm, i + 1)
                nc.vector.tensor_scalar(q[:, 4 * i:4 * i + 4, :].rearrange("p b x -> p (b x)"), bank[:, 4 + i, 0:HW], m.column("s_bq"), SCALE, ALU.add, ALU.mult).then_inc(q_out, 1)
            dve.wait_ge(const_in, 32)
            nc.vector.tensor_tensor(bias[:, :, :], bias[:, :, :], mask[:, :].unsqueeze(1).to_broadcast([Q, H, Q]), ALU.add).then_inc(masked, 1)
            for i in range(NB):
                dve.wait_ge(v_mm, i + 1)
                nc.vector.tensor_copy(v[:, 4 * i:4 * i + 4, :].rearrange("p b x -> p (b x)"), bank[0:Q, i, :]).then_inc(v_out, 1)
            dve.wait_ge(masked, 1)

            def shift_scores(b, i):
                probs = probss[i]
                dve.wait_ge(turned_mm, b * 2 - 2 + 2 * LEAD)
                for g in range(4):
                    dve.wait_ge(scored, b * 4 + g + 1 + LEAD)
                    nc.vector.tensor_tensor(probs[:, 4 * g:4 * g + 4, :], bank[0:Q, g, 0:4 * Q].rearrange("p (h x) -> p h x", h=4), bias[:, 4 * g:4 * g + 4, :], ALU.add).then_inc(biased_s, 1)
                dve.wait_ge(biased_s, b * 4 + 4 + LEAD)
                nc.vector.tensor_reduce(top[:, :], probs[:, :, :], AX.X, ALU.max).then_inc(topped, 1)
                dve.wait_ge(topped, b + 1 + LEAD)
                nc.vector.tensor_tensor(probs[:, :, :], probs[:, :, :], top[:, :].unsqueeze(2).to_broadcast([Q, H, Q]), ALU.subtract).then_inc(shifted, 1)

            def step(b, i, ahead):
                if ahead:
                    shift_scores(b + 1, 1 - i)
                dve.wait_ge(expd, b + 1 + LEAD)
                nc.vector.tensor_reduce(total[:, :], probss[i][:, :, :], AX.X, ALU.add).then_inc(summed, 1)
                dve.wait_ge(summed, b + 1 + LEAD)
                nc.vector.reciprocal(total[:, :], total[:, :]).then_inc(inverted, 1)
                dve.wait_ge(inverted, b + 1 + LEAD)
                dve.wait_ge(averaged, b + 1 + LEAD)
                nc.vector.tensor_tensor(out[:, :].rearrange("p (h d) -> p h d", h=H), bank[0:Q, 6, 0:D].rearrange("p (h d) -> p h d", h=H), total[:, :].unsqueeze(2).to_broadcast([Q, H, HD]), ALU.mult).then_inc(scaled, 1)
                dve.wait_ge(scaled, b + 1 + LEAD)
                nc.vector.tensor_tensor(biased[:, :], out[:, :], m.row("s_bv")[0:Q, :], ALU.add).then_inc(biased_o, 1)
                dve.wait_ge(back, b + 1 + LEAD)
                nc.vector.tensor_copy(att[:, :, :].rearrange("p i (b x) -> p (i b) x", x=Q)[:, bass.ds(b, 1), :].rearrange("p o x -> p (o x)"), bank[:, 7, 0:Q]).then_inc(att_out, 1)

            shift_scores(0, 0)
            in_pairs(dve, step)
            for i in range(NB):
                dve.wait_ge(proj, i + 1)
                nc.vector.scalar_tensor_tensor(out=m.y[:, i, :], in0=bank[:, 4 + i, 0:HW], scalar=m.column("s_bo"), in1=m.y[:, i, :], op0=ALU.add, op1=ALU.add).then_inc(y_out, 1)
            n2.vector(dve, m.y, mean_ps)
            for i in range(NB):
                dve.wait_ge(cq_mm, i + 1)
                nc.vector.tensor_scalar(m.cq[:, 4 * i:4 * i + 4, :].rearrange("p b x -> p (b x)"), bank[:, 6 + i, 0:HW], m.column("c_bq"), SCALE, ALU.add, ALU.mult).then_inc(cq_out, 1)


def target_cross_phase(nc, m):
    fp32 = DTS["fp32"]
    ALU, ACT, AX = mybir.AluOpType, mybir.ActivationFunctionType, mybir.AxisListType
    ctx = ExitStack()
    with ctx:
        sb = lambda name, shape: ctx.enter_context(nc.sbuf_tensor(f"x_{name}", shape, fp32))
        sem = lambda name: nc.alloc_semaphore(f"x_{name}")
        bias = sb("bias", [Q, H, T])
        keys = [sb(f"keys{i}", [128, T]) for i in range(2)]
        vals = [sb(f"vals{i}", [KT, NT, D]) for i in range(2)]
        qh = [sb(f"qh{i}", [128, H, Q]) for i in range(2)]
        probs = sb("probs", [Q, 2, T])
        turned = sb("turned", [KT, NT, Q])
        tops, top = sb("tops", [Q, 2, NQ]), sb("top", [Q, 2])
        total = sb("total", [Q, 2, H])
        own = sb("own", [128, 4])
        gather_w = sb("gather_w", [128, 32])
        part = sb("part", [128, 2, Q])
        inv_rows, inv, product = sb("inv_rows", [Q, H, HD]), sb("inv", [128, Q]), sb("product", [128, Q])
        s_ps = ctx.enter_context(nc.psum_tensor("x_s_ps", [128, NQ, 512], fp32))
        t_ps = ctx.enter_context(nc.psum_tensor("x_t_ps", [128, 3, 512], fp32))
        o_ps = ctx.enter_context(nc.psum_tensor("x_o_ps", [128, 512], fp32))
        part_ps, inv_ps, sum_ps = o_ps[:, 0:2 * Q], o_ps[:, 2 * Q:3 * Q], o_ps[:, 3 * Q:4 * Q]
        (bias_in, const_in, gathered, scored, biased_s, topped, expd, turned_mm, low_out, high_out, averaged, parted, summed, inverted, spread, inv_mm, inv_out, scaled, att_out) = (sem(n) for n in (
            "bias_in", "const_in", "gathered", "scored", "biased_s", "topped", "expd", "turned_mm", "low_out", "high_out", "averaged", "parted", "summed", "inverted", "spread", "inv_mm", "inv_out", "scaled", "att_out"))
        loaded = [sem(f"loaded{i}") for i in range(2)]
        passed = {e: sem(f"passed_{e}") for e in ("pool", "dve", "act", "sp")}
        block = ctx.enter_context(nc.Block())

        def steps(pair, last=False):
            for i in range(2):
                for h in range(H):
                    over = h + 2 >= H
                    ahead = None if last and i and over else (pair * 2 + i + over, (i + over) % 2, (h + 2) % H)
                    yield pair * 2 + i, i, h, ahead

        @block.sync
        def _(sp):
            sp.dma_start(own[:, :], m.inputs["own_of_four"]).then_inc(const_in, 16)
            sp.dma_start(gather_w[:, :], m.inputs["gather_w"]).then_inc(const_in, 16)
            for g in range(4):
                sp.dma_start(bias[:, 4 * g:4 * g + 4, :], bass.AP(m.inputs["cross_line"].tensor, 4 * g * Q * (T + Q) + Q - 1, [[T + Q - 1, Q], [Q * (T + Q), 4], [1, T]])).then_inc(bias_in, 16)
            with sp.Fori(0, B // 2) as pair:
                for i in range(2):
                    b = pair * 2 + i
                    wait_alone(sp, att_out, b - 1 + LEAD, passed["sp"])
                    sp.dma_start(keys[i][:, :], m.d_kc[b, :, :]).then_inc(loaded[i], 16)
                    sp.dma_start(vals[i][:, :, :], m.d_vc[b, :, :, :]).then_inc(loaded[i], 16)

        @block.gpsimd
        def _(pool):
            pool.sem_inc(gathered, LEAD)
            with pool.Fori(0, B // 2) as pair:
                for i in range(2):
                    b = pair * 2 + i
                    wait_alone(pool, att_out, b - 1 + LEAD, passed["pool"])
                    nc.gpsimd.tensor_tensor(qh[i][:, :, :], m.cq[:, bass.ds(b, 1), :].to_broadcast([128, H, Q]), m.head_mask[:, :].unsqueeze(2).to_broadcast([128, H, Q]), ALU.mult).then_inc(gathered, 1)

        @block.tensor
        def _(pe):
            for s in (scored, turned_mm, averaged, summed, inv_mm):
                pe.sem_inc(s, LEAD)

            def scores(b, i, h):
                n = b * H + h
                if h == 0:
                    pe.wait_ge(loaded[i], (b - i) * 16 + 32)
                    pe.wait_ge(gathered, b + 1 + LEAD)
                for c in range(NQ):
                    pe.wait_ge(biased_s, n * NQ + c + 1)
                    nc.tensor.matmul(s_ps[0:Q, c, 0:QC], qh[i][:, h, :], keys[i][:, QC * c:QC * c + QC], start=True, stop=True).then_inc(scored, 1)

            def turn(n, buffer):
                pe.wait_ge(expd, n + 1 + LEAD)
                pe.wait_ge(low_out, n + LEAD)
                pe.wait_ge(high_out, n + LEAD)
                for t in range(NT):
                    rows = rows_of(t)
                    last = nc.tensor.transpose(t_ps[0:rows, t // 4, Q * (t % 4):Q * (t % 4) + Q], probs[:, buffer, KT * t:KT * t + rows], m.ident[0:Q, 0:Q])
                last.then_inc(turned_mm, 1)

            def average(i, n, h):
                pe.wait_ge(low_out, n + 1 + LEAD)
                pe.wait_ge(high_out, n + 1 + LEAD)
                pe.wait_ge(parted, n - 1 + LEAD)
                for t in range(NT):
                    rows, g = rows_of(t), t % 4
                    last = nc.tensor.matmul(part_ps[32 * g:32 * g + 32, Q * (h % 2):Q * (h % 2) + Q], vals[i][0:rows, t, h // 4 * 32:h // 4 * 32 + 32], turned[0:rows, t, :],
                                            start=(t < 4), stop=(t >= NT - 4), skip_group_check=True)
                last.then_inc(averaged, 1)

            def add_up(b, k):
                pe.wait_ge(parted, b * H + 4 * k + 4 + LEAD)
                if k == 0:
                    pe.wait_ge(att_out, b + LEAD)
                nc.tensor.matmul(sum_ps[32 * k:32 * k + 32, :], gather_w[:, :], part[:, k % 2, :], start=True, stop=True, skip_group_check=True).then_inc(summed, 1)

            def batches(pair, last=False):
                for b, i, h, ahead in steps(pair, last):
                    turn(b * H + h, h % 2)
                    if h and h % 4 == 0:
                        add_up(b, h // 4 - 1)
                    if ahead:
                        scores(*ahead)
                    average(i, b * H + h, h)
                    if h == H - 1:
                        add_up(b, h // 4)
                        pe.wait_ge(spread, b + 1 + LEAD)
                        nc.tensor.matmul(inv_ps, inv_rows[:, :, :].rearrange("p h d -> p (h d)"), m.ident[0:Q, 0:Q], start=True, stop=True, skip_group_check=True).then_inc(inv_mm, 1)

            pe.wait_ge(const_in, 32)
            scores(0, 0, 0)
            scores(0, 0, 1)
            with pe.Fori(0, B // 2 - 1) as pair:
                batches(pair)
            batches(B // 2 - 1, last=True)

        @block.scalar
        def _(act):
            act.sem_inc(expd, LEAD)
            act.sem_inc(high_out, LEAD)

            def exponentiate(b, i, h):
                n = b * H + h
                wait_alone(act, topped, n + 1 + LEAD, passed["act"])
                if h == 0:
                    wait_alone(act, inverted, b - 1 + LEAD, passed["act"])
                part = probs[:, h % 2, :]
                nc.scalar.activation(part, part, ACT.Exp, bias=top[:, h % 2:h % 2 + 1], accum_out=total[:, i, h:h + 1]).then_inc(expd, 1)

            def batches(pair, last=False):
                for b, i, h, ahead in steps(pair, last):
                    wait_alone(act, turned_mm, b * H + h + 1 + LEAD, passed["act"])
                    nc.scalar.activation(turned[0:KT, 8:11, :].rearrange("p t x -> p (t x)"), t_ps[0:KT, 2, 0:3 * Q], ACT.Copy)
                    nc.scalar.activation(turned[0:LAST, 11, :], t_ps[0:LAST, 2, 3 * Q:4 * Q], ACT.Copy).then_inc(high_out, 1)
                    if ahead:
                        exponentiate(*ahead)

            exponentiate(0, 0, 0)
            exponentiate(0, 0, 1)
            with act.Fori(0, B // 2 - 1) as pair:
                batches(pair)
            batches(B // 2 - 1, last=True)

        @block.vector
        def _(dve):
            dve.sem_inc(biased_s, NQ)
            for s in (topped, low_out, parted, inverted, spread, inv_out, scaled, att_out):
                dve.sem_inc(s, LEAD)
            dve.wait_ge(bias_in, 64)
            dve.wait_ge(const_in, 32)

            def add_bias(b, i, h):
                n = b * H + h
                wait_alone(dve, turned_mm, n - 1 + LEAD, passed["dve"])
                for c in range(NQ):
                    wait_alone(dve, scored, n * NQ + c + 1 + LEAD, passed["dve"])
                    nc.vector.tensor_tensor_reduce(out=probs[:, h % 2, QC * c:QC * c + QC], in0=s_ps[0:Q, c, 0:QC], in1=bias[:, h, QC * c:QC * c + QC], scale=1.0, scalar=-3e38,
                                                   op0=ALU.add, op1=ALU.max, accum_out=tops[:, h % 2, c:c + 1]).then_inc(biased_s, 1)
                dve.wait_ge(biased_s, n * NQ + NQ + NQ)
                dve.wait_ge(expd, n - 1 + LEAD)
                nc.vector.tensor_reduce(top[:, h % 2:h % 2 + 1], tops[:, h % 2, :], AX.X, ALU.max, negate=True).then_inc(topped, 1)

            def keep_own(b, h):
                n, k = b * H + h, h // 4
                dve.wait_ge(averaged, n + 1 + LEAD)
                mine, others = part_ps[:, Q * (h % 2):Q * (h % 2) + Q], part[:, k % 2, :]
                if h % 4 == 0:
                    dve.wait_ge(summed, b * 4 + k - 1 + LEAD)
                    nc.vector.tensor_scalar(others, mine, own[:, 0:1], None, ALU.mult).then_inc(parted, 1)
                else:
                    dve.wait_ge(parted, n + LEAD)
                    nc.vector.scalar_tensor_tensor(out=others, in0=mine, scalar=own[:, h % 4:h % 4 + 1], in1=others, op0=ALU.mult, op1=ALU.add).then_inc(parted, 1)

            def finish(b, i):
                dve.wait_ge(expd, b * H + H + LEAD)
                nc.vector.reciprocal(total[:, i, :], total[:, i, :]).then_inc(inverted, 1)
                dve.wait_ge(inverted, b + 1 + LEAD)
                nc.vector.tensor_copy(inv_rows[:, :, :], total[:, i, :].unsqueeze(2).to_broadcast([Q, H, HD])).then_inc(spread, 1)
                dve.wait_ge(inv_mm, b + 1 + LEAD)
                nc.vector.tensor_copy(inv[:, :], inv_ps).then_inc(inv_out, 1)
                dve.wait_ge(inv_out, b + 1 + LEAD)
                dve.wait_ge(summed, b * 4 + 4 + LEAD)
                nc.vector.tensor_tensor(product[:, :], sum_ps, inv[:, :], ALU.mult).then_inc(scaled, 1)
                dve.wait_ge(scaled, b + 1 + LEAD)
                nc.vector.tensor_scalar(m.att[:, :, :].rearrange("p i (b x) -> p (i b) x", x=Q)[:, bass.ds(b, 1), :].rearrange("p o x -> p (o x)"), product[:, :], m.column("c_bv"), None, ALU.add).then_inc(att_out, 1)

            def batches(pair, last=False):
                for b, i, h, ahead in steps(pair, last):
                    dve.wait_ge(turned_mm, b * H + h + 1 + LEAD)
                    nc.vector.tensor_copy(turned[0:KT, :, :].rearrange("p (g t) x -> p g (t x)", g=3)[:, 0:2, :], t_ps[0:KT, 0:2, 0:4 * Q]).then_inc(low_out, 1)
                    if ahead:
                        add_bias(*ahead)
                    keep_own(b, h)
                    if h == H - 1:
                        finish(b, i)

            add_bias(0, 0, 0)
            add_bias(0, 0, 1)
            with dve.Fori(0, B // 2 - 1) as pair:
                batches(pair)
            batches(B // 2 - 1, last=True)


def target_forward_phase(nc, m):
    fp32 = DTS["fp32"]
    ALU, ACT, AX = mybir.AluOpType, mybir.ActivationFunctionType, mybir.AxisListType
    ctx = ExitStack()
    with ctx:
        sb = lambda name, shape: ctx.enter_context(nc.sbuf_tensor(f"f_{name}", shape, fp32))
        sem = lambda name: nc.alloc_semaphore(f"f_{name}")
        hid = sb("hid", [128, NB, 4, HW])
        score = sb("score", [1, B * Q])
        row, col = sb("row", [Q, B, Q]), sb("col", [Q, B])
        above, level = sb("above", [Q, B, Q]), sb("level", [Q, B, Q])
        rank = sb("rank", [Q, B])
        onehot = sb("onehot", [Q, B, TOPK])
        before, slots = sb("before", [Q, Q]), sb("slots", [Q, TOPK])
        picked, tq = sb("picked", [128, B * TOPK]), sb("tq", [128, B, TOPK])
        bank = ctx.enter_context(nc.psum_tensor("f_bank", [128, 8, 512], fp32))
        n3 = Norm(nc, ctx, m, "n3", "d_n3s", "d_n3b")
        (const_in, proj, y2, f1_mm, relu, f2_mm, y3, score_mm, score_out, score_st, rank_in, tok_mm, tok_out, ranked, pick_mm, picked_s,
         q_mm, q_out, hot_mm, step) = (sem(n) for n in (
             "const_in", "proj", "y2", "f1_mm", "relu", "f2_mm", "y3", "score_mm", "score_out", "score_st", "rank_in", "tok_mm", "tok_out", "ranked", "pick_mm", "picked_s",
             "q_mm", "q_out", "hot_mm", "step"))
        block = ctx.enter_context(nc.Block())
        mean_ps, var_ps = [bank[:, i, :] for i in (0, 1)], [bank[:, i, :] for i in (2, 3)]

        @block.sync
        def _(sp):
            sp.dma_start(before[:, :], m.inputs["before"]).then_inc(const_in, 16)
            sp.dma_start(slots[:, :], m.inputs["slots"]).then_inc(const_in, 16)
            sp.wait_ge(score_out, 3)
            sp.dma_start(m.d_score[0:1, :], score[:, :]).then_inc(score_st, 16)
            sp.wait_ge(score_st, 16)
            sp.dma_start(row[:, :, :], m.d_score[0:1, :].to_broadcast([Q, B * Q]).rearrange("p (b x) -> p b x", b=B)).then_inc(rank_in, 16)
            sp.dma_start(col[:, :], m.d_score[0, :].rearrange("(b x) -> x b", b=B), allow_slow_non_contiguous=True).then_inc(rank_in, 16)
            sp.wait_ge(const_in, 32)

        @block.tensor
        def _(pe):
            for i in range(NB):
                nc.tensor.matmul(bank[:, 4 + i, 0:HW], m.weight("c_o"), m.att[:, i, :], start=True, stop=True).then_inc(proj, 1)
            n3.tensor(pe, m.y, y2, mean_ps, var_ps)
            for i in range(NB):
                pe.wait_ge(n3.normed, i + 1)
                for j in range(4):
                    k = 4 * i + j
                    if k >= 2:
                        pe.wait_ge(relu, k - 1)
                    nc.tensor.matmul(bank[:, 4 + k % 2, 0:HW], m.weight("d_f1", j), n3.out[:, i, :], start=True, stop=True).then_inc(f1_mm, 1)
                for j in range(4):
                    pe.wait_ge(relu, 4 * i + j + 1)
                    last = nc.tensor.matmul(bank[:, 6 + i, 0:HW], m.weight("d_f2", j), hid[:, i, j, :], start=(j == 0), stop=(j == 3))
                last.then_inc(f2_mm, 1)
            for i in range(NB):
                pe.wait_ge(y3, i + 1)
                nc.tensor.matmul(bank[0:1, i, 0:HW], m.column("score"), m.y[:, i, :], start=True, stop=True).then_inc(score_mm, 1)
            for i in range(NB):
                for b in range(4):
                    last = nc.tensor.transpose(bank[0:Q, 2 + i, D * b:D * b + D], m.y[:, i, Q * b:Q * b + Q], m.ident[:, :])
                last.then_inc(tok_mm, 1)
            pe.wait_ge(tok_out, 2)
            pe.wait_ge(ranked, 1)
            for b in range(B):
                last = nc.tensor.matmul(bank[:, 4, TOPK * b:TOPK * b + TOPK], m.tok[:, b, :], onehot[:, b, :], start=True, stop=True)
            last.then_inc(pick_mm, 1)
            for b in range(B):
                last = nc.tensor.transpose(bank[0:TOPK, 6 + b // 4, Q * (b % 4):Q * (b % 4) + Q], onehot[:, b, :], m.ident[0:Q, 0:Q])
            last.then_inc(hot_mm, 1)
            pe.wait_ge(picked_s, 1)
            nc.tensor.matmul(bank[:, 5, 0:B * TOPK], m.weight("t_q"), picked[:, :], start=True, stop=True).then_inc(q_mm, 1)

        @block.gpsimd
        def _(pool):
            n3.gpsimd(pool)
            pool.wait_ge(q_out, 1)
            nc.gpsimd.tensor_tensor(m.tqh[:, :, :, :], tq[:, :, :].unsqueeze(2).to_broadcast([128, B, H, TOPK]),
                                    m.head_mask[:, :].unsqueeze(1).unsqueeze(3).to_broadcast([128, B, H, TOPK]), ALU.mult).then_inc(q_out, 1)

        @block.scalar
        def _(act):
            n3.scalar(act, var_ps)
            for k in range(4 * NB):
                act.wait_ge(f1_mm, k + 1)
                nc.scalar.activation(hid[:, k // 4, k % 4, :], bank[:, 4 + k % 2, 0:HW], ACT.Relu, bias=m.column("d_b1", k % 4)).then_inc(relu, 1)
            act.wait_ge(hot_mm, 1)
            nc.scalar.activation(m.hot[:, :, :].rearrange("p (g b) x -> p g (b x)", g=2), bank[0:TOPK, 6:8, 0:4 * Q], ACT.Copy).then_inc(hot_mm, 1)

        @block.vector
        def _(dve):
            for i in range(NB):
                dve.wait_ge(proj, i + 1)
                nc.vector.scalar_tensor_tensor(out=m.y[:, i, :], in0=bank[:, 4 + i, 0:HW], scalar=m.column("c_bo"), in1=m.y[:, i, :], op0=ALU.add, op1=ALU.add).then_inc(y2, 1)
            n3.vector(dve, m.y, mean_ps)
            for i in range(NB):
                dve.wait_ge(f2_mm, i + 1)
                nc.vector.scalar_tensor_tensor(out=m.y[:, i, :], in0=bank[:, 6 + i, 0:HW], scalar=m.column("d_b2"), in1=m.y[:, i, :], op0=ALU.add, op1=ALU.add).then_inc(y3, 1)
            for i in range(NB):
                dve.wait_ge(score_mm, i + 1)
                nc.vector.tensor_copy(score[:, HW * i:HW * i + HW], bank[0:1, i, 0:HW]).then_inc(score_out, 1)
            dve.wait_ge(score_out, 2)
            nc.vector.tensor_scalar(score[:, :], score[:, :], m.score_b[0:1, 0:1], None, ALU.add).then_inc(score_out, 1)
            for i in range(NB):
                dve.wait_ge(tok_mm, i + 1)
                nc.vector.tensor_copy(m.tok[:, 4 * i:4 * i + 4, :].rearrange("p b x -> p (b x)"), bank[0:Q, 2 + i, :]).then_inc(tok_out, 1)
            dve.wait_ge(const_in, 32)
            dve.wait_ge(rank_in, 32)
            mine = col[:, :].unsqueeze(2).to_broadcast([Q, B, Q])
            nc.vector.tensor_tensor(above[:, :, :], row[:, :, :], mine, ALU.is_gt).then_inc(step, 1)
            nc.vector.tensor_tensor(level[:, :, :], row[:, :, :], mine, ALU.is_equal).then_inc(step, 1)
            dve.wait_ge(step, 2)
            nc.vector.tensor_tensor(level[:, :, :], level[:, :, :], before[:, :].unsqueeze(1).to_broadcast([Q, B, Q]), ALU.mult).then_inc(step, 1)
            dve.wait_ge(step, 3)
            nc.vector.tensor_tensor(above[:, :, :], above[:, :, :], level[:, :, :], ALU.add).then_inc(step, 1)
            dve.wait_ge(step, 4)
            nc.vector.tensor_reduce(rank[:, :], above[:, :, :], AX.X, ALU.add).then_inc(step, 1)
            dve.wait_ge(step, 5)
            nc.vector.tensor_scalar(m.kept[:, :], rank[:, :], float(TOPK), None, ALU.is_ge).then_inc(step, 1)
            nc.vector.tensor_tensor(onehot[:, :, :], rank[:, :].unsqueeze(2).to_broadcast([Q, B, TOPK]), slots[:, :].unsqueeze(1).to_broadcast([Q, B, TOPK]), ALU.is_equal).then_inc(ranked, 1)
            dve.wait_ge(pick_mm, 1)
            nc.vector.tensor_copy(picked[:, :], bank[:, 4, 0:B * TOPK]).then_inc(picked_s, 1)
            dve.wait_ge(q_mm, 1)
            nc.vector.tensor_scalar(tq[:, :, :].rearrange("p b r -> p (b r)"), bank[:, 5, 0:B * TOPK], m.column("t_bq"), SCALE, ALU.add, ALU.mult).then_inc(q_out, 1)


GH = H // 2
GR = GH * TOPK


def last_attention_phase(nc, m):
    fp32 = DTS["fp32"]
    ALU, ACT, AX = mybir.AluOpType, mybir.ActivationFunctionType, mybir.AxisListType
    ctx = ExitStack()
    with ctx:
        sb = lambda name, shape: ctx.enter_context(nc.sbuf_tensor(f"l_{name}", shape, fp32))
        sem = lambda name: nc.alloc_semaphore(f"l_{name}")
        keys = [sb(f"keys{i}", [128, T]) for i in range(2)]
        vals = [sb(f"vals{i}", [KT, NT, D]) for i in range(2)]
        qh = [sb(f"qh{i}", [128, H, TOPK]) for i in range(2)]
        probs, turned = sb("probs", [GR, NQ, QC]), sb("turned", [KT, NT, GR])
        top, total = sb("top", [GR, 2]), sb("total", [GR, 2])
        own = sb("own", [GR, 2, D])
        fold = sb("fold", [GR, TOPK])
        mine = sb("mine", [GR, 2, D])
        joined, rows_out = sb("joined", [128, TOPK]), sb("rows_out", [TOPK, B, D])
        final = sb("final", [Q, B, D])
        s_ps = ctx.enter_context(nc.psum_tensor("l_s_ps", [128, NQ, 512], fp32))
        t_ps = ctx.enter_context(nc.psum_tensor("l_t_ps", [128, 2, 512], fp32))
        o_ps = ctx.enter_context(nc.psum_tensor("l_o_ps", [128, 512], fp32))
        j_ps = ctx.enter_context(nc.psum_tensor("l_j_ps", [128, 512], fp32))
        (const_in, gathered, scored, topped, expd, turned_mm, turned_out, averaged, inverted, masked, folded, joined_s, proj, rows_s, placed, out_s, out_st) = (sem(n) for n in (
            "const_in", "gathered", "scored", "topped", "expd", "turned_mm", "turned_out", "averaged", "inverted", "masked", "folded", "joined_s", "proj", "rows_s", "placed", "out_s", "out_st"))
        loaded = [sem(f"loaded{i}") for i in range(2)]
        passed = {e: sem(f"passed_{e}") for e in ("pool", "sp", "act", "dve")}
        block = ctx.enter_context(nc.Block())

        def steps(pair, last=False):
            for i in range(2):
                for g in range(2):
                    ahead = None if last and i and g else (pair * 2 + i + g, (i + g) % 2, 1 - g)
                    yield pair * 2 + i, i, g, ahead

        @block.sync
        def _(sp):
            sp.dma_start(own[:, :, :], m.inputs["own"]).then_inc(const_in, 16)
            sp.dma_start(fold[:, :], m.inputs["fold"]).then_inc(const_in, 16)
            with sp.Fori(0, B // 2) as pair:
                for i in range(2):
                    b = pair * 2 + i
                    wait_alone(sp, rows_s, b - 1 + LEAD, passed["sp"])
                    sp.dma_start(keys[i][:, :], m.d_kl[b, :, :]).then_inc(loaded[i], 16)
                    sp.dma_start(vals[i][:, :, :], m.d_vl[b, :, :, :]).then_inc(loaded[i], 16)
            for b in range(B):
                sp.wait_ge(out_s, b + 1)
                sp.dma_start(m.out[b, :, :], final[:, b, :]).then_inc(out_st, 16)
            sp.wait_ge(out_st, 16 * B)

        @block.gpsimd
        def _(pool):
            pool.sem_inc(gathered, LEAD)
            with pool.Fori(0, B // 2) as pair:
                for i in range(2):
                    b = pair * 2 + i
                    wait_alone(pool, rows_s, b - 1 + LEAD, passed["pool"])
                    nc.gpsimd.tensor_copy(qh[i][:, :, :], m.tqh[:, bass.ds(b, 1), :, :].rearrange("p o h r -> p (o h) r")).then_inc(gathered, 1)

        @block.tensor
        def _(pe):
            for s in (scored, turned_mm, averaged, folded, proj):
                pe.sem_inc(s, LEAD)
            pe.wait_ge(const_in, 32)

            def scores(b, i, g):
                n = b * 2 + g
                if g == 0:
                    pe.wait_ge(loaded[i], (b - i) * 16 + 32)
                    pe.wait_ge(gathered, b + 1 + LEAD)
                pe.wait_ge(expd, n + LEAD)
                for c in range(NQ):
                    last = nc.tensor.matmul(s_ps[0:GR, c, 0:QC], qh[i][:, GH * g:GH * g + GH, :].rearrange("p h r -> p (h r)"), keys[i][:, QC * c:QC * c + QC], start=True, stop=True)
                last.then_inc(scored, 1)

            def turn(n):
                pe.wait_ge(expd, n + 1 + LEAD)
                pe.wait_ge(turned_out, n + LEAD)
                for t in range(NT):
                    rows = rows_of(t)
                    last = nc.tensor.transpose(t_ps[0:rows, t // 6, GR * (t % 6):GR * (t % 6) + GR], probs[:, :, :].rearrange("p c x -> p (c x)")[:, KT * t:KT * t + rows], m.ident[0:GR, 0:GR])
                last.then_inc(turned_mm, 1)

            def average(i, n):
                pe.wait_ge(turned_out, n + 1 + LEAD)
                pe.wait_ge(masked, n + LEAD)
                for t in range(NT):
                    rows = rows_of(t)
                    last = nc.tensor.matmul(o_ps[0:GR, 0:D], turned[0:rows, t, :], vals[i][0:rows, t, :], start=(t == 0), stop=(t == NT - 1))
                last.then_inc(averaged, 1)

            def project(b):
                pe.wait_ge(masked, b * 2 + 2 + LEAD)
                pe.wait_ge(rows_s, b + LEAD)
                for g in range(2):
                    last = nc.tensor.matmul(j_ps[:, 0:TOPK], mine[:, g, :], fold[:, :], start=(g == 0), stop=(g == 1))
                last.then_inc(folded, 1)
                pe.wait_ge(joined_s, b + 1 + LEAD)
                nc.tensor.matmul(j_ps[0:TOPK, 128:128 + D], joined[:, :], m.weight("t_o"), start=True, stop=True).then_inc(proj, 1)

            def batches(pair, last=False):
                for b, i, g, ahead in steps(pair, last):
                    turn(b * 2 + g)
                    if ahead:
                        scores(*ahead)
                    average(i, b * 2 + g)
                    if g:
                        project(b)

            scores(0, 0, 0)
            with pe.Fori(0, B // 2 - 1) as pair:
                batches(pair)
            batches(B // 2 - 1, last=True)
            pe.wait_ge(rows_s, B + LEAD)
            for b in range(B):
                last = nc.tensor.matmul(s_ps[0:Q, b // 4, D * (b % 4):D * (b % 4) + D], m.hot[:, b, :], rows_out[:, b, :], start=True, stop=True)
                last.then_inc(placed, 1)

        @block.scalar
        def _(act):
            act.sem_inc(expd, LEAD)
            act.sem_inc(turned_out, LEAD)

            def exponentiate(b, i, g):
                n = b * 2 + g
                wait_alone(act, topped, n + 1 + LEAD, passed["act"])
                wait_alone(act, turned_mm, n + LEAD, passed["act"])
                wait_alone(act, masked, n - 1 + LEAD, passed["act"])
                nc.scalar.activation(probs[:, :, :], s_ps[0:GR, :, 0:QC], ACT.Exp, bias=top[:, g:g + 1], accum_out=total[:, g:g + 1]).then_inc(expd, 1)

            def batches(pair, last=False):
                for b, i, g, ahead in steps(pair, last):
                    n = b * 2 + g
                    wait_alone(act, turned_mm, n + 1 + LEAD, passed["act"])
                    nc.scalar.activation(turned[0:KT, 0:6, :].rearrange("p t x -> p (t x)"), t_ps[0:KT, 0, 0:6 * GR], ACT.Copy)
                    nc.scalar.activation(turned[0:KT, 6:11, :].rearrange("p t x -> p (t x)"), t_ps[0:KT, 1, 0:5 * GR], ACT.Copy)
                    nc.scalar.activation(turned[0:LAST, 11, :], t_ps[0:LAST, 1, 5 * GR:6 * GR], ACT.Copy).then_inc(turned_out, 1)
                    if ahead:
                        exponentiate(*ahead)

            exponentiate(0, 0, 0)
            with act.Fori(0, B // 2 - 1) as pair:
                batches(pair)
            batches(B // 2 - 1, last=True)

        @block.vector
        def _(dve):
            for s in (topped, inverted, masked, joined_s, rows_s):
                dve.sem_inc(s, LEAD)
            dve.wait_ge(const_in, 32)

            def maximum(b, i, g):
                dve.wait_ge(scored, b * 2 + g + 1 + LEAD)
                nc.vector.tensor_reduce(top[:, g:g + 1], s_ps[0:GR, :, 0:QC], AX.XY, ALU.max, negate=True).then_inc(topped, 1)

            def batches(pair, last=False):
                for b, i, g, ahead in steps(pair, last):
                    n = b * 2 + g
                    if ahead:
                        maximum(*ahead)
                    dve.wait_ge(expd, n + 1 + LEAD)
                    nc.vector.reciprocal(total[:, g:g + 1], total[:, g:g + 1]).then_inc(inverted, 1)
                    dve.wait_ge(inverted, n + 1 + LEAD)
                    dve.wait_ge(averaged, n + 1 + LEAD)
                    dve.wait_ge(folded, b + LEAD)
                    nc.vector.scalar_tensor_tensor(out=mine[:, g, :], in0=o_ps[0:GR, 0:D], scalar=total[:, g:g + 1], in1=own[:, g, :], op0=ALU.mult, op1=ALU.mult).then_inc(masked, 1)
                    if g:
                        dve.wait_ge(folded, b + 1 + LEAD)
                        nc.vector.tensor_scalar(joined[:, :], j_ps[:, 0:TOPK], m.column("t_bv"), None, ALU.add).then_inc(joined_s, 1)
                        dve.wait_ge(proj, b + 1 + LEAD)
                        nc.vector.tensor_tensor(rows_out[:, bass.ds(b, 1), :].rearrange("p o x -> p (o x)"), j_ps[0:TOPK, 128:128 + D], m.row("t_bo")[0:TOPK, :], ALU.add).then_inc(rows_s, 1)

            maximum(0, 0, 0)
            with dve.Fori(0, B // 2 - 1) as pair:
                batches(pair)
            batches(B // 2 - 1, last=True)
            for b in range(B):
                dve.wait_ge(placed, b // 4 * 4 + 4)
                nc.vector.scalar_tensor_tensor(out=final[:, b, :], in0=m.tok[:, b, :], scalar=m.kept[:, b:b + 1], in1=s_ps[0:Q, b // 4, D * (b % 4):D * (b % 4) + D], op0=ALU.mult, op1=ALU.add).then_inc(out_s, 1)



PHASES = [setup_phase, norm_and_project_phase, attention_phase, context_phase,
          target_self_phase, target_cross_phase, target_forward_phase, last_attention_phase]


def build(nc, inputs, out):
    fp32, bf16 = DTS["fp32"], DTS["bf16"]
    m = Mem()
    m.inputs = inputs
    m.out = out

    def dram(name, shape, dt):
        return nc.dram_tensor(name, shape, dt, kind="Internal").ap()

    m.d_qp = dram("d_qp", (B, 3, D, T), bf16)
    m.d_kp = dram("d_kp", (B, 3, D, T), bf16)
    m.d_v = dram("d_v", (B, H, KT, NT * HD), fp32)
    m.d_band = dram("d_band", (H, 3 * SUB, 4, BW), bf16)
    m.d_step = dram("d_step", (H, NSTEP, T), bf16)
    m.d_att = dram("d_att", (NU, HD, T), fp32)
    m.d_den = dram("d_den", (NU, T), fp32)
    m.d_shift = dram("d_shift", (SLOTS, 3, KT * NT), bf16)
    m.d_inv = dram("d_inv", (NU, T), fp32)
    m.d_kl, m.d_kc = (dram(n, (B, D, T), fp32) for n in ("d_kl", "d_kc"))
    m.d_vl, m.d_vc = (dram(n, (B, KT, NT, D), fp32) for n in ("d_vl", "d_vc"))
    m.d_score = dram("d_score", (1, B * Q), fp32)
    ctx = ExitStack()
    with ctx:
        sb = lambda name, shape, dt: ctx.enter_context(nc.sbuf_tensor(name, shape, dt))
        m.w = sb("w", [128, NW * 128], fp32)
        m.vec = sb("vec", [128, NV], fp32)
        m.rowv = sb("rowv", [128, len(ROWV), D], fp32)
        m.ident = sb("ident", [128, 128], fp32)
        m.mean_w = sb("mean_w", [128, 128], fp32)
        m.den_sel = sb("den_sel", [128, 128], fp32)
        m.eps = sb("eps", [128, 1], fp32)
        m.left = sb("left_bias", [128, H], fp32)
        m.head_mask = sb("head_mask", [128, H], fp32)
        m.score_b = sb("score_b", [1, 1], fp32)
        m.y = sb("y", [128, NB, HW], fp32)
        m.att = sb("att", [128, NB, HW], fp32)
        m.cq = sb("cq", [128, B, Q], fp32)
        m.tok = sb("tok", [Q, B, D], fp32)
        m.kept = sb("kept", [Q, B], fp32)
        m.hot = sb("hot", [TOPK, B, Q], fp32)
        m.tqh = sb("tqh", [128, B, H, TOPK], fp32)
        m.weight = lambda n, j=0: m.w[:, 128 * (WCOL[n][0] + j):128 * (WCOL[n][0] + j + 1)]
        m.column = lambda n, j=0: m.vec[:, VCOL[n][0] + j:VCOL[n][0] + j + 1]
        m.row = lambda n: m.rowv[:, ROWV.index(n), :]
        for phase in PHASES:
            with nc.cleanup_on_exit():
                phase(nc, m)


def lay_out(x):
    import numpy as np

    g = lambda n: np.asarray(x[n])
    e, t = "L0_xattn_", "L1_xattn_"

    def qkv(w):
        return [w[0:D].T, w[D:2 * D].T, w[2 * D:3 * D].T]

    def down(w):
        return [w.T[D * j:D * j + D] for j in range(4)]

    w = qkv(g(e + "enc_in_w")) + [g(e + "enc_out_w").T, g(e + "enc_ff1_w").T] + down(g(e + "enc_ff2_w"))
    w += qkv(g(e + "dec_sa_in_w")) + [g(e + "dec_sa_out_w").T] + qkv(g(e + "dec_ca_in_w")) + [g(e + "dec_ca_out_w").T]
    w += [g(e + "dec_ff1_w").T] + down(g(e + "dec_ff2_w")) + qkv(g(t + "in_proj_w")) + [g(t + "out_w").T]
    two = lambda n: [g(n)[0:D], g(n)[D:2 * D]]
    four = lambda n: [g(n)[D * j:D * j + D] for j in range(4)]
    vec = two(e + "enc_in_b") + [g(e + "enc_out_b")] + four(e + "enc_ff1_b") + [g(e + "enc_ff2_b")]
    vec += [g(e + n) for n in ("enc_n1_s", "enc_n1_b", "enc_n2_s", "enc_n2_b")]
    vec += two(e + "dec_sa_in_b") + [g(e + "dec_sa_out_b")] + two(e + "dec_ca_in_b") + [g(e + "dec_ca_in_b")[2 * D:], g(e + "dec_ca_out_b")]
    vec += four(e + "dec_ff1_b") + [g(e + "dec_ff2_b")]
    vec += [g(e + n) for n in ("dec_n1_s", "dec_n1_b", "dec_n2_s", "dec_n2_b", "dec_n3_s", "dec_n3_b")]
    vec += two(t + "in_proj_b") + [g(t + "in_proj_b")[2 * D:], g(t + "score_w")[0]]
    rowv = [g(n)[2 * D:] for n in (e + "enc_in_b", e + "dec_sa_in_b")] + [g(t + "out_b")]
    pos = np.arange(GLEN) - G0
    at = lambda p: np.where(p < 0, np.minimum(-p, MD - 1), np.minimum(p, MD - 1) + MD)
    rev = HALO + SUB - 1 - np.arange(RLEN)
    keys, part = np.arange(T), np.arange(128)
    tile_of = keys // KT
    ind = np.zeros((96, T), np.float32)
    q_steps = np.zeros((NSTEP, T), np.float32)
    for s in range(3):
        for k in range(NT):
            ind[32 * s + k] = tile_of == k
            q_steps[NT * s + k] = keys < KT * k + SPLIT
    line = lambda n, many: np.tile(g(e + n)[at(np.arange(many) - (Q - 1))].T, (1, Q))
    token, group_row = np.arange(Q), np.arange(8 * TOPK)
    own = part[None, None, :] // HD == (8 * np.arange(2)[None, :, None] + group_row[:, None, None] // TOPK)
    bf16 = mybir.dt.np(mybir.dt.bfloat16)
    return {
        "ctx": g("ctx_1024").transpose(0, 2, 1), "tgt": g("x").transpose(2, 0, 1).reshape(D, B * Q),
        "w": np.concatenate(w, 1), "vec": np.stack(vec, 1), "rowv": np.stack(rowv),
        "line": np.tile(g(e + "enc_rel")[at(pos)].T, (1, KT)), "rev": np.tile(g(e + "enc_rel")[at(rev)].T, (1, SUB)),
        "edge": np.stack([g(e + "enc_rel")[MD - 1], g(e + "enc_rel")[2 * MD - 1]]),
        "tile_ind": ind.astype(bf16), "q_steps": q_steps.astype(bf16),
        "ones3": np.ones((3, T), bf16), "ident3": np.tile(np.eye(SUB), (3, 1)).astype(bf16),
        "ident": np.eye(128, dtype=np.float32), "mean": np.full((128, 128), 1 / D, np.float32),
        "den_sel": (part[:, None] == part[None, :] // 32 * 32 + HD).astype(np.float32),
        "self_line": line("dec_rel_self", 2 * Q), "cross_line": line("dec_rel_cross", T + Q),
        "causal": np.where(token[None, :] > token[:, None], -1e30, 0).astype(np.float32),
        "head_mask": (part[:, None] // HD == np.arange(H)[None, :]).astype(np.float32),
        "score_b": g(t + "score_b").reshape(1, 1),
        "own_of_four": (part[:, None] % 32 // HD == np.arange(4)[None, :]).astype(np.float32),
        "gather_w": (part[:, None] % 32 == np.arange(32)[None, :]).astype(np.float32),
        "before": (token[None, :] < token[:, None]).astype(np.float32),
        "slots": np.tile(np.arange(TOPK, dtype=np.float32), (Q, 1)),
        "own": own.astype(np.float32), "fold": (group_row[:, None] % TOPK == np.arange(TOPK)[None, :]).astype(np.float32),
        "eps": np.full((128, 1), EPS, np.float32),
    }


def kernel(**inputs):
    import numpy as np
    import concourse.bacc as bacc
    from concourse.bass_utils import run_bass_kernel_spmd

    arrays = {f"in_{n}": np.ascontiguousarray(a) for n, a in lay_out(inputs).items()}
    nc = bacc.Bacc("TRN2", target_bir_lowering=False, num_devices=1)
    aps = {n[3:]: nc.dram_tensor(n, a.shape, mybir.dt.from_np(a.dtype), kind="ExternalInput").ap() for n, a in arrays.items()}
    out = nc.dram_tensor("out", (B, Q, D), mybir.dt.float32, kind="ExternalOutput").ap()
    build(nc, aps, out)
    return run_bass_kernel_spmd(nc, [arrays], core_ids=[0]).results[0]["out"]
```
